# Optimizing a Trainium2 kernel written in Bass

```python
import numpy as np
import jax
import jax.numpy as jnp

def _softmax(x, axis=-1):
    return jax.nn.softmax(x, axis=axis)

def _gelu(x):
    return jax.nn.gelu(x, approximate=True)

def _silu(x):
    return jax.nn.silu(x)

def _sigmoid(x):
    return jax.nn.sigmoid(x)

def _layernorm(x, axis=-1, eps=1e-05):
    m = jnp.mean(x, axis=axis, keepdims=True)
    v = jnp.var(x, axis=axis, keepdims=True)
    return (x - m) / jnp.sqrt(v + eps)

def _scatter_add(tgt, idx, src, axis=0):
    return tgt.at[idx].add(src)

def _segment_sum(src, seg, n):
    return jax.ops.segment_sum(src, seg, n)
kernel_name = 'mk_gnn_preln_d4_gnn_r32_3507f9'

def setup_inputs(seed: int=0):
    np.random.seed(seed)
    _w = jnp.asarray

    def _rec_inputs():
        import jax
        import jax.numpy as jnp
        _gk = jax.random.key(seed)
        x = -0.0002117 + 1 * jax.random.normal(jax.random.fold_in(_gk, 1), (3125, 256), jnp.float32)
        src = jax.random.randint(jax.random.fold_in(_gk, 2), (50000,), 0, 3125, jnp.int32)
        dst = jax.random.randint(jax.random.fold_in(_gk, 3), (50000,), 0, 3125, jnp.int32)
        _o = jnp.argsort(dst, stable=True)
        src = src[_o]
        dst = dst[_o]
        edge_weight = jax.random.uniform(jax.random.fold_in(_gk, 13), (50000,), jnp.float32, 0.0, 0.999998)
        edge_weight_n2 = jax.random.uniform(jax.random.fold_in(_gk, 14), (50000,), jnp.float32, 0.0, 0.999998)
        return (x, src, dst, edge_weight, edge_weight_n2)
    x, src, dst, edge_weight, edge_weight_n2 = _rec_inputs()

    def _L0_gnn_setup():
        import jax, jax.numpy as jnp
        import numpy as np
        N = 3125
        D = 256
        E = 9375
        BN_EPS = 1e-05

        def _batchnorm(x, gamma, beta):
            mean = jnp.mean(x, axis=0)
            var = jnp.var(x, axis=0)
            return (x - mean) * jax.lax.rsqrt(var + BN_EPS) * gamma + beta
        key = jax.random.key(seed)
        ks = jax.random.split(key, 8)
        h = jax.random.normal(ks[0], (N, D), dtype=jnp.float32)
        edge_index = jax.random.randint(ks[1], (2, E), 0, N, dtype=jnp.int64)
        W1 = jax.random.normal(ks[2], (D, 2 * D), dtype=jnp.float32) / np.sqrt(D)
        b1 = jnp.zeros((2 * D,), dtype=jnp.float32)
        g1 = jnp.ones((2 * D,), dtype=jnp.float32)
        bt1 = jnp.zeros((2 * D,), dtype=jnp.float32)
        W2 = jax.random.normal(ks[3], (2 * D, D), dtype=jnp.float32) / np.sqrt(2 * D)
        b2 = jnp.zeros((D,), dtype=jnp.float32)
        g2 = jnp.ones((D,), dtype=jnp.float32)
        bt2 = jnp.zeros((D,), dtype=jnp.float32)
        eps_gin = jnp.zeros((), dtype=jnp.float32)
        return {'h': h, 'edge_index': edge_index, 'W1': W1, 'b1': b1, 'g1': g1, 'bt1': bt1, 'W2': W2, 'b2': b2, 'g2': g2, 'bt2': bt2, 'eps_gin': eps_gin}
    _L0_gnn_all = _L0_gnn_setup()
    _L0_gnn_in = {k: v for k, v in _L0_gnn_all.items() if k in ('W1', 'b1', 'g1', 'bt1', 'W2', 'b2', 'g2', 'bt2', 'eps_gin')}
    del _L0_gnn_all

    def _L1_gnn_setup():
        import jax, jax.numpy as jnp
        import numpy as np
        N_NODES = 3125
        N_EDGES = 25000
        DIM = 256
        EPS = 1e-05
        key = jax.random.key(seed)
        ks = jax.random.split(key, 12)
        H = DIM
        s = 1.0 / np.sqrt(H)
        s2 = 1.0 / np.sqrt(2 * H)
        return {'feat': jax.random.normal(ks[0], (N_NODES, DIM), dtype=jnp.float32), 'src': jax.random.randint(ks[1], (N_EDGES,), 0, N_NODES, dtype=jnp.int32), 'dst': jax.random.randint(ks[2], (N_EDGES,), 0, N_NODES, dtype=jnp.int32), 'iw': jax.random.uniform(ks[3], (N_EDGES,), dtype=jnp.float32), 'ow': jax.random.uniform(ks[4], (N_EDGES,), dtype=jnp.float32), 'gamma': jnp.ones((DIM,), jnp.float32), 'beta': jnp.zeros((DIM,), jnp.float32), 'W_in': jax.random.uniform(ks[5], (H, H), jnp.float32, -s, s), 'b_in': jax.random.uniform(ks[6], (H,), jnp.float32, -s, s), 'W_out': jax.random.uniform(ks[7], (H, H), jnp.float32, -s, s), 'b_out': jax.random.uniform(ks[8], (H,), jnp.float32, -s, s), 'W_x2i': jax.random.uniform(ks[9], (2 * H, 2 * H), jnp.float32, -s2, s2), 'b_x2i': jax.random.uniform(ks[10], (2 * H,), jnp.float32, -s2, s2), 'W_h2h': jax.random.uniform(ks[11], (H, 2 * H), jnp.float32, -s, s)}
    _L1_gnn_all = _L1_gnn_setup()
    _L1_gnn_in = {k: v for k, v in _L1_gnn_all.items() if k in ('gamma', 'beta', 'W_in', 'b_in', 'W_out', 'b_out', 'W_x2i', 'b_x2i', 'W_h2h')}
    del _L1_gnn_all

    def _L2_gnn_setup():
        import jax, jax.numpy as jnp
        import numpy as np
        N = 3125
        E = 100000
        DI = 256
        DO = 256
        BN_EPS = 1e-05

        def _bn_relu(h, gamma, beta):
            mean = jnp.mean(h, axis=0)
            var = jnp.var(h, axis=0)
            hn = (h - mean) * jax.lax.rsqrt(var + BN_EPS)
            return jax.nn.relu(hn * gamma + beta)
        key = jax.random.key(seed)
        ks = jax.random.split(key, 6)
        x = jax.random.normal(ks[0], (N, DI), dtype=jnp.float32)
        edge_row = jax.random.randint(ks[1], (E,), 0, N, dtype=jnp.int32)
        edge_col = jax.random.randint(ks[2], (E,), 0, N, dtype=jnp.int32)
        edge_vals = jnp.ones((E,), dtype=jnp.float32)
        eps = jnp.zeros((1,), dtype=jnp.float32)
        W1 = jax.random.normal(ks[3], (DI, DO), dtype=jnp.float32) * 0.05
        b1 = jnp.zeros((DO,), dtype=jnp.float32)
        g1 = jnp.ones((DO,), dtype=jnp.float32)
        be1 = jnp.zeros((DO,), dtype=jnp.float32)
        W2 = jax.random.normal(ks[4], (DO, DO), dtype=jnp.float32) * 0.05
        b2 = jnp.zeros((DO,), dtype=jnp.float32)
        g2 = jnp.ones((DO,), dtype=jnp.float32)
        be2 = jnp.zeros((DO,), dtype=jnp.float32)
        return {'x': x, 'edge_row': edge_row, 'edge_col': edge_col, 'edge_vals': edge_vals, 'eps': eps, 'W1': W1, 'b1': b1, 'g1': g1, 'be1': be1, 'W2': W2, 'b2': b2, 'g2': g2, 'be2': be2}
    _L2_gnn_all = _L2_gnn_setup()
    _L2_gnn_in = {k: v for k, v in _L2_gnn_all.items() if k in ('eps', 'W1', 'b1', 'g1', 'be1', 'W2', 'b2', 'g2', 'be2')}
    del _L2_gnn_all

    def _L3_gnn_setup():
        import jax, jax.numpy as jnp
        import numpy as np
        N_NODES = 512
        D_FEAT = 256
        N_EDGES = 8192
        HIDDEN = 512
        D_OUT = 256
        key = jax.random.key(seed)
        ks = jax.random.split(key, 5)
        x = jax.random.normal(ks[0], (N_NODES, D_FEAT), dtype=jnp.float32)
        W1 = jax.random.normal(ks[1], (2 * D_FEAT, HIDDEN), dtype=jnp.float32) * (1.0 / np.sqrt(2 * D_FEAT))
        b1 = jnp.zeros((HIDDEN,), dtype=jnp.float32)
        W2 = jax.random.normal(ks[2], (HIDDEN, D_OUT), dtype=jnp.float32) * (1.0 / np.sqrt(HIDDEN))
        b2 = jnp.zeros((D_OUT,), dtype=jnp.float32)
        nn_index = jax.random.randint(ks[3], (2, N_EDGES), 0, N_NODES, dtype=jnp.int64)
        return {'x': x, 'W1': W1, 'b1': b1, 'W2': W2, 'b2': b2, 'nn_index': nn_index, 'k': 16}
    _L3_gnn_all = _L3_gnn_setup()
    _L3_gnn_in = {k: v for k, v in _L3_gnn_all.items() if k in ('W1', 'b1', 'W2', 'b2')}
    del _L3_gnn_all
    return {'x': x, 'src': src, 'dst': dst, 'edge_weight': edge_weight, 'edge_weight_n2': edge_weight_n2, 'L0_gnn_W1': _L0_gnn_in['W1'], 'L0_gnn_b1': _L0_gnn_in['b1'], 'L0_gnn_g1': _L0_gnn_in['g1'], 'L0_gnn_bt1': _L0_gnn_in['bt1'], 'L0_gnn_W2': _L0_gnn_in['W2'], 'L0_gnn_b2': _L0_gnn_in['b2'], 'L0_gnn_g2': _L0_gnn_in['g2'], 'L0_gnn_bt2': _L0_gnn_in['bt2'], 'L0_gnn_eps_gin': _L0_gnn_in['eps_gin'], 'L1_gnn_gamma': _L1_gnn_in['gamma'], 'L1_gnn_beta': _L1_gnn_in['beta'], 'L1_gnn_W_in': _L1_gnn_in['W_in'], 'L1_gnn_b_in': _L1_gnn_in['b_in'], 'L1_gnn_W_out': _L1_gnn_in['W_out'], 'L1_gnn_b_out': _L1_gnn_in['b_out'], 'L1_gnn_W_x2i': _L1_gnn_in['W_x2i'], 'L1_gnn_b_x2i': _L1_gnn_in['b_x2i'], 'L1_gnn_W_h2h': _L1_gnn_in['W_h2h'], 'L2_gnn_eps': _L2_gnn_in['eps'], 'L2_gnn_W1': _L2_gnn_in['W1'], 'L2_gnn_b1': _L2_gnn_in['b1'], 'L2_gnn_g1': _L2_gnn_in['g1'], 'L2_gnn_be1': _L2_gnn_in['be1'], 'L2_gnn_W2': _L2_gnn_in['W2'], 'L2_gnn_b2': _L2_gnn_in['b2'], 'L2_gnn_g2': _L2_gnn_in['g2'], 'L2_gnn_be2': _L2_gnn_in['be2'], 'L3_gnn_W1': _L3_gnn_in['W1'], 'L3_gnn_b1': _L3_gnn_in['b1'], 'L3_gnn_W2': _L3_gnn_in['W2'], 'L3_gnn_b2': _L3_gnn_in['b2']}

def reference(x, src, dst, edge_weight, edge_weight_n2, L0_gnn_W1, L0_gnn_b1, L0_gnn_g1, L0_gnn_bt1, L0_gnn_W2, L0_gnn_b2, L0_gnn_g2, L0_gnn_bt2, L0_gnn_eps_gin, L1_gnn_gamma, L1_gnn_beta, L1_gnn_W_in, L1_gnn_b_in, L1_gnn_W_out, L1_gnn_b_out, L1_gnn_W_x2i, L1_gnn_b_x2i, L1_gnn_W_h2h, L2_gnn_eps, L2_gnn_W1, L2_gnn_b1, L2_gnn_g1, L2_gnn_be1, L2_gnn_W2, L2_gnn_b2, L2_gnn_g2, L2_gnn_be2, L3_gnn_W1, L3_gnn_b1, L3_gnn_W2, L3_gnn_b2):
    import jax
    import jax.numpy as jnp

    def _L0_gnn_ref(h, edge_index, W1, b1, g1, bt1, W2, b2, g2, bt2, eps_gin):
        import jax, jax.numpy as jnp
        import numpy as np
        N = 3125
        D = 256
        E = 9375
        BN_EPS = 1e-05

        def _batchnorm(x, gamma, beta):
            mean = jnp.mean(x, axis=0)
            var = jnp.var(x, axis=0)
            return (x - mean) * jax.lax.rsqrt(var + BN_EPS) * gamma + beta
        src, dst = (edge_index[0], edge_index[1])
        agg = jax.ops.segment_sum(h[src], dst, num_segments=N)
        z = (1.0 + eps_gin) * h + agg
        t = jnp.dot(z, W1) + b1
        t = jax.nn.relu(_batchnorm(t, g1, bt1))
        conv_out = jnp.dot(t, W2) + b2
        out = jax.nn.relu(_batchnorm(conv_out + h, g2, bt2))
        return out

    def _L1_gnn_ref(feat, src, dst, iw, ow, gamma, beta, W_in, b_in, W_out, b_out, W_x2i, b_x2i, W_h2h):
        import jax, jax.numpy as jnp
        import numpy as np
        N_NODES = 3125
        N_EDGES = 25000
        DIM = 256
        EPS = 1e-05
        N = feat.shape[0]
        num_steps = 1
        mean = jnp.mean(feat, axis=0)
        var = jnp.var(feat, axis=0)
        h = (feat - mean) * jax.lax.rsqrt(var + EPS) * gamma + beta
        for _ in range(num_steps):
            feat_in = h @ W_in + b_in
            feat_out = h @ W_out + b_out
            a_in = jax.ops.segment_sum(feat_in[src] * iw[:, None], dst, num_segments=N)
            a_out = jax.ops.segment_sum(feat_out[dst] * ow[:, None], src, num_segments=N)
            a = jnp.concatenate((a_in, a_out), axis=1)
            xi = a @ W_x2i + b_x2i
            hh = h @ W_h2h
            i_i, i_n = jnp.split(xi, 2, axis=1)
            h_i, h_n = jnp.split(hh, 2, axis=1)
            input_gate = jax.nn.sigmoid(i_i + h_i)
            new_gate = jnp.tanh(i_n + h_n)
            h = new_gate + input_gate * (h - new_gate)
        return h

    def _L2_gnn_ref(x, edge_row, edge_col, edge_vals, eps, W1, b1, g1, be1, W2, b2, g2, be2):
        import jax, jax.numpy as jnp
        import numpy as np
        N = 3125
        E = 100000
        DI = 256
        DO = 256
        BN_EPS = 1e-05

        def _bn_relu(h, gamma, beta):
            mean = jnp.mean(h, axis=0)
            var = jnp.var(h, axis=0)
            hn = (h - mean) * jax.lax.rsqrt(var + BN_EPS)
            return jax.nn.relu(hn * gamma + beta)
        n = x.shape[0]
        msgs = edge_vals[:, None] * x[edge_col]
        agg = jax.ops.segment_sum(msgs, edge_row, num_segments=n)
        h = (1.0 + eps[0]) * x + agg
        h = _bn_relu(h @ W1 + b1, g1, be1)
        h = _bn_relu(h @ W2 + b2, g2, be2)
        return h

    def _L3_gnn_ref(x, W1, b1, W2, b2, nn_index, k):
        import jax, jax.numpy as jnp
        import numpy as np
        N_NODES = 512
        D_FEAT = 256
        N_EDGES = 8192
        HIDDEN = 512
        D_OUT = 256
        num_nodes = x.shape[0]
        src = nn_index[0]
        tgt = nn_index[1]
        x_i = x[tgt]
        x_j = x[src]
        feat = jnp.concatenate([x_i, x_j - x_i], axis=-1)
        h = jax.nn.relu(feat @ W1 + b1)
        msg = h @ W2 + b2
        out = jax.ops.segment_sum(msg, tgt, num_segments=num_nodes)
        deg = jax.ops.segment_sum(jnp.ones((msg.shape[0], 1), dtype=msg.dtype), tgt, num_segments=num_nodes)
        return out / (deg + 1e-08)
    edge_index = jnp.stack([src, dst])
    h = jnp.maximum(_layernorm(x, axis=-1), 0.0)
    x = x + _L0_gnn_ref(h, edge_index, L0_gnn_W1, L0_gnn_b1, L0_gnn_g1, L0_gnn_bt1, L0_gnn_W2, L0_gnn_b2, L0_gnn_g2, L0_gnn_bt2, L0_gnn_eps_gin)
    h = jnp.maximum(_layernorm(x, axis=-1), 0.0)
    x = x + _L1_gnn_ref(h, src, dst, edge_weight, edge_weight_n2, L1_gnn_gamma, L1_gnn_beta, L1_gnn_W_in, L1_gnn_b_in, L1_gnn_W_out, L1_gnn_b_out, L1_gnn_W_x2i, L1_gnn_b_x2i, L1_gnn_W_h2h)
    h = jnp.maximum(_layernorm(x, axis=-1), 0.0)
    x = x + _L2_gnn_ref(h, src, dst, edge_weight, L2_gnn_eps, L2_gnn_W1, L2_gnn_b1, L2_gnn_g1, L2_gnn_be1, L2_gnn_W2, L2_gnn_b2, L2_gnn_g2, L2_gnn_be2)
    h = jnp.maximum(_layernorm(x, axis=-1), 0.0)
    x = x + _L3_gnn_ref(h, L3_gnn_W1, L3_gnn_b1, L3_gnn_W2, L3_gnn_b2, edge_index, 16)
    return x

_drawn_inputs = setup_inputs


def setup_inputs(seed=0):
    import zlib

    import numpy as np

    out = dict(_drawn_inputs(seed))
    spreads = {'L0_gnn_b1': (0.0, 0.8),
     'L0_gnn_g1': (1.0, 0.2),
     'L0_gnn_bt1': (0.0, 0.272),
     'L0_gnn_b2': (0.0, 0.8),
     'L0_gnn_g2': (1.0, 0.2),
     'L0_gnn_bt2': (0.0, 0.1),
     'L1_gnn_gamma': (1.0, 0.2),
     'L1_gnn_beta': (0.0, 0.1),
     'L2_gnn_b1': (0.0, 0.8),
     'L2_gnn_g1': (1.0, 0.2),
     'L2_gnn_be1': (0.0, 0.289),
     'L2_gnn_b2': (0.0, 0.8),
     'L2_gnn_g2': (1.0, 0.2),
     'L2_gnn_be2': (0.0, 0.1),
     'L3_gnn_b1': (0.0, 0.283),
     'L3_gnn_b2': (0.0, 0.1)}
    factors = {'L1_gnn_b_x2i': 8.0}
    for name, (base, spread) in spreads.items():
        noise = np.random.default_rng([zlib.crc32(name.encode()), seed]).standard_normal(out[name].shape)
        drawn = base * np.exp(spread * noise) if base else spread * noise
        out[name] = jnp.asarray(drawn.astype(out[name].dtype))
    for name, factor in factors.items():
        out[name] = (out[name] * factor).astype(out[name].dtype)
    return out
```

```python
import concourse.bass as bass
from concourse import mybir
from contextlib import ExitStack

P = 128
N = 3125
D = 256
E = 50000
EP = 125
EC = E // EP
NB = -(-N // P)
LAST = N - (NB - 1) * P
NP = NB * P
PAIR = 2 * P
PAIRS = (E + NB * (PAIR - 1)) // PAIR
CHUNKS = 2 * PAIRS
SP_IT = 5
CH_IT = 2 * SP_IT
ITERS = PAIRS // SP_IT
assert ITERS * SP_IT == PAIRS and EP * EC == E
LEAD = 2
TAB = 8
HID = 512
W = 448
NT = -(-N // W)
LN_EPS = 1e-5
SC = 10
SIT = EC // (2 * SC)
SPLIT = 5
GROUP = 5


def rows(t):
    return LAST if t == NB - 1 else P


def width(n):
    return min(W, N - n * W)


def cols(n):
    return slice(n * W, n * W + width(n))


def gnn_kernel(nc, a, out):
    f32, bf16, i32 = mybir.dt.float32, mybir.dt.bfloat16, mybir.dt.int32
    ALU, ACT, AX = mybir.AluOpType, mybir.ActivationFunctionType, mybir.AxisListType
    ds = bass.ds

    table = nc.dram_tensor("table", [N, D], f32).ap()
    qtable = nc.dram_tensor("qtable", [N, HID], f32).ap()
    xpark = nc.dram_tensor("xpark", [N, D], f32).ap()
    degrow = nc.dram_tensor("degrow", [1, N], f32).ap()
    recs_dram = [[nc.dram_tensor(f"recs{o}_{k}", [P * CHUNKS, 4], f32).ap() for k in range(SPLIT)]
                 for o in range(2)]

    ctx = ExitStack()
    with ctx:
        def sb(name, shape, dt):
            return ctx.enter_context(nc.sbuf_tensor(name, shape, dt))

        def sem(name):
            return ctx.enter_context(nc.semaphore(name))

        def sems(name, n):
            return [sem(f"{name}{k}") for k in range(n)]

        x = sb("x", [P, NB * D], f32)
        xt = x[:, :].rearrange("p (t f) -> p t f", t=NB)
        TTm = sb("TT", [P, 2 * N], f32)
        TT = TTm[:, :].rearrange("p (k n) -> p k n", k=2)
        acc = sb("acc", [P, 2 * 3 * NP], f32)
        sums = [acc[:, o * 3 * NP:(o + 1) * 3 * NP].rearrange("p (k n) -> p k n", k=3) for o in range(2)]
        Hm = sb("H", [P, 4 * NP + 260], f32)
        H = Hm[:, 0:4 * NP].rearrange("p (k n) -> p k n", k=4)
        Tm = Hm[:, 0:NB * D].rearrange("p (t f) -> p t f", t=NB)
        g0 = NB * D
        rowsbuf = Hm[:, g0:g0 + CH_IT * D].rearrange("p (c f) -> p c f", c=CH_IT)
        w0 = g0 + CH_IT * D
        Win = Hm[:, w0:w0 + 512].rearrange("p (k n) -> p k n", k=2)
        Wout = Hm[:, w0 + 512:w0 + 1024].rearrange("p (k n) -> p k n", k=2)
        Wx2i = Hm[:, w0 + 1024:w0 + 3072].rearrange("p (k n) -> p k n", k=4)
        Wh2h = Hm[:, w0 + 3072:w0 + 4096].rearrange("p (k n) -> p k n", k=2)
        W1e = Hm[:, w0:w0 + 2048].rearrange("p (k n) -> p k n", k=4)
        recs = [sb(f"rec{o}", [P, CHUNKS, 4], f32) for o in range(2)]
        Wm = sb("Wm", [P, 2048], f32)
        W1a = Wm[:, 0:1024].rearrange("p (k n) -> p k n", k=2)
        W2a = Wm[:, 1024:2048].rearrange("p (k n) -> p k n", k=4)
        W1c = Wm[:, 0:512].rearrange("p (k n) -> p k n", k=2)
        W2c = Wm[:, 512:1024].rearrange("p (k n) -> p k n", k=2)
        W2e = Wm[:, 1024:2048].rearrange("p (k n) -> p k n", k=4)
        b1bc = Wm[:, 0:HID]
        oh = sb("oh", [P, CH_IT, P], f32)
        iota1 = sb("iota1", [P, P], f32)
        ident = sb("ident", [P, P], f32)
        identb = sb("identb", [P, P], bf16)
        ones = sb("ones", [P, P], f32)
        stg_idx = sb("stg_idx", [P, CH_IT], i32)
        stg_lw = sb("stg_lw", [P, CH_IT, 3], f32)
        blk_tabs = sb("blk_tabs", [64, TAB * ITERS], i32)
        blk_tab = [blk_tabs[32 * o:32 * o + 1, :] for o in range(2)]
        vec = sb("vec", [P, 48], f32)
        lnst = sb("lnst", [P, GROUP, 6], f32)
        lnmv = sb("lnmv", [P, NB, 2], f32)
        lnr = sb("lnr", [P, NB], f32)
        lnb = sb("lnb", [P, NB], f32)
        bst = sb("bst", [P, 4, NT, 6], f32)
        bmv = sb("bmv", [P, 4, 2], f32)
        bA = sb("bA", [P, 4], f32)
        bC = sb("bC", [P, 4], f32)
        epst = sb("epst", [P, 1], f32)

        mask = acc[0:EP, 0:NB * EC // 2].bitcast(bf16).rearrange("p (b c) -> p b c", b=NB)
        run0 = NB * EC // 2
        run = acc[0:EP, run0:run0 + NB * EC].rearrange("p (b c) -> p b c", b=NB)
        key_i = [Hm[0:EP, 0:EC].bitcast(i32), Hm[0:EP, EC:2 * EC].bitcast(i32)]
        wts = [Hm[0:EP, 2 * EC:3 * EC], Hm[0:EP, 3 * EC:4 * EC]]
        ti = Hm[0:EP, 4 * EC:5 * EC].bitcast(i32)
        ti2 = Hm[0:EP, 5 * EC:6 * EC].bitcast(i32)
        blkf = Hm[0:EP, 6 * EC:7 * EC]
        pos = Hm[0:EP, 7 * EC:8 * EC]
        slot = [TTm[0:EP, o * EC:(o + 1) * EC] for o in range(2)]
        erec = [TTm[0:EP, 2 * EC + o * 4 * EC:2 * EC + (o + 1) * 4 * EC].rearrange("p (c r) -> p c r", r=4)
                for o in range(2)]
        zeros = Hm[:, 8 * EC:8 * EC + 4 * CHUNKS]
        tri = Hm[0:EP, 8 * EC + 4 * CHUNKS:8 * EC + 4 * CHUNKS + EP]
        iota_b = Hm[0:P, 8 * EC + 4 * CHUNKS + P:8 * EC + 4 * CHUNKS + P + NB]
        ends0 = 8 * EC + 4 * CHUNKS + 2 * P
        pstart = Hm[:, ends0:ends0 + PAIRS]
        lt0 = ends0 + PAIRS
        pairlt = acc[:, 0:PAIRS * (NB - 1)].rearrange("p (j b) -> p j b", b=NB - 1)
        pairbf = Hm[:, lt0:lt0 + PAIRS]
        srt0 = lt0 + PAIRS
        srt = Hm[:, srt0:srt0 + 5 * NB].rearrange("p (k b) -> p k b", b=NB)
        srti = Hm[:, srt0 + 5 * NB:srt0 + 6 * NB].bitcast(i32)
        sst_idx = oh[0:EP, 0:1, 0:2 * SC].bitcast(i32).rearrange("p a c -> p (a c)")
        sst_rec = oh[0:EP, 1:3, :].rearrange("p a c -> p (a c)")[:, 0:2 * SC * 4].rearrange(
            "p (c r) -> p c r", r=4)

        part = [acc[:, 3 * NP + k * 4 * CHUNKS:3 * NP + (k + 1) * 4 * CHUNKS].rearrange("p (c r) -> p c r", r=4)
                for k in range(SPLIT - 1)]

        quad = [Hm[:, q * 4 * W:(q + 1) * 4 * W].rearrange("p (f n) -> p f n", f=4) for q in range(4)]
        AB, GT = quad[0:2], quad[2:4]
        U = sums[0]
        PT = acc[:, 0:NB * 3 * HID // 2].bitcast(bf16).rearrange("p (b r f) -> p b r f", b=NB, r=3)
        PTf = acc[:, 0:NB * 3 * HID // 2].bitcast(bf16)
        hbuf = x[:, 0:CH_IT * HID].rearrange("p (c f) -> p c f", c=CH_IT)
        pf = [x[:, CH_IT * HID + q * HID:CH_IT * HID + (q + 1) * HID] for q in range(2)]
        qst = rowsbuf.rearrange("p c f -> p (c f)").rearrange("p (q f) -> p q f", f=HID)
        QS = 5
        OB = CH_IT // 2
        ohb, ohT = (TTm[:, N + q * OB * P // 2:N + (q + 1) * OB * P // 2].bitcast(bf16).rearrange(
            "p (c n) -> p c n", n=P) for q in range(2))
        deg = TT[:, 0, :]
        rdeg = TT[:, 1, :]

        VCOL, at = {}, 0
        for name, n in (("L0_gnn_b1", 4), ("L0_gnn_g1", 4), ("L0_gnn_bt1", 4), ("L0_gnn_b2", 2),
                        ("L0_gnn_g2", 2), ("L0_gnn_bt2", 2), ("L1_gnn_gamma", 2), ("L1_gnn_beta", 2),
                        ("L1_gnn_b_in", 2), ("L1_gnn_b_out", 2), ("L1_gnn_b_x2i", 4),
                        ("L2_gnn_b1", 2), ("L2_gnn_g1", 2), ("L2_gnn_be1", 2), ("L2_gnn_b2", 2),
                        ("L2_gnn_g2", 2), ("L2_gnn_be2", 2), ("L3_gnn_b2", 2)):
            VCOL[name] = (at, n)
            at += n
        eps_col = {0: at, 2: at + 1}
        NVEC = len(VCOL) + 2

        def v(name, k=None):
            o, n = VCOL[name]
            return vec[:, o:o + n] if k is None else vec[:, o + k:o + k + 1]

        ps = [ctx.enter_context(nc.psum_tensor(f"ps{b}", [P, 512], f32)) for b in range(8)]

        def flip_bank(c):
            return ps[5 + c % 2][:, 0:P // 2].bitcast(bf16)

        def spread_bank(c):
            return ps[3 + c % 2][:, :]

        edges_loaded = sem("edges_loaded")
        x_loaded = sem("x_loaded")
        vec_loaded = sem("vec_loaded")
        w_loaded = sems("w_loaded", 4)
        b1_loaded = sem("b1_loaded")
        consts = sem("consts")
        stages_begun = sem("stages_begun")
        zero_filled = sems("zero_filled", 2)
        vstep = sem("vstep")
        totals_ready = sem("totals_ready")
        order_ready = sem("order_ready")
        sc_staged = sems("sc_staged", 2)
        sc_done = sems("sc_done", SPLIT)
        merged = sem("merged")
        rec_loaded = sems("rec_loaded", 2)
        filled = sems("filled", 8)
        emptied = sems("emptied", 8)
        ln_ready = sem("ln_ready")
        std_ready = sem("std_ready")
        normed = sem("normed")
        tab_written = sem("tab_written")
        bn_var = sem("bn_var")
        bn_std = sem("bn_std")
        bn_ready = sem("bn_ready")
        act_ready = sem("act_ready")
        staged = sems("staged", SP_IT)
        landed = sems("landed", SP_IT)
        hot = sems("hot", SP_IT)
        summed = sems("summed", SP_IT)
        added = sems("added", SP_IT)
        sums_clear = sem("sums_clear")
        z_ready = sem("z_ready")
        scaled = sem("scaled")
        u_ready = sem("u_ready")
        deg_stored = sem("deg_stored")
        deg_loaded = sem("deg_loaded")
        parked = sem("parked")
        unparked = sem("unparked")
        q_stored = sems("q_stored", QS)
        wdiff = sem("wdiff")
        p_sum = sem("p_sum")
        p_hi = sem("p_hi")
        p_ready = sem("p_ready")
        hotb = sems("hotb", CH_IT)
        flipped = sems("flipped", CH_IT)
        flip_copied = sems("flip_copied", CH_IT)
        spread = sems("spread", CH_IT)
        joined = sems("joined", CH_IT)
        relued = sems("relued", CH_IT)
        out_stored = sem("out_stored")

        fills = [0] * 8
        jobs = {}

        def plan(stage, count, banks=range(8)):
            banks = list(banks)
            jobs[stage] = []
            for k in range(count):
                b = banks[k % len(banks)]
                fills[b] += 1
                jobs[stage].append((b, fills[b]))

        TG = [(g, min(4, NB - 4 * g)) for g in range(-(-NB // 4))]
        for o in range(2):
            plan(f"count{o}", 1)
        plan("T0", 2 * len(TG))
        plan("up0", 4 * NT)
        plan("down0", 2 * NT)
        plan("back0", NB)
        plan("T1", 2 * len(TG))
        jobs["ab1"], jobs["gates1"] = [], []
        banks = iter(range(16 * NT))

        def plan_more(stage):
            for _ in range(4):
                b = next(banks) % 8
                fills[b] += 1
                jobs[stage].append((b, fills[b]))

        plan_more("ab1")
        for n in range(NT):
            if n + 1 < NT:
                plan_more("ab1")
            plan_more("gates1")
        plan("back1", NB)
        plan("T2", 2 * len(TG))
        plan("up2", 2 * NT)
        plan("down2", 2 * NT)
        plan("back2", NB)
        plan("T3", 2 * len(TG))
        plan("q3", NB)
        plan("p3", NB)
        plan("down3", 2 * NT)
        plan("back3", NB)

        def wait_filled(eng, stage, k):
            b, c = jobs[stage][k]
            eng.wait_ge(filled[b], c)
            return ps[b]

        def wait_emptied(eng, stage, k):
            b, c = jobs[stage][k]
            eng.wait_ge(emptied[b], c)

        def bank(stage, k):
            return jobs[stage][k][0]

        def block_starts(eng, o, row, first, count):
            at = row * TAB + first
            return nc.values_load_multi_w_load_instructions(
                blk_tab[o][:, ds(at, count)], engines=[eng], min_val=0, max_val=(NB - 1) * P,
                skip_runtime_bounds_check_because="a count of blocks times their nodes")[1]

        def iterations(eng, n, body):
            with eng.Fori(n * ITERS, (n + 1) * ITERS - 1) as i:
                body(i, False)
            body((n + 1) * ITERS - 1, True)

        def ahead(i, j, d, last):
            if j + d < SP_IT:
                return i, j + d
            return None if last else (i + 1, j + d - SP_IT)

        PASSES = [(0, None, 0), (0, 1, 0), (1, 2, 1), (1, 1, 0), (0, None, 0)]
        ORDER = ["count0", "count1", "T0", "up0", "down0", "back0", "T1", "ab1", "gates1", "back1", "T2", "up2",
                 "down2", "back2", "T3", "q3", "p3", "down3", "back3"]

        block = ctx.enter_context(nc.Block())

        @block.sync
        def _(sp):
            def edge_view(name):
                return a[name].rearrange("(p c) -> p c", p=EP)

            sp.dma_start(key_i[0], edge_view("dst")).then_inc(edges_loaded, 16)
            sp.dma_start(key_i[1], edge_view("src")).then_inc(edges_loaded, 16)
            sp.dma_start(wts[0], edge_view("edge_weight")).then_inc(edges_loaded, 16)
            sp.dma_start(wts[1], edge_view("edge_weight_n2")).then_inc(edges_loaded, 16)
            nfull = NB - 1

            def tiles(dram):
                return (dram[0:nfull * P, :].rearrange("(t p) f -> p t f", p=P), dram[nfull * P:N, :])

            main, tail = tiles(a["x"])
            sp.dma_start(xt[:, 0:nfull, :], main).then_inc(x_loaded, 16)
            sp.dma_start(xt[0:LAST, nfull, :], tail).then_inc(x_loaded, 16)
            with nc.allow_non_contiguous_dma(reason="per-feature vectors"):
                for name, (o, n) in VCOL.items():
                    sp.dma_start(vec[:, o:o + n], a[name].rearrange("(k p) -> p k", p=P)).then_inc(vec_loaded, 16)
            sp.dma_start(vec[:, eps_col[0]:eps_col[0] + 1],
                         a["L0_gnn_eps_gin"].to_broadcast([P, 1])).then_inc(vec_loaded, 16)
            sp.dma_start(vec[:, eps_col[2]:eps_col[2] + 1],
                         a["L2_gnn_eps"].to_broadcast([P, 1])).then_inc(vec_loaded, 16)

            def weight(dst, name, s):
                sp.dma_start(dst, a[name].rearrange("(k p) n -> p k n", p=P)).then_inc(s, 16)

            weight(W1a, "L0_gnn_W1", w_loaded[0])
            weight(W2a, "L0_gnn_W2", w_loaded[0])
            sp.wait_ge(consts, 1)
            for o in range(2):
                for k in range(SPLIT):
                    sp.dma_start(recs_dram[o][k].rearrange("(p c) r -> p (c r)", p=P), zeros).then_inc(zero_filled[o], 16)
            def load_records(o):
                for k in range(SPLIT):
                    sp.wait_ge(sc_done[k], 16 * (o + 1) * (EC // SPLIT))
                    sp.dma_start(recs[o][:, :, :] if k == 0 else part[k - 1],
                                 recs_dram[o][k].rearrange("(p c) r -> p c r", p=P)).then_inc(rec_loaded[o], 16)

            sp.wait_ge(order_ready, 2)
            load_records(0)
            sp.wait_ge(merged, SPLIT - 1)
            load_records(1)

            def store_table(layer):
                for gidx in range(NB // GROUP):
                    sp.wait_ge(normed, layer * NB + (gidx + 1) * GROUP)
                    t0, t1 = gidx * GROUP, (gidx + 1) * GROUP
                    full = min(t1, nfull)
                    sp.dma_start(table[t0 * P:full * P, :].rearrange("(t p) f -> p t f", p=P),
                                 Tm[:, t0:full, :]).then_inc(tab_written, 16)
                sp.dma_start(table[nfull * P:N, :], Tm[0:LAST, nfull, :]).then_inc(tab_written, 16)

            store_table(0)
            for j in range(SP_IT):
                sp.wait_ge(added[j], ITERS + 1)
            sp.dma_start(degrow, sums[0][0:1, 2, 0:N]).then_inc(deg_stored, 16)
            b, c = jobs["down0"][-1]
            sp.wait_ge(filled[b], c)
            weight(W1c, "L2_gnn_W1", w_loaded[2])
            weight(W2c, "L2_gnn_W2", w_loaded[2])
            weight(W2e, "L3_gnn_W2", w_loaded[3])
            weight(Win, "L1_gnn_W_in", w_loaded[1])
            weight(Wout, "L1_gnn_W_out", w_loaded[1])
            weight(Wx2i, "L1_gnn_W_x2i", w_loaded[1])
            weight(Wh2h, "L1_gnn_W_h2h", w_loaded[1])
            store_table(1)
            store_table(2)
            b, c = jobs["gates1"][-1]
            sp.wait_ge(filled[b], c)
            weight(W1e, "L3_gnn_W1", w_loaded[3])
            b, c = jobs["down2"][-1]
            sp.wait_ge(filled[b], c)
            sp.dma_start(b1bc, a["L3_gnn_b1"].rearrange("(o n) -> o n", o=1).to_broadcast([P, HID])).then_inc(b1_loaded, 16)
            sp.wait_ge(normed, 4 * NB)
            main, tail = tiles(xpark)
            sp.dma_start(main, xt[:, 0:nfull, :]).then_inc(parked, 16)
            sp.dma_start(tail, xt[0:LAST, nfull, :]).then_inc(parked, 16)
            for t in range(NB):
                wait_emptied(sp, "q3", t)
                sp.dma_start(qtable[t * P:t * P + rows(t), :], qst[0:rows(t), t % QS, :]).then_inc(q_stored[t % QS], 16)
            b, c = jobs["p3"][-1]
            sp.wait_ge(filled[b], c)
            sp.wait_ge(deg_stored, 16)
            sp.dma_start(deg, degrow.to_broadcast([P, N])).then_inc(deg_loaded, 16)
            sp.wait_ge(parked, 32)
            for j in range(SP_IT):
                sp.wait_ge(summed[j], 5 * ITERS + 1)
            sp.dma_start(xt[:, 0:nfull, :], main).then_inc(unparked, 16)
            sp.dma_start(xt[0:LAST, nfull, :], tail).then_inc(unparked, 16)
            for gidx in range(NB // GROUP):
                for t in range(gidx * GROUP, (gidx + 1) * GROUP):
                    wait_emptied(sp, "back3", t)
                t0, t1 = gidx * GROUP, (gidx + 1) * GROUP
                full = min(t1, nfull)
                sp.dma_start(out[t0 * P:full * P, :].rearrange("(t p) f -> p t f", p=P),
                             xt[:, t0:full, :]).then_inc(out_stored, 16)
            sp.dma_start(out[nfull * P:N, :], xt[0:LAST, nfull, :]).then_inc(out_stored, 16)
            sp.wait_ge(out_stored, 16 * (NB // GROUP + 1))

        @block.gpsimd
        def _(pool):
            nc.gpsimd.memset(zeros, 0.0).then_inc(consts, 1)
            nc.gpsimd.iota(iota1[:, :], [[1, P]], base=1, channel_multiplier=0,
                           allow_small_or_imprecise_dtypes=True).then_inc(consts, 1)
            nc.gpsimd.iota(iota_b, [[1, NB]], base=0, channel_multiplier=0,
                           allow_small_or_imprecise_dtypes=True).then_inc(consts, 1)
            nc.gpsimd.iota(pstart, [[PAIR, PAIRS]], base=0, channel_multiplier=0,
                           allow_small_or_imprecise_dtypes=True).then_inc(consts, 1)
            nc.gpsimd.memset(ones[:, :], 1.0).then_inc(consts, 1)
            nc.gpsimd.memset(ident[:, :], 0.0).then_inc(consts, 1)
            nc.gpsimd.memset(tri, 1.0).then_inc(consts, 1)
            pool.wait_ge(consts, 7)
            nc.gpsimd.affine_select(out=ident[:, :], in_=ident[:, :], compare_op=ALU.not_equal, fill=1.0, base=0,
                                    pattern=[[-1, P]], channel_multiplier=1).then_inc(consts, 1)
            nc.gpsimd.affine_select(out=tri, in_=tri, compare_op=ALU.is_gt, fill=0.0, base=0,
                                    pattern=[[1, EP]], channel_multiplier=-1).then_inc(consts, 1)
            pool.wait_ge(consts, 9)
            nc.gpsimd.tensor_copy(identb[:, :], ident[:, :]).then_inc(consts, 1)

            def scatter_stage(i, o):
                for q in range(2):
                    pool.wait_ge(sc_staged[q], i + 1)
                    pool.sem_inc(stages_begun, 1)
                    for k in range(SC):
                        s = q * SC + k
                        if not isinstance(i, int) or s >= SPLIT:
                            pool.wait_ge(sc_done[k % SPLIT], 16 * (2 * q + k // SPLIT) + i * (32 * SC // SPLIT))
                            pool.sem_inc(stages_begun, 1)
                        pool.indirect_dma_start(
                            out=recs_dram[o][k % SPLIT],
                            out_offset=bass.IndirectOffsetOnAxis(ap=sst_idx[:, s:s + 1], axis=0),
                            in_=sst_rec[:, s, :], in_offset=None).then_inc(sc_done[k % SPLIT], 16)

            for o in range(2):
                pool.wait_ge(zero_filled[o], 16 * SPLIT)
                n0 = o * SIT
                if o == 0:
                    scatter_stage(0, o)
                with pool.Fori(n0 + (o == 0), n0 + SIT) as i:
                    scatter_stage(i, o)

            for n in range(4):
                layer = (0, 1, 1, 2)[n]
                pool.wait_ge(tab_written, 16 * (NB // GROUP + 1) * (layer + 1))
                with pool.Fori(n * ITERS, (n + 1) * ITERS) as i:
                    for j in range(SP_IT):
                        pool.wait_ge(staged[j], i + 1)
                        pool.sem_inc(stages_begun, 1)
                        for c in (2 * j, 2 * j + 1):
                            pool.indirect_dma_start(
                                out=rowsbuf[:, c, :], out_offset=None, in_=table,
                                in_offset=bass.IndirectOffsetOnAxis(ap=stg_idx[:, c:c + 1], axis=0)
                            ).then_inc(landed[j], 16)
            pool.wait_ge(parked, 32)
            for q in range(QS):
                pool.wait_ge(q_stored[q], 16 * (NB // QS))
            with pool.Fori(4 * ITERS, 5 * ITERS) as i:
                for j in range(SP_IT):
                    pool.wait_ge(staged[j], i + 1)
                    pool.sem_inc(stages_begun, 1)
                    for c in (2 * j, 2 * j + 1):
                        pool.indirect_dma_start(
                            out=hbuf[:, c, :], out_offset=None, in_=qtable,
                            in_offset=bass.IndirectOffsetOnAxis(ap=stg_idx[:, c:c + 1], axis=0)
                        ).then_inc(landed[j], 16)

        @block.scalar
        def _(act):
            def stage_half(i, o, q):
                uses = 2 * SC // SPLIT
                if not isinstance(i, int):
                    for k in range(SPLIT):
                        act.wait_ge(sc_done[k], i * (16 * uses) + (0 if q else -8 * uses))
                c0 = (i - o * SIT) * (2 * SC) + q * SC
                nc.scalar.copy(sst_idx[:, q * SC:(q + 1) * SC], slot[o][:, ds(c0, SC)])
                nc.scalar.copy(sst_rec[:, q * SC:(q + 1) * SC, :], erec[o][:, ds(c0, SC), :]).then_inc(sc_staged[q], 1)

            def stage_scatter(o):
                act.wait_ge(order_ready, o + 1)
                if o == 0:
                    stage_half(0, 0, 0)
                    stage_half(0, 0, 1)
                with act.Fori(o * SIT + (o == 0), (o + 1) * SIT) as i:
                    for q in range(2):
                        stage_half(i, o, q)

            def norm_rows(layer):
                for g in range(NB // GROUP):
                    n = layer * (NB // GROUP) + g
                    t0 = g * GROUP
                    act.wait_ge(ln_ready, 2 * n + 1)
                    nc.scalar.activation(lnr[:, t0:t0 + GROUP], lnmv[:, t0:t0 + GROUP, 1], ACT.Sqrt,
                                         bias=epst[:, 0:1], scale=1.0).then_inc(std_ready, 1)
                    act.wait_ge(ln_ready, 2 * n + 2)
                    for t in range(t0, t0 + GROUP):
                        r = rows(t)
                        nc.scalar.activation(Tm[0:r, t, :], xt[0:r, t, :], ACT.Relu, bias=lnb[0:r, t:t + 1],
                                             scale=lnr[0:r, t:t + 1]).then_inc(normed, 1)

            def take_transposes(layer):
                st = f"T{layer}"
                for g in range(len(TG)):
                    src = wait_filled(act, st, 2 * g)
                    n = min(512, N - 512 * g)
                    nc.scalar.copy(TT[:, 0, 512 * g:512 * g + n], src[:, 0:n]).then_inc(emptied[bank(st, 2 * g)], 1)

            def stage_pair(i, n, j):
                act.wait_ge(summed[j], i + 1)
                c0 = (i - n * ITERS) * CH_IT + 2 * j
                o = PASSES[n][0]
                nc.scalar.copy(stg_lw[:, 2 * j:2 * j + 2, :], recs[o][:, ds(c0, 2), 1:4])
                nc.scalar.copy(stg_idx[:, 2 * j:2 * j + 2], recs[o][:, ds(c0, 2), 0]).then_inc(staged[j], 1)

            def stage_pass(n):
                act.wait_ge(merged, (SPLIT - 1) * (PASSES[n][0] + 1))
                with act.Fori(n * ITERS, (n + 1) * ITERS) as i:
                    for j in range(SP_IT):
                        stage_pair(i, n, j)

            def take_products(st, bias, dst, nf):
                for n in range(NT):
                    for f in range(nf):
                        src = wait_filled(act, st, n * nf + f)
                        nc.scalar.activation(dst[:, f, cols(n)], src[:, 0:width(n)], ACT.Identity, bias=v(bias, f),
                                             scale=1.0).then_inc(emptied[bank(st, n * nf + f)], 1)

            def bn_deviation(k, nf):
                act.wait_ge(bn_var, k)
                nc.scalar.activation(bA[:, 0:nf], bmv[:, 0:nf, 1], ACT.Sqrt, bias=epst[:, 0:1],
                                     scale=1.0).then_inc(bn_std, 1)
                act.wait_ge(bn_ready, k)

            def scale_tiles(dst, nf, func):
                for n in range(NT):
                    for f in range(nf):
                        nc.scalar.activation(dst[:, f, cols(n)], dst[:, f, cols(n)], func, bias=bC[:, f:f + 1],
                                             scale=bA[:, f:f + 1]).then_inc(act_ready, 1)

            for s in flip_copied:
                act.sem_inc(s, 1)
            stage_scatter(0)
            act.wait_ge(order_ready, 2)
            for o in range(2):
                act.wait_ge(zero_filled[o], 16 * SPLIT)
            norm_rows(0)
            stage_scatter(1)
            act.wait_ge(sc_staged[1], 2 * SIT)
            take_transposes(0)
            stage_pass(0)
            act.wait_ge(vec_loaded, 16 * NVEC)
            take_products("up0", "L0_gnn_b1", H, 4)
            bn_deviation(1, 4)
            scale_tiles(H, 4, ACT.Relu)
            bn_deviation(2, 2)
            scale_tiles(U, 2, ACT.Relu)
            norm_rows(1)
            take_transposes(1)
            bn_deviation(3, 2)
            scale_tiles(TT, 2, ACT.Identity)
            stage_pass(1)
            stage_pass(2)
            for q in range(2):
                for j in range(SP_IT):
                    act.wait_ge(added[j], (2 + q) * ITERS + 1)
                for k in range(2):
                    nc.scalar.activation(sums[q][:, k, 0:N], sums[q][:, k, 0:N], ACT.Copy,
                                         scale=bA[:, k:k + 1]).then_inc(scaled, 1)
            for n in range(NT):
                if n >= 2:
                    act.wait_ge(u_ready, n - 1)
                for f in range(4):
                    src = wait_filled(act, "gates1", n * 4 + f)
                    nc.scalar.activation(GT[n % 2][:, f, 0:width(n)], src[:, 0:width(n)],
                                         ACT.Sigmoid if f < 2 else ACT.Tanh, bias=v("L1_gnn_b_x2i", f),
                                         scale=1.0).then_inc(emptied[bank("gates1", n * 4 + f)], 1)
            norm_rows(2)
            take_transposes(2)
            stage_pass(3)
            take_products("up2", "L2_gnn_b1", H, 2)
            bn_deviation(4, 2)
            scale_tiles(H, 2, ACT.Relu)
            take_products("down2", "L2_gnn_b2", U, 2)
            bn_deviation(5, 2)
            scale_tiles(U, 2, ACT.Relu)
            norm_rows(3)
            take_transposes(3)
            for t in range(NB):
                src = wait_filled(act, "q3", t)
                if t >= QS:
                    act.wait_ge(q_stored[t % QS], 16 * (t // QS))
                nc.scalar.copy(qst[0:rows(t), t % QS, :], src[0:rows(t), :]).then_inc(
                    emptied[bank("q3", t)], 1)
            for t in range(NB):
                r = rows(t)
                wait_emptied(act, "p3", t)
                if t == NB - 1:
                    act.wait_ge(sums_clear, 5)
                nc.scalar.copy(PT[0:r, t, 0, :], pf[t % 2][0:r, :]).then_inc(p_hi, 1)
                act.wait_ge(p_sum, t + 1)
                nc.scalar.copy(PT[0:r, t, 1, :], pf[t % 2][0:r, :]).then_inc(p_hi, 1)

            def flips(i, j):
                l = i - 4 * ITERS
                for c in (2 * j, 2 * j + 1):
                    act.wait_ge(flipped[c], l + 2)
                    act.wait_ge(spread[(c + OB) % CH_IT], l + 2 if c >= OB else l + 1)
                    nc.scalar.copy(ohT[:, c % OB, :], flip_bank(c)).then_inc(flip_copied[c], 1)

            def relus(i, j):
                for c in (2 * j, 2 * j + 1):
                    act.wait_ge(joined[c], i - 4 * ITERS + 2)
                    nc.scalar.activation(hbuf[:, c, :], hbuf[:, c, :], ACT.Relu).then_inc(relued[c], 1)

            for j in range(4):
                stage_pair(4 * ITERS, 4, j)
            flips(4 * ITERS, 0)
            flips(4 * ITERS, 1)
            relus(4 * ITERS, 0)

            def body4(i, last):
                for j in range(SP_IT):
                    for d, do in ((4, lambda i, j: stage_pair(i, 4, j)), (2, flips), (1, relus)):
                        if (nxt := ahead(i, j, d, last)) is not None:
                            do(*nxt)

            iterations(act, 4, body4)

        @block.vector
        def _(dve):
            nstep = [0]

            def link(ins):
                nstep[0] += 1
                ins.then_inc(vstep, 1)
                dve.wait_ge(vstep, nstep[0])

            V = nc.vector

            def sort(o):
                key, other = key_i[o], key_i[1 - o]
                link(V.tensor_scalar(ti, key, 7, None, ALU.arith_shift_right))
                link(V.tensor_copy(blkf, ti))
                link(V.tensor_scalar(ti2, key, 127, None, ALU.bitwise_and))
                V.tensor_scalar(erec[o][:, :, 1], ti2, 1.0, None, ALU.add)
                V.tensor_copy(erec[o][:, :, 0], other)
                V.tensor_copy(erec[o][:, :, 2], wts[0])
                V.tensor_copy(erec[o][:, :, 3], wts[1])
                link(V.tensor_tensor(mask, blkf[:, None, :].to_broadcast([EP, NB, EC]),
                                     iota_b[0:EP, :, None].to_broadcast([EP, NB, EC]), ALU.is_equal))
                flat = "p b c -> p (b c)"
                link(V.tensor_tensor_scan(run.rearrange(flat), ones[0:EP, 0:1].to_broadcast([EP, NB * EC]),
                                          mask.rearrange(flat), 0.0, ALU.mult, ALU.add))
                ends, tot, padded, bend, off = (srt[:, k, :] for k in range(5))
                link(V.tensor_copy(ends[0:EP, :], run[:, :, EC - 1]))
                V.tensor_copy(tot[0:EP, 0:1], ends[0:EP, 0:1])
                V.tensor_tensor(tot[0:EP, 1:NB], ends[0:EP, 1:NB], ends[0:EP, 0:NB - 1],
                                ALU.subtract).then_inc(totals_ready, 1)
                cnt = wait_filled(dve, f"count{o}", 0)
                link(V.tensor_scalar(srti[:, :], cnt[:, 32:32 + NB], float(PAIR - 1), None, ALU.add))
                link(V.tensor_scalar(srti[:, :], srti[:, :], 8, 8, ALU.arith_shift_right, ALU.logical_shift_left))
                link(V.tensor_copy(padded, srti[:, :]))
                link(V.tensor_tensor_scan(bend, ones[:, 0:NB], padded, 0.0, ALU.mult, ALU.add))
                e = slice(0, EP)
                link(V.tensor_tensor(off[e], bend[e], padded[e], ALU.subtract))
                V.tensor_tensor(off[e], off[e], cnt[e, 0:NB], ALU.add).then_inc(emptied[bank(f"count{o}", 0)], 1)
                wait_emptied(dve, f"count{o}", 0)
                link(V.tensor_tensor(off[e], off[e], ends[e], ALU.subtract))
                link(V.scalar_tensor_tensor(off[e], off[e], -1.0, tot[e], ALU.add, ALU.add))
                link(V.tensor_tensor(run, run, off[e][:, :, None].to_broadcast([EP, NB, EC]), ALU.add))
                link(V.tensor_tensor(run, run, mask, ALU.mult))
                link(V.tensor_reduce(pos, run.rearrange("p b c -> p c b"), AX.X, ALU.add))
                link(V.tensor_copy(ti, pos))
                V.tensor_scalar(ti2, ti, P - 1, None, ALU.bitwise_and)
                link(V.tensor_scalar(ti, ti, 7, None, ALU.arith_shift_right))
                link(V.scalar_tensor_tensor(slot[o], ti2, float(CHUNKS), ti, ALU.mult, ALU.add))
                q = slice(32 * o, 32 * o + 1)
                link(V.tensor_tensor(pairlt[q], pstart[q][:, :, None].to_broadcast([1, PAIRS, NB - 1]),
                                     bend[q][:, None, 0:NB - 1].to_broadcast([1, PAIRS, NB - 1]), ALU.is_ge))
                link(V.tensor_reduce(pairbf[q], pairlt[q], AX.X, ALU.add))
                V.tensor_scalar(blk_tab[o].rearrange("p (i j) -> p i j", j=TAB)[:, :, 0:SP_IT],
                                pairbf[q].rearrange("p (i j) -> p i j", j=SP_IT), float(P), None,
                                ALU.mult).then_inc(order_ready, 1)
                dve.wait_ge(order_ready, o + 1)

            def ln_stats(g, add=None):
                for t in range(g * GROUP, (g + 1) * GROUP):
                    r = rows(t)
                    if add is not None:
                        add(t)
                    link(V.bn_stats(lnst[0:r, t % GROUP, :], xt[0:r, t, :]))
                    last = V.bn_aggr(lnmv[0:r, t, :], lnst[0:r, t % GROUP, :])
                last.then_inc(ln_ready, 1)

            def ln_scale(layer, g):
                sl = slice(g * GROUP, (g + 1) * GROUP)
                dve.wait_ge(std_ready, layer * (NB // GROUP) + g + 1)
                dve.wait_ge(ln_ready, 2 * (layer * (NB // GROUP) + g) + 1)
                link(V.reciprocal(lnr[:, sl], lnr[:, sl]))
                V.scalar_tensor_tensor(lnb[:, sl], lnmv[:, sl, 0], -1.0, lnr[:, sl], ALU.mult,
                                       ALU.mult).then_inc(ln_ready, 1)

            def layer_norm(layer, add=None):
                for g in range(NB // GROUP):
                    ln_stats(g, add)
                    ln_scale(layer, g)

            def add_back(st):
                def add(t):
                    r = rows(t)
                    src = wait_filled(dve, st, t)
                    b, c = jobs[st][t]
                    V.tensor_tensor(xt[0:r, t, :], xt[0:r, t, :], src[0:r, 0:D], ALU.add).then_inc(emptied[b], 1)
                    dve.wait_ge(emptied[b], c)
                return add

            def take_transposes(layer):
                st = f"T{layer}"
                for g in range(len(TG)):
                    src = wait_filled(dve, st, 2 * g + 1)
                    n = min(512, N - 512 * g)
                    V.tensor_copy(TT[:, 1, 512 * g:512 * g + n], src[:, 0:n]).then_inc(emptied[bank(st, 2 * g + 1)], 1)
                wait_emptied(dve, st, 2 * len(TG) - 2)
                wait_emptied(dve, st, 2 * len(TG) - 1)

            def clear(which, count):
                V.memset(acc[:, which * 3 * NP:(which + 1) * 3 * NP], 0.0).then_inc(sums_clear, 1)
                dve.wait_ge(sums_clear, count)

            def make_hot(i, j, wcol):
                dve.wait_ge(staged[j], i + 1)
                for c in (2 * j, 2 * j + 1):
                    if wcol is None:
                        last = V.tensor_scalar(oh[:, c, :], iota1[:, :], stg_lw[:, c, 0:1], None, ALU.is_equal)
                    else:
                        last = V.tensor_scalar(oh[:, c, :], iota1[:, :], stg_lw[:, c, 0:1], stg_lw[:, c, wcol:wcol + 1],
                                               ALU.is_equal, ALU.mult)
                last.then_inc(hot[j], 1)

            def add_pair(i, j, dst, src, block0, slots):
                dve.wait_ge(summed[j], i + 2)
                dve.wait_ge(added[(j - 1) % SP_IT], i + 2 if j else i + 1)
                at = dst[:, 0:slots, ds(block0, P)]
                V.tensor_tensor(at, at, src.rearrange("p (k n) -> p k n", k=slots), ALU.add).then_inc(added[j], 1)

            def sum_pass(n):
                o, wcol, d = PASSES[n]

                def body(i, last):
                    first = block_starts(mybir.EngineType.DVE, o, i - n * ITERS, 0, SP_IT)
                    for j in range(SP_IT):
                        if (nxt := ahead(i, j, LEAD, last)) is not None:
                            make_hot(*nxt, wcol)
                        add_pair(i, j, sums[d], ps[j][:, 0:3 * P], first[j], 3)

                for j in range(LEAD):
                    make_hot(n * ITERS, j, wcol)
                iterations(dve, n, body)
                dve.wait_ge(added[SP_IT - 1], (n + 1) * ITERS + 1)

            def gin_input(col):
                for n in range(NT):
                    for k in range(2):
                        V.scalar_tensor_tensor(sums[0][:, k, cols(n)], TT[:, k, cols(n)], vec[:, col:col + 1],
                                               sums[0][:, k, cols(n)], ALU.mult, ALU.add).then_inc(z_ready, 1)

            def bn_scale(k, nf, gamma, beta):
                for f in range(nf):
                    last = V.bn_aggr(bmv[:, f, :], bst[:, f, :, :].rearrange("p n s -> p (n s)"))
                last.then_inc(bn_var, 1)
                dve.wait_ge(bn_std, k)
                dve.wait_ge(bn_var, k)
                link(V.reciprocal(bA[:, 0:nf], bA[:, 0:nf]))
                link(V.tensor_tensor(bA[:, 0:nf], bA[:, 0:nf], v(gamma), ALU.mult))
                link(V.tensor_tensor(bC[:, 0:nf], bmv[:, 0:nf, 0], bA[:, 0:nf], ALU.mult))
                V.tensor_tensor(bC[:, 0:nf], v(beta), bC[:, 0:nf], ALU.subtract).then_inc(bn_ready, 1)

            def stats_of(st, src, nf):
                last = None
                for n in range(NT):
                    for f in range(nf):
                        wait_emptied(dve, st, n * nf + f)
                        last = V.bn_stats(bst[:, f, n, :], src[:, f, cols(n)])
                link(last)

            def merge(o):
                dve.wait_ge(rec_loaded[o], 16 * SPLIT)
                for k in range(SPLIT - 1):
                    V.tensor_tensor(recs[o][:, :, :], recs[o][:, :, :], part[k], ALU.add).then_inc(merged, 1)
                    dve.wait_ge(merged, (SPLIT - 1) * o + k + 1)

            for s in added + joined:
                dve.sem_inc(s, 1)
            V.memset(epst[:, :], LN_EPS)
            link(V.memset(lnmv[:, :, :], 1.0))
            dve.wait_ge(edges_loaded, 64)
            dve.wait_ge(consts, 10)
            sort(0)
            sort(1)
            dve.wait_ge(x_loaded, 32)
            layer_norm(0)
            dve.wait_ge(vec_loaded, 16 * NVEC)
            V.tensor_scalar(vec[:, eps_col[0]:eps_col[0] + 1], vec[:, eps_col[0]:eps_col[0] + 1], 1.0, None, ALU.add)
            link(V.tensor_scalar(vec[:, eps_col[2]:eps_col[2] + 1], vec[:, eps_col[2]:eps_col[2] + 1], 1.0, None,
                                 ALU.add))
            clear(0, 1)
            merge(0)
            dve.wait_ge(sc_staged[1], 2 * SIT)
            take_transposes(0)
            for k in range(SPLIT):
                dve.wait_ge(sc_done[k], 32 * (EC // SPLIT))
            sum_pass(0)
            gin_input(eps_col[0])
            stats_of("up0", H, 4)
            bn_scale(1, 4, "L0_gnn_g1", "L0_gnn_bt1")
            for n in range(NT):
                for f in range(2):
                    k = n * 2 + f
                    src = wait_filled(dve, "down0", k)
                    V.scalar_tensor_tensor(U[:, f, cols(n)], src[:, 0:width(n)], v("L0_gnn_b2", f), TT[:, f, cols(n)],
                                           ALU.add, ALU.add).then_inc(emptied[bank("down0", k)], 1)
            stats_of("down0", U, 2)
            bn_scale(2, 2, "L0_gnn_g2", "L0_gnn_bt2")
            layer_norm(1, add_back("back0"))
            dve.wait_ge(deg_stored, 16)
            take_transposes(1)
            for n in range(NT):
                for f in range(2):
                    last = V.bn_stats(bst[:, f, n, :], TT[:, f, cols(n)])
            link(last)
            bn_scale(3, 2, "L1_gnn_gamma", "L1_gnn_beta")
            clear(0, 2)
            merge(1)
            clear(1, 3)
            sum_pass(1)
            sum_pass(2)

            def finish(n):
                w, q = width(n), n % 2
                wait_emptied(dve, "gates1", 4 * n + 3)
                t = AB[q][:, 0:2, 0:w]
                link(V.tensor_tensor(t, TT[:, :, cols(n)], GT[q][:, 2:4, 0:w], ALU.subtract))
                link(V.tensor_tensor(t, t, GT[q][:, 0:2, 0:w], ALU.mult))
                V.tensor_tensor(U[:, 0:2, cols(n)], t, GT[q][:, 2:4, 0:w], ALU.add).then_inc(u_ready, 1)

            def linear_in(n):
                if n >= 2:
                    dve.wait_ge(u_ready, n - 1)
                for q in range(2):
                    for f in range(2):
                        src = wait_filled(dve, "ab1", 4 * n + 2 * q + f)
                        V.scalar_tensor_tensor(AB[n % 2][:, 2 * q + f, 0:width(n)], sums[q][:, 2, cols(n)],
                                               v("L1_gnn_b_out" if q else "L1_gnn_b_in", f), src[:, 0:width(n)],
                                               ALU.mult, ALU.add).then_inc(emptied[bank("ab1", 4 * n + 2 * q + f)], 1)

            def shift(n):
                for q in range(2):
                    for k in range(2):
                        if n == 0:
                            dve.wait_ge(scaled, 2 * q + k + 1)
                        V.scalar_tensor_tensor(sums[q][:, k, cols(n)], sums[q][:, 2, cols(n)], bC[:, k:k + 1],
                                               sums[q][:, k, cols(n)], ALU.mult, ALU.add).then_inc(z_ready, 1)

            shift(0)
            for n in range(NT):
                if n + 1 < NT:
                    shift(n + 1)
                linear_in(n)
                if n >= 1:
                    finish(n - 1)
            finish(NT - 1)
            layer_norm(2, add_back("back1"))
            take_transposes(2)
            clear(0, 4)
            sum_pass(3)
            gin_input(eps_col[2])
            stats_of("up2", H, 2)
            bn_scale(4, 2, "L2_gnn_g1", "L2_gnn_be1")
            stats_of("down2", U, 2)
            bn_scale(5, 2, "L2_gnn_g2", "L2_gnn_be2")
            layer_norm(3, add_back("back2"))
            take_transposes(3)
            dve.wait_ge(w_loaded[3], 32)
            V.tensor_tensor(W1e[:, 0:2, :], W1e[:, 0:2, :], W1e[:, 2:4, :], ALU.subtract).then_inc(wdiff, 1)
            V.memset(PT[:, NB - 1, :, :].rearrange("p r f -> p (r f)"), 0.0).then_inc(sums_clear, 1)
            dve.wait_ge(parked, 32)
            dve.wait_ge(b1_loaded, 16)
            for t in range(NB):
                r = rows(t)
                p = pf[t % 2][0:r, :]
                src = wait_filled(dve, "p3", t)
                V.tensor_tensor(p, src[0:r, :], b1bc[0:r, :], ALU.add).then_inc(emptied[bank("p3", t)], 1)
                dve.wait_ge(p_hi, 2 * t + 1)
                V.tensor_tensor(p, p, PT[0:r, t, 0, :], ALU.subtract).then_inc(p_sum, 1)
                dve.wait_ge(p_hi, 2 * t + 2)
                V.tensor_tensor(PT[0:r, t, 2, :], p, PT[0:r, t, 1, :], ALU.subtract).then_inc(p_ready, 1)
            for q in range(QS):
                dve.wait_ge(q_stored[q], 16 * (NB // QS))
            V.memset(Hm[:, 0:4 * NP], 0.0).then_inc(sums_clear, 1)
            dve.wait_ge(sums_clear, 6)

            def hots(i, j):
                l = i - 4 * ITERS
                make_hot(i, j, None)
                for c in (2 * j, 2 * j + 1):
                    dve.wait_ge(flipped[(c + OB) % CH_IT], l + 2 if c >= OB else l + 1)
                    V.tensor_scalar(ohb[:, c % OB, :], iota1[:, :], stg_lw[:, c, 0:1], None,
                                    ALU.is_equal).then_inc(hotb[c], 1)

            def join(i, j):
                dve.wait_ge(landed[j], 32 * i + 32)
                for c in (2 * j, 2 * j + 1):
                    dve.wait_ge(spread[c], i - 4 * ITERS + 2)
                    V.tensor_tensor(hbuf[:, c, :], hbuf[:, c, :], spread_bank(c), ALU.add).then_inc(joined[c], 1)

            def add_hidden(i, j, start):
                add_pair(i, j, H, ps[j % 3][:, :], start, 4)

            hots(4 * ITERS, 0)
            hots(4 * ITERS, 1)
            join(4 * ITERS, 0)

            def body4(i, last):
                first = block_starts(mybir.EngineType.DVE, 0, i - 4 * ITERS, 0, SP_IT)
                for j in range(SP_IT):
                    if (nxt := ahead(i, j, 2, last)) is not None:
                        hots(*nxt)
                    if j >= 1:
                        add_hidden(i, j - 1, first[j - 1])
                    if (nxt := ahead(i, j, 1, last)) is not None:
                        join(*nxt)
                add_hidden(i, SP_IT - 1, first[SP_IT - 1])

            iterations(dve, 4, body4)
            dve.wait_ge(added[SP_IT - 1], 5 * ITERS + 1)
            dve.wait_ge(deg_loaded, 16)
            link(V.tensor_scalar(rdeg, deg, 1e-8, None, ALU.add))
            link(V.reciprocal(rdeg, rdeg))
            for n in range(NT):
                for f in range(2):
                    k = n * 2 + f
                    src = wait_filled(dve, "down3", k)
                    b, c = jobs["down3"][k]
                    V.scalar_tensor_tensor(U[:, f, cols(n)], deg[:, cols(n)], v("L3_gnn_b2", f), src[:, 0:width(n)],
                                           ALU.mult, ALU.add).then_inc(emptied[b], 1)
                    dve.wait_ge(emptied[b], c)
                    V.tensor_tensor(U[:, f, cols(n)], U[:, f, cols(n)], rdeg[:, cols(n)], ALU.mult).then_inc(u_ready, 1)
            dve.wait_ge(unparked, 32)
            add = add_back("back3")
            for t in range(NB):
                add(t)

        @block.tensor
        def _(pe):
            mm = nc.tensor.matmul

            def take_bank(st, k):
                b, c = jobs[st][k]
                if c > 1:
                    pe.wait_ge(emptied[b], c - 1)
                return ps[b]

            def done(ins, st, k):
                ins.then_inc(filled[bank(st, k)], 1)

            def counts(o):
                pe.wait_ge(totals_ready, o + 1)
                dst = take_bank(f"count{o}", 0)
                tot = srt[0:EP, 1, :]
                mm(dst[0:EP, 0:NB], tri, tot, start=True, stop=True)
                done(mm(dst[:, 32:32 + NB], ones[0:EP, :], tot, start=True, stop=True), f"count{o}", 0)

            def transposes(layer):
                st = f"T{layer}"
                for g, (g0_, m) in enumerate(TG):
                    pe.wait_ge(normed, layer * NB + 4 * g + m)
                    for k in range(2):
                        dst = take_bank(st, 2 * g + k)
                        for t in range(4 * g, 4 * g + m):
                            r = rows(t)
                            o = (t - 4 * g) * P
                            last = nc.tensor.transpose(dst[:, o:o + r], Tm[0:r, t, k * P:(k + 1) * P],
                                                       ident[0:r, 0:r])
                        done(last, st, 2 * g + k)

            def back(st, ready, count):
                for t in range(NB):
                    r = rows(t)
                    pe.wait_ge(ready, count(min(NT - 1, (t * P + r - 1) // W)))
                    dst = take_bank(st, t)
                    for k in range(2):
                        last = nc.tensor.transpose(dst[0:r, k * P:(k + 1) * P], U[:, k, t * P:t * P + r],
                                                   ident[:, :])
                    done(last, st, t)

            def drained():
                for b in range(8):
                    if fills_at[0][b]:
                        pe.wait_ge(emptied[b], fills_at[0][b])

            fills_at = [[0] * 8]

            def before(stage):
                b0 = [0] * 8
                for name in ORDER[:ORDER.index(stage)]:
                    for b, c in jobs[name]:
                        b0[b] = max(b0[b], c)
                fills_at[0] = b0
                drained()

            def sum_pass(n):
                with pe.Fori(n * ITERS, (n + 1) * ITERS) as i:
                    for j in range(SP_IT):
                        pe.wait_ge(hot[j], i + 1)
                        pe.wait_ge(landed[j], 32 * i + 32)
                        pe.wait_ge(added[j], i + 1)
                        for k in range(3):
                            for c in (2 * j, 2 * j + 1):
                                lhs = rowsbuf[:, c, k * P:(k + 1) * P] if k < 2 else ones[:, :]
                                last = mm(ps[j][:, k * P:(k + 1) * P], lhs, oh[:, c, :], start=(c == 2 * j),
                                          stop=(c == 2 * j + 1))
                        last.then_inc(summed[j], 1)
                for j in range(SP_IT):
                    pe.wait_ge(added[j], (n + 1) * ITERS + 1)

            def products(st, n, nf, terms, k0=0):
                for f in range(nf):
                    dst = take_bank(st, k0 + f)
                    for m, (w, src) in enumerate(terms):
                        last = mm(dst[:, 0:width(n)], w[:, f * P:(f + 1) * P], src, start=(m == 0),
                                  stop=(m == len(terms) - 1))
                    done(last, st, k0 + f)

            def up(st, w, nf, z0):
                for n in range(NT):
                    pe.wait_ge(z_ready, z0 + 2 * (n + 1))
                    products(st, n, nf, [(w[:, k, :], sums[0][:, k, cols(n)]) for k in range(2)], n * nf)

            def down(st, w, nk, a0):
                for n in range(NT):
                    if a0 is not None:
                        pe.wait_ge(act_ready, a0 + nk * (n + 1))
                    products(st, n, 2, [(w[:, k, :], H[:, k, cols(n)]) for k in range(nk)], n * 2)

            for s in summed + flipped + spread:
                pe.sem_inc(s, 1)
            pe.wait_ge(consts, 10)
            counts(0)
            counts(1)
            pe.wait_ge(order_ready, 2)
            transposes(0)
            before("up0")
            sum_pass(0)
            pe.wait_ge(w_loaded[0], 32)
            up("up0", W1a, 4, 0)
            down("down0", W2a, 4, 0)
            back("back0", act_ready, lambda n: 4 * NT + 2 * (n + 1))
            transposes(1)
            before("ab1")
            sum_pass(1)
            sum_pass(2)
            pe.wait_ge(w_loaded[1], 64)
            pe.wait_ge(act_ready, 8 * NT)

            def linear_in(n):
                pe.wait_ge(z_ready, 2 * NT + 4 * (n + 1))
                if n >= 2:
                    pass
                for q, w in ((0, Win), (1, Wout)):
                    products("ab1", n, 2, [(w[:, k, :], sums[q][:, k, cols(n)]) for k in range(2)], 4 * n + 2 * q)

            linear_in(0)
            for n in range(NT):
                if n + 1 < NT:
                    linear_in(n + 1)
                for f in range(4):
                    b, c = jobs["ab1"][4 * n + f]
                    pe.wait_ge(emptied[b], c)
                products("gates1", n, 4, [(Wx2i[:, k, :], AB[n % 2][:, k, 0:width(n)]) for k in range(4)]
                         + [(Wh2h[:, k, :], TT[:, k, cols(n)]) for k in range(2)], 4 * n)
            back("back1", u_ready, lambda n: n + 1)
            transposes(2)
            before("up2")
            sum_pass(3)
            pe.wait_ge(w_loaded[2], 32)
            up("up2", W1c, 2, 6 * NT)
            down("down2", W2c, 2, 8 * NT)
            back("back2", act_ready, lambda n: 10 * NT + 2 * (n + 1))
            transposes(3)
            for k in (-1, -2):
                wait_emptied(pe, "T3", k)
            pe.wait_ge(w_loaded[3], 32)
            for st, w in (("q3", 2), ("p3", 0)):
                if st == "p3":
                    pe.wait_ge(wdiff, 1)
                for t in range(NB):
                    r = rows(t)
                    dst = take_bank(st, t)
                    for k in range(2):
                        last = mm(dst[0:r, :], TT[:, k, t * P:t * P + r], W1e[:, w + k, :], start=(k == 0),
                                  stop=(k == 1))
                    done(last, st, t)
            before("down3")
            pe.wait_ge(p_ready, NB)

            def flip(i, j):
                l = i - 4 * ITERS
                for c in (2 * j, 2 * j + 1):
                    pe.wait_ge(hotb[c], l + 1)
                    pe.wait_ge(flip_copied[(c - 2) % CH_IT], l + 2 if c >= 2 else l + 1)
                    nc.tensor.transpose(flip_bank(c), ohb[:, c % OB, :], identb[:, :]).then_inc(flipped[c], 1)

            def spread_pair(i, j, start):
                l = i - 4 * ITERS
                for c in (2 * j, 2 * j + 1):
                    pe.wait_ge(flip_copied[c], l + 2)
                    pe.wait_ge(joined[(c - 2) % CH_IT], l + 2 if c >= 2 else l + 1)
                    for part3 in range(3):
                        last = mm(spread_bank(c), ohT[:, c % OB, :],
                                  PTf[:, ds(start * (3 * HID // P) + part3 * HID, HID)], start=(part3 == 0),
                                  stop=(part3 == 2))
                    last.then_inc(spread[c], 1)

            def sum_hidden(i, j):
                l = i - 4 * ITERS
                before_j = (j - 3) if j >= 3 else (j + 3 if j + 3 < SP_IT else j)
                pe.wait_ge(added[before_j], i + 2 if j >= 3 else i + 1)
                pe.wait_ge(relued[2 * j], l + 1)
                pe.wait_ge(relued[2 * j + 1], l + 1)
                pe.wait_ge(hot[j], i + 1)
                for k in range(4):
                    for c in (2 * j, 2 * j + 1):
                        last = mm(ps[j % 3][:, k * P:(k + 1) * P], hbuf[:, c, k * P:(k + 1) * P], oh[:, c, :],
                                  start=(c == 2 * j), stop=(c == 2 * j + 1))
                last.then_inc(summed[j], 1)

            PEE = mybir.EngineType.PE
            flip(4 * ITERS, 0)
            flip(4 * ITERS, 1)
            spread_pair(4 * ITERS, 0, block_starts(PEE, 0, 0, 0, 1)[0])

            def body4(i, last):
                l = i - 4 * ITERS
                first = block_starts(PEE, 0, l, 1, SP_IT - 1)
                if not last:
                    first = (*first, *block_starts(PEE, 0, l + 1, 0, 1))
                for j in range(SP_IT):
                    if (nxt := ahead(i, j, 1, last)) is not None:
                        spread_pair(*nxt, first[j])
                    if (nxt := ahead(i, j, 2, last)) is not None:
                        flip(*nxt)
                    sum_hidden(i, j)

            iterations(pe, 4, body4)
            for j in range(SP_IT):
                pe.wait_ge(added[j], 5 * ITERS + 1)
            down("down3", W2e, 4, None)
            back("back3", u_ready, lambda n: NT + 2 * (n + 1))


_IN2D = {"L0_gnn_eps_gin": (1, 1), "L2_gnn_eps": (1, 1)}
_NAMES = ["x", "src", "dst", "edge_weight", "edge_weight_n2", "L0_gnn_W1", "L0_gnn_b1", "L0_gnn_g1", "L0_gnn_bt1",
          "L0_gnn_W2", "L0_gnn_b2", "L0_gnn_g2", "L0_gnn_bt2", "L0_gnn_eps_gin", "L1_gnn_gamma", "L1_gnn_beta",
          "L1_gnn_W_in", "L1_gnn_b_in", "L1_gnn_W_out", "L1_gnn_b_out", "L1_gnn_W_x2i", "L1_gnn_b_x2i",
          "L1_gnn_W_h2h", "L2_gnn_eps", "L2_gnn_W1", "L2_gnn_b1", "L2_gnn_g1", "L2_gnn_be1", "L2_gnn_W2", "L2_gnn_b2",
          "L2_gnn_g2", "L2_gnn_be2", "L3_gnn_W1", "L3_gnn_b1", "L3_gnn_W2", "L3_gnn_b2"]


def kernel(**inputs):
    import numpy as np
    import concourse.bacc as bacc
    from concourse import mybir as mb
    from concourse.bass_utils import run_bass_kernel_spmd

    nc = bacc.Bacc("TRN2", target_bir_lowering=False, num_devices=1)
    arrays, aps = {}, {}
    for name in _NAMES:
        arr = np.ascontiguousarray(inputs[name])
        if name in _IN2D:
            arr = arr.reshape(_IN2D[name])
        arrays[f"in_{name}"] = arr
        aps[name] = nc.dram_tensor(f"in_{name}", arr.shape, mb.dt.from_np(arr.dtype), kind="ExternalInput").ap()
    out = nc.dram_tensor("out_x", (N, D), mb.dt.float32, kind="ExternalOutput").ap()
    gnn_kernel(nc, aps, out)
    r = run_bass_kernel_spmd(nc, [arrays], core_ids=[0])
    return r.results[0]["out_x"]
```

```python
import concourse.bass as bass
from concourse import mybir
from contextlib import ExitStack

P = 128
N = 3125
D = 256
E = 50000
EP = 125
EC = E // EP
NB = -(-N // P)
LAST = N - (NB - 1) * P
NP = NB * P
PAIR = 2 * P
PAIRS = (E + NB * (PAIR - 1)) // PAIR
CHUNKS = 2 * PAIRS
SP_IT = 5
CH_IT = 2 * SP_IT
ITERS = PAIRS // SP_IT
assert ITERS * SP_IT == PAIRS and EP * EC == E
LEAD = 2
TAB = 8
HID = 512
W = 448
NT = -(-N // W)
LN_EPS = 1e-5
SC = 10
SIT = EC // (2 * SC)
NORM_AT = 4
SPLIT = 5
RING = 5
PIT = SIT - NORM_AT
ROUNDS = EC // (PIT * RING)
COLS = ROUNDS * RING
FIELDS = 7
PARTS = FIELDS - 2
assert PIT * COLS == EC
MID = N // 2
GROUP = 5


def rows(t):
    return LAST if t == NB - 1 else P


def width(n):
    return min(W, N - n * W)


def cols(n):
    return slice(n * W, n * W + width(n))


def gnn_kernel(nc, a, out):
    f32, bf16, f16, i32 = mybir.dt.float32, mybir.dt.bfloat16, mybir.dt.float16, mybir.dt.int32
    ALU, ACT, AX = mybir.AluOpType, mybir.ActivationFunctionType, mybir.AxisListType
    ds = bass.ds

    table = nc.dram_tensor("table", [N, D], f32).ap()
    qtable = nc.dram_tensor("qtable", [N, HID], f32).ap()
    xpark = nc.dram_tensor("xpark", [N, D], f32).ap()
    degrow = nc.dram_tensor("degrow", [1, N], f32).ap()
    recs_dram = [nc.dram_tensor(f"recs_{k}", [P * CHUNKS, 4], f32).ap() for k in range(SPLIT)]

    ctx = ExitStack()
    with ctx:
        def sb(name, shape, dt):
            return ctx.enter_context(nc.sbuf_tensor(name, shape, dt))

        def sem(name):
            return ctx.enter_context(nc.semaphore(name))

        def sems(name, n):
            return [sem(f"{name}{k}") for k in range(n)]

        x = sb("x", [P, NB * D], f32)
        xt = x[:, :].rearrange("p (t f) -> p t f", t=NB)
        TTm = sb("TT", [P, 2 * N], f32)
        TT = TTm[:, :].rearrange("p (k n) -> p k n", k=2)
        acc = sb("acc", [P, 2 * 3 * NP], f32)
        sums = [acc[:, o * 3 * NP:(o + 1) * 3 * NP].rearrange("p (k n) -> p k n", k=3) for o in range(2)]
        Hm = sb("H", [P, 4 * NP + 260], f32)
        H = Hm[:, 0:4 * NP].rearrange("p (k n) -> p k n", k=4)
        Tm = Hm[:, 0:NB * D].rearrange("p (t f) -> p t f", t=NB)
        g0 = NB * D
        rowsbuf = Hm[:, g0:g0 + CH_IT * D].rearrange("p (c f) -> p c f", c=CH_IT)
        w0 = g0 + CH_IT * D
        Win = Hm[:, w0:w0 + 512].rearrange("p (k n) -> p k n", k=2)
        Wout = Hm[:, w0 + 512:w0 + 1024].rearrange("p (k n) -> p k n", k=2)
        Wx2i = Hm[:, w0 + 1024:w0 + 3072].rearrange("p (k n) -> p k n", k=4)
        Wh2h = Hm[:, w0 + 3072:w0 + 4096].rearrange("p (k n) -> p k n", k=2)
        W1e = Hm[:, w0:w0 + 2048].rearrange("p (k n) -> p k n", k=4)
        recs = [sb(f"rec{o}", [P, CHUNKS, 4], f32) for o in range(2)]
        Wm = sb("Wm", [P, 2048], f32)
        W1a = Wm[:, 0:1024].rearrange("p (k n) -> p k n", k=2)
        W2a = Wm[:, 1024:2048].rearrange("p (k n) -> p k n", k=4)
        W1c = Wm[:, 0:512].rearrange("p (k n) -> p k n", k=2)
        W2c = Wm[:, 512:1024].rearrange("p (k n) -> p k n", k=2)
        W2e = Wm[:, 1024:2048].rearrange("p (k n) -> p k n", k=4)
        b1bc = Wm[:, 0:HID]
        oh = sb("oh", [P, CH_IT, P], f32)
        iota1 = sb("iota1", [P, P], f32)
        ident = sb("ident", [P, P], f32)
        identb = sb("identb", [P, P], bf16)
        ones = sb("ones", [P, P], f32)
        stg_idx = sb("stg_idx", [P, CH_IT], i32)
        stg_lw = sb("stg_lw", [P, CH_IT, 3], f32)
        blk_tabs = sb("blk_tabs", [64, TAB * ITERS], i32)
        blk_tab = [blk_tabs[32 * o:32 * o + 1, :] for o in range(2)]
        vec = sb("vec", [P, 48], f32)
        lnst = sb("lnst", [P, GROUP, 6], f32)
        lnmv = sb("lnmv", [P, NB, 2], f32)
        lnr = sb("lnr", [P, NB], f32)
        lnb = sb("lnb", [P, NB], f32)
        bst = sb("bst", [P, 4, NT, 6], f32)
        bmv = sb("bmv", [P, 4, 2], f32)
        bA = sb("bA", [P, 4], f32)
        bC = sb("bC", [P, 4], f32)
        epst = sb("epst", [P, 1], f32)

        mask = acc[0:EP, 0:NB * EC // 2].bitcast(bf16).rearrange("p (b c) -> p b c", b=NB)
        run0 = NB * EC // 2
        run = acc[0:EP, run0:run0 + NB * EC].rearrange("p (b c) -> p b c", b=NB)
        key_i = [Hm[0:EP, 0:EC].bitcast(i32), Hm[0:EP, EC:2 * EC].bitcast(i32)]
        wts = [Hm[0:EP, 2 * EC:3 * EC], Hm[0:EP, 3 * EC:4 * EC]]
        ti = Hm[0:EP, 4 * EC:5 * EC].bitcast(i32)
        ti2 = Hm[0:EP, 5 * EC:6 * EC].bitcast(i32)
        blkf = Hm[0:EP, 6 * EC:7 * EC]
        pos = Hm[0:EP, 7 * EC:8 * EC]
        slot = TTm[0:EP, 0:EC]
        erec = TTm[0:EP, EC:5 * EC].rearrange("p (c r) -> p c r", r=4)
        fields = TTm[0:EP, 5 * EC:(5 + FIELDS) * EC].rearrange("p (c r) -> p c r", r=FIELDS)
        part16 = TTm[0:EP, (5 + FIELDS) * EC:(5 + FIELDS) * EC + EC // 2].bitcast(bf16)
        r0 = g0 + CH_IT * D
        hi_ring = Hm[0:EP, r0:r0 + RING * CHUNKS // 2].bitcast(bf16).rearrange("p (s c) -> p s c", s=RING)
        r1 = r0 + RING * CHUNKS // 2
        src_ring = Hm[0:EP, r1:r1 + RING * P // 2].bitcast(f16).rearrange("p (s n) -> p s n", s=RING)
        r2 = r1 + RING * P // 2
        val_ring = Hm[0:EP, r2:r2 + RING * 4 * P // 2].bitcast(bf16).rearrange("p (s v n) -> p s v n", s=RING, v=4)
        r3 = r2 + RING * 4 * P // 2
        zero16 = Hm[0:EP, r3:r3 + CHUNKS // 2].bitcast(bf16)
        r4 = r3 + CHUNKS // 2
        iota_hi = Hm[0:EP, r4:r4 + CHUNKS // 2].bitcast(f16)
        r5 = r4 + CHUNKS // 2
        iota_lo = Hm[0:EP, r5:r5 + P // 2].bitcast(f16)
        r6 = r5 + P // 2
        held = Hm[0:EP, r6:r6 + COLS * FIELDS].rearrange("p (h c r) -> p h c r", h=ROUNDS, r=FIELDS)
        r7 = r6 + COLS * FIELDS
        lo_ring = Hm[0:EP, r7:r7 + RING * P // 2].bitcast(bf16).rearrange("p (s n) -> p s n", s=RING)
        assert r7 + RING * P // 2 <= 4 * NP + 260
        zeros = Hm[:, 8 * EC:8 * EC + 4 * CHUNKS]
        tri = Hm[0:EP, 8 * EC + 4 * CHUNKS:8 * EC + 4 * CHUNKS + EP]
        iota_b = Hm[0:P, 8 * EC + 4 * CHUNKS + P:8 * EC + 4 * CHUNKS + P + NB]
        ends0 = 8 * EC + 4 * CHUNKS + 2 * P
        pstart = Hm[:, ends0:ends0 + PAIRS]
        lt0 = ends0 + PAIRS
        pairlt = acc[:, 0:PAIRS * (NB - 1)].rearrange("p (j b) -> p j b", b=NB - 1)
        pairbf = Hm[:, lt0:lt0 + PAIRS]
        srt0 = lt0 + PAIRS
        srt = Hm[:, srt0:srt0 + 5 * NB].rearrange("p (k b) -> p k b", b=NB)
        srti = Hm[:, srt0 + 5 * NB:srt0 + 6 * NB].bitcast(i32)
        sst_idx = oh[0:EP, 0:1, 0:2 * SC].bitcast(i32).rearrange("p a c -> p (a c)")
        sst_rec = oh[0:EP, 1:3, :].rearrange("p a c -> p (a c)")[:, 0:2 * SC * 4].rearrange(
            "p (c r) -> p c r", r=4)

        part = [acc[:, 3 * NP + k * 4 * CHUNKS:3 * NP + (k + 1) * 4 * CHUNKS].rearrange("p (c r) -> p c r", r=4)
                for k in range(SPLIT - 1)]

        quad = [Hm[:, q * 4 * W:(q + 1) * 4 * W].rearrange("p (f n) -> p f n", f=4) for q in range(4)]
        AB, GT = quad[0:2], quad[2:4]
        U = sums[0]
        PT = acc[:, 0:NB * 3 * HID // 2].bitcast(bf16).rearrange("p (b r f) -> p b r f", b=NB, r=3)
        PTf = acc[:, 0:NB * 3 * HID // 2].bitcast(bf16)
        hbuf = x[:, 0:CH_IT * HID].rearrange("p (c f) -> p c f", c=CH_IT)
        pf = [x[:, CH_IT * HID + q * HID:CH_IT * HID + (q + 1) * HID] for q in range(2)]
        qst = rowsbuf.rearrange("p c f -> p (c f)").rearrange("p (q f) -> p q f", f=HID)
        QS = 5
        OB = CH_IT // 2
        ohb, ohT = (TTm[:, N + q * OB * P // 2:N + (q + 1) * OB * P // 2].bitcast(bf16).rearrange(
            "p (c n) -> p c n", n=P) for q in range(2))
        deg = TT[:, 0, :]
        rdeg = TT[:, 1, :]

        VCOL, at = {}, 0
        for name, n in (("L0_gnn_b1", 4), ("L0_gnn_g1", 4), ("L0_gnn_bt1", 4), ("L0_gnn_b2", 2),
                        ("L0_gnn_g2", 2), ("L0_gnn_bt2", 2), ("L1_gnn_gamma", 2), ("L1_gnn_beta", 2),
                        ("L1_gnn_b_in", 2), ("L1_gnn_b_out", 2), ("L1_gnn_b_x2i", 4),
                        ("L2_gnn_b1", 2), ("L2_gnn_g1", 2), ("L2_gnn_be1", 2), ("L2_gnn_b2", 2),
                        ("L2_gnn_g2", 2), ("L2_gnn_be2", 2), ("L3_gnn_b2", 2)):
            VCOL[name] = (at, n)
            at += n
        eps_col = {0: at, 2: at + 1}
        NVEC = len(VCOL) + 2

        def v(name, k=None):
            o, n = VCOL[name]
            return vec[:, o:o + n] if k is None else vec[:, o + k:o + k + 1]

        ps = [ctx.enter_context(nc.psum_tensor(f"ps{b}", [P, 512], f32)) for b in range(8)]

        def flip_bank(c):
            return ps[5 + c % 2][:, 0:P // 2].bitcast(bf16)

        def spread_bank(c):
            return ps[3 + c % 2][:, :]

        CONSTS = 13

        edges_loaded = sem("edges_loaded")
        x_loaded = sem("x_loaded")
        vec_loaded = sem("vec_loaded")
        w_loaded = sems("w_loaded", 4)
        b1_loaded = sem("b1_loaded")
        consts = sem("consts")
        stages_begun = sem("stages_begun")
        zero_filled = sem("zero_filled")
        held_ready = sem("held_ready")
        lo_made = sem("lo_made")
        made = sem("made")
        weighed = sem("weighed")
        used = sem("used")
        placed = sem("placed")
        rec0_ready = sem("rec0_ready")
        vstep = sem("vstep")
        totals_ready = sem("totals_ready")
        order_ready = sem("order_ready")
        sc_staged = sems("sc_staged", 2)
        sc_done = sems("sc_done", SPLIT)
        merged = sem("merged")
        rec_loaded = sem("rec_loaded")
        filled = sems("filled", 8)
        emptied = sems("emptied", 8)
        ln_ready = sem("ln_ready")
        std_ready = sem("std_ready")
        normed = sem("normed")
        tab_written = sem("tab_written")
        bn_var = sem("bn_var")
        bn_std = sem("bn_std")
        bn_ready = sem("bn_ready")
        act_ready = sem("act_ready")
        staged = sems("staged", SP_IT)
        landed = sems("landed", SP_IT)
        hot = sems("hot", SP_IT)
        summed = sems("summed", SP_IT)
        added = sems("added", SP_IT)
        sums_clear = sem("sums_clear")
        last_clear = sem("last_clear")
        z_ready = sem("z_ready")
        scaled = sem("scaled")
        u_ready = sem("u_ready")
        deg_stored = sem("deg_stored")
        deg_loaded = sem("deg_loaded")
        parked = sem("parked")
        unparked = sem("unparked")
        q_stored = sems("q_stored", QS)
        wdiff = sem("wdiff")
        p_sum = sem("p_sum")
        p_hi = sem("p_hi")
        p_ready = sem("p_ready")
        hotb = sem("hotb")
        flipped = sem("flipped")
        flip_copied = sems("flip_copied", CH_IT)
        spread = sems("spread", CH_IT)
        joined = sems("joined", CH_IT)
        relued = sem("relued")
        out_stored = sem("out_stored")

        fills = [0] * 8
        jobs = {}

        def plan(stage, count, banks=range(8)):
            banks = list(banks)
            jobs[stage] = []
            for k in range(count):
                b = banks[k % len(banks)]
                fills[b] += 1
                jobs[stage].append((b, fills[b]))

        TG = [(g, min(4, NB - 4 * g)) for g in range(-(-NB // 4))]
        for o in range(2):
            plan(f"count{o}", 1, [6 + o])
        plan("T0", 2 * len(TG), range(PARTS, 8))
        plan("up0", 4 * NT)
        plan("down0", 2 * NT)
        plan("back0", NB)
        plan("T1", 2 * len(TG))
        jobs["ab1"], jobs["gates1"] = [], []
        banks = iter(range(16 * NT))

        def plan_more(stage):
            for _ in range(4):
                b = next(banks) % 8
                fills[b] += 1
                jobs[stage].append((b, fills[b]))

        plan_more("ab1")
        for n in range(NT):
            if n + 1 < NT:
                plan_more("ab1")
            plan_more("gates1")
        plan("back1", NB)
        plan("T2", 2 * len(TG))
        plan("up2", 2 * NT)
        plan("down2", 2 * NT)
        plan("back2", NB)
        plan("T3", 2 * len(TG))
        plan("q3", NB)
        plan("p3", NB)
        plan("down3", 2 * NT)
        plan("back3", NB)

        def wait_filled(eng, stage, k):
            b, c = jobs[stage][k]
            eng.wait_ge(filled[b], c)
            return ps[b]

        def wait_emptied(eng, stage, k):
            b, c = jobs[stage][k]
            eng.wait_ge(emptied[b], c)

        def bank(stage, k):
            return jobs[stage][k][0]

        def block_starts(eng, o, row, first, count):
            at = row * TAB + first
            return nc.values_load_multi_w_load_instructions(
                blk_tab[o][:, ds(at, count)], engines=[eng], min_val=0, max_val=(NB - 1) * P,
                skip_runtime_bounds_check_because="a count of blocks times their nodes")[1]

        def iterations(eng, n, body):
            with eng.Fori(n * ITERS, (n + 1) * ITERS - 1) as i:
                body(i, False)
            body((n + 1) * ITERS - 1, True)

        def ahead(i, j, d, last):
            if j + d < SP_IT:
                return i, j + d
            return None if last else (i + 1, j + d - SP_IT)

        PASSES = [(0, None, 0), (0, 1, 0), (1, 2, 1), (1, 1, 0), (0, None, 0)]
        ORDER = ["count1", "count0", "T0", "up0", "down0", "back0", "T1", "ab1", "gates1", "back1", "T2", "up2",
                 "down2", "back2", "T3", "q3", "p3", "down3", "back3"]

        block = ctx.enter_context(nc.Block())

        @block.sync
        def _(sp):
            def edge_view(name):
                return a[name].rearrange("(p c) -> p c", p=EP)

            sp.dma_start(key_i[0], edge_view("dst")).then_inc(edges_loaded, 16)
            sp.dma_start(key_i[1], edge_view("src")).then_inc(edges_loaded, 16)
            sp.dma_start(wts[0], edge_view("edge_weight")).then_inc(edges_loaded, 16)
            sp.dma_start(wts[1], edge_view("edge_weight_n2")).then_inc(edges_loaded, 16)
            nfull = NB - 1

            def tiles(dram):
                return (dram[0:nfull * P, :].rearrange("(t p) f -> p t f", p=P), dram[nfull * P:N, :])

            main, tail = tiles(a["x"])
            sp.dma_start(xt[:, 0:nfull, :], main).then_inc(x_loaded, 16)
            sp.dma_start(xt[0:LAST, nfull, :], tail).then_inc(x_loaded, 16)
            with nc.allow_non_contiguous_dma(reason="per-feature vectors"):
                for name, (o, n) in VCOL.items():
                    sp.dma_start(vec[:, o:o + n], a[name].rearrange("(k p) -> p k", p=P)).then_inc(vec_loaded, 16)
            sp.dma_start(vec[:, eps_col[0]:eps_col[0] + 1],
                         a["L0_gnn_eps_gin"].to_broadcast([P, 1])).then_inc(vec_loaded, 16)
            sp.dma_start(vec[:, eps_col[2]:eps_col[2] + 1],
                         a["L2_gnn_eps"].to_broadcast([P, 1])).then_inc(vec_loaded, 16)

            def weight(dst, name, s):
                sp.dma_start(dst, a[name].rearrange("(k p) n -> p k n", p=P)).then_inc(s, 16)

            weight(W1a, "L0_gnn_W1", w_loaded[0])
            weight(W2a, "L0_gnn_W2", w_loaded[0])
            sp.wait_ge(consts, 1)
            for k in range(SPLIT):
                sp.dma_start(recs_dram[k].rearrange("(p c) r -> p (c r)", p=P), zeros).then_inc(zero_filled, 16)
            def store_table(layer):
                for gidx in range(NB // GROUP):
                    sp.wait_ge(normed, layer * NB + (gidx + 1) * GROUP)
                    t0, t1 = gidx * GROUP, (gidx + 1) * GROUP
                    full = min(t1, nfull)
                    sp.dma_start(table[t0 * P:full * P, :].rearrange("(t p) f -> p t f", p=P),
                                 Tm[:, t0:full, :]).then_inc(tab_written, 16)
                sp.dma_start(table[nfull * P:N, :], Tm[0:LAST, nfull, :]).then_inc(tab_written, 16)

            store_table(0)
            for k in range(SPLIT):
                sp.wait_ge(sc_done[k], 16 * (EC // SPLIT))
                sp.dma_start(recs[1][:, :, :] if k == 0 else part[k - 1],
                             recs_dram[k].rearrange("(p c) r -> p c r", p=P)).then_inc(rec_loaded, 16)
            for j in range(SP_IT):
                sp.wait_ge(added[j], ITERS + 1)
            sp.dma_start(degrow, sums[0][0:1, 2, 0:N]).then_inc(deg_stored, 16)
            b, c = jobs["down0"][-1]
            sp.wait_ge(filled[b], c)
            weight(W1c, "L2_gnn_W1", w_loaded[2])
            weight(W2c, "L2_gnn_W2", w_loaded[2])
            weight(W2e, "L3_gnn_W2", w_loaded[3])
            weight(Win, "L1_gnn_W_in", w_loaded[1])
            weight(Wout, "L1_gnn_W_out", w_loaded[1])
            weight(Wx2i, "L1_gnn_W_x2i", w_loaded[1])
            weight(Wh2h, "L1_gnn_W_h2h", w_loaded[1])
            store_table(1)
            store_table(2)
            b, c = jobs["gates1"][-1]
            sp.wait_ge(filled[b], c)
            weight(W1e, "L3_gnn_W1", w_loaded[3])
            b, c = jobs["down2"][-1]
            sp.wait_ge(filled[b], c)
            sp.dma_start(b1bc, a["L3_gnn_b1"].rearrange("(o n) -> o n", o=1).to_broadcast([P, HID])).then_inc(b1_loaded, 16)
            sp.wait_ge(normed, 4 * NB)
            main, tail = tiles(xpark)
            sp.dma_start(main, xt[:, 0:nfull, :]).then_inc(parked, 16)
            sp.dma_start(tail, xt[0:LAST, nfull, :]).then_inc(parked, 16)
            for t in range(NB):
                wait_emptied(sp, "q3", t)
                sp.dma_start(qtable[t * P:t * P + rows(t), :], qst[0:rows(t), t % QS, :]).then_inc(q_stored[t % QS], 16)
            b, c = jobs["p3"][-1]
            sp.wait_ge(filled[b], c)
            sp.wait_ge(deg_stored, 16)
            sp.dma_start(deg, degrow.to_broadcast([P, N])).then_inc(deg_loaded, 16)
            sp.wait_ge(parked, 32)
            for j in range(SP_IT):
                sp.wait_ge(summed[j], 5 * ITERS + 1)
            sp.dma_start(xt[:, 0:nfull, :], main).then_inc(unparked, 16)
            sp.dma_start(xt[0:LAST, nfull, :], tail).then_inc(unparked, 16)
            for gidx in range(NB // GROUP):
                for t in range(gidx * GROUP, (gidx + 1) * GROUP):
                    wait_emptied(sp, "back3", t)
                t0, t1 = gidx * GROUP, (gidx + 1) * GROUP
                full = min(t1, nfull)
                sp.dma_start(out[t0 * P:full * P, :].rearrange("(t p) f -> p t f", p=P),
                             xt[:, t0:full, :]).then_inc(out_stored, 16)
            sp.dma_start(out[nfull * P:N, :], xt[0:LAST, nfull, :]).then_inc(out_stored, 16)
            sp.wait_ge(out_stored, 16 * (NB // GROUP + 1))

        @block.gpsimd
        def _(pool):
            nc.gpsimd.memset(zeros, 0.0).then_inc(consts, 1)
            nc.gpsimd.iota(iota1[:, :], [[1, P]], base=1, channel_multiplier=0,
                           allow_small_or_imprecise_dtypes=True).then_inc(consts, 1)
            nc.gpsimd.iota(iota_b, [[1, NB]], base=0, channel_multiplier=0,
                           allow_small_or_imprecise_dtypes=True).then_inc(consts, 1)
            nc.gpsimd.iota(pstart, [[PAIR, PAIRS]], base=0, channel_multiplier=0,
                           allow_small_or_imprecise_dtypes=True).then_inc(consts, 1)
            nc.gpsimd.memset(ones[:, :], 1.0).then_inc(consts, 1)
            nc.gpsimd.memset(ident[:, :], 0.0).then_inc(consts, 1)
            nc.gpsimd.memset(tri, 1.0).then_inc(consts, 1)
            nc.gpsimd.memset(zero16, 0.0).then_inc(consts, 1)
            nc.gpsimd.iota(iota_hi, [[1, CHUNKS]], base=0, channel_multiplier=0,
                           allow_small_or_imprecise_dtypes=True).then_inc(consts, 1)
            nc.gpsimd.iota(iota_lo, [[1, P]], base=0, channel_multiplier=0,
                           allow_small_or_imprecise_dtypes=True).then_inc(consts, 1)
            pool.wait_ge(consts, 10)
            nc.gpsimd.affine_select(out=ident[:, :], in_=ident[:, :], compare_op=ALU.not_equal, fill=1.0, base=0,
                                    pattern=[[-1, P]], channel_multiplier=1).then_inc(consts, 1)
            nc.gpsimd.affine_select(out=tri, in_=tri, compare_op=ALU.is_gt, fill=0.0, base=0,
                                    pattern=[[1, EP]], channel_multiplier=-1).then_inc(consts, 1)
            pool.wait_ge(consts, CONSTS - 1)
            nc.gpsimd.tensor_copy(identb[:, :], ident[:, :]).then_inc(consts, 1)

            def scatter_stage(i):
                for q in range(2):
                    pool.wait_ge(sc_staged[q], i + 1)
                    pool.sem_inc(stages_begun, 1)
                    for k in range(SC):
                        s = q * SC + k
                        if not isinstance(i, int) or s >= SPLIT:
                            pool.wait_ge(sc_done[k % SPLIT], 16 * (2 * q + k // SPLIT) + i * (32 * SC // SPLIT))
                            pool.sem_inc(stages_begun, 1)
                        pool.indirect_dma_start(
                            out=recs_dram[k % SPLIT],
                            out_offset=bass.IndirectOffsetOnAxis(ap=sst_idx[:, s:s + 1], axis=0),
                            in_=sst_rec[:, s, :], in_offset=None).then_inc(sc_done[k % SPLIT], 16)

            def gathers(n, src, dst):
                with pool.Fori(n * ITERS, (n + 1) * ITERS) as i:
                    for j in range(SP_IT):
                        pool.wait_ge(staged[j], i + 1)
                        pool.sem_inc(stages_begun, 1)
                        for c in (2 * j, 2 * j + 1):
                            pool.indirect_dma_start(
                                out=dst[:, c, :], out_offset=None, in_=src,
                                in_offset=bass.IndirectOffsetOnAxis(ap=stg_idx[:, c:c + 1], axis=0)
                            ).then_inc(landed[j], 16)

            def table_ready(layer):
                pool.wait_ge(tab_written, 16 * (NB // GROUP + 1) * (layer + 1))

            def clear(which):
                nc.gpsimd.memset(acc[:, which * 3 * NP:(which + 1) * 3 * NP], 0.0).then_inc(sums_clear, 1)

            def all_filled(st):
                b, c = jobs[st][-1]
                pool.wait_ge(filled[b], c)

            pool.wait_ge(zero_filled, 16 * SPLIT)
            scatter_stage(0)
            with pool.Fori(1, SIT) as i:
                scatter_stage(i)
            pool.wait_ge(order_ready, 2)
            clear(0)
            table_ready(0)
            gathers(0, table, rowsbuf)
            pool.wait_ge(rec_loaded, 16 * SPLIT)
            for k in range(SPLIT - 1):
                nc.gpsimd.tensor_tensor(recs[1][:, :, :], recs[1][:, :, :], part[k], ALU.add).then_inc(merged, 1)
                pool.wait_ge(merged, k + 1)
            clear(1)
            all_filled("back0")
            pool.wait_ge(deg_stored, 16)
            clear(0)
            table_ready(1)
            gathers(1, table, rowsbuf)
            gathers(2, table, rowsbuf)
            all_filled("back1")
            clear(0)
            table_ready(2)
            gathers(3, table, rowsbuf)
            all_filled("T3")
            nc.gpsimd.memset(Hm[:, 0:NB * D], 0.0).then_inc(sums_clear, 1)
            pool.wait_ge(parked, 32)
            for q in range(QS):
                pool.wait_ge(q_stored[q], 16 * (NB // QS))
            gathers(4, qtable, hbuf)

        @block.scalar
        def _(act):
            def stage_half(i, q):
                uses = 2 * SC // SPLIT
                if not isinstance(i, int):
                    for k in range(SPLIT):
                        act.wait_ge(sc_done[k], i * (16 * uses) + (0 if q else -8 * uses))
                c0 = i * (2 * SC) + q * SC
                nc.scalar.copy(sst_idx[:, q * SC:(q + 1) * SC], slot[:, ds(c0, SC)])
                nc.scalar.copy(sst_rec[:, q * SC:(q + 1) * SC, :], erec[:, ds(c0, SC), :]).then_inc(sc_staged[q], 1)

            def stage_scatter(first, end):
                with act.Fori(first, end) as i:
                    for q in range(2):
                        stage_half(i, q)

            def weigh(n, m, c):
                act.wait_ge(lo_made, n + 1)
                for k in range(1, 4):
                    last = nc.scalar.activation(val_ring[:, c, k, :], lo_ring[:, c, :], ACT.Copy,
                                                scale=held[:, m, c, 3 + k:4 + k])
                last.then_inc(weighed, 1)

            def deviations(n, t0, m):
                act.wait_ge(ln_ready, n)
                nc.scalar.activation(lnr[:, t0:t0 + m], lnmv[:, t0:t0 + m, 1], ACT.Sqrt,
                                     bias=epst[:, 0:1], scale=1.0).then_inc(std_ready, 1)

            def norm_blocks(n, t0, m):
                act.wait_ge(ln_ready, n)
                for t in range(t0, t0 + m):
                    r = rows(t)
                    nc.scalar.activation(Tm[0:r, t, :], xt[0:r, t, :], ACT.Relu, bias=lnb[0:r, t:t + 1],
                                         scale=lnr[0:r, t:t + 1]).then_inc(normed, 1)

            def norm_rows(layer):
                for g in range(NB // GROUP):
                    n = (layer - 1) * (NB // GROUP) + g + 1
                    deviations(2 * n + 1, g * GROUP, GROUP)
                    norm_blocks(2 * n + 2, g * GROUP, GROUP)

            def take_transposes(layer):
                st = f"T{layer}"
                for g in range(len(TG)):
                    src = wait_filled(act, st, 2 * g)
                    n = min(512, N - 512 * g)
                    nc.scalar.copy(TT[:, 0, 512 * g:512 * g + n], src[:, 0:n]).then_inc(emptied[bank(st, 2 * g)], 1)

            def stage_pair(i, n, j):
                act.wait_ge(summed[j], i + 1)
                c0 = (i - n * ITERS) * CH_IT + 2 * j
                o = PASSES[n][0]
                nc.scalar.copy(stg_lw[:, 2 * j:2 * j + 2, :], recs[o][:, ds(c0, 2), 1:4])
                nc.scalar.copy(stg_idx[:, 2 * j:2 * j + 2], recs[o][:, ds(c0, 2), 0]).then_inc(staged[j], 1)

            def stage_pass(n):
                if PASSES[n][0] == 1:
                    act.wait_ge(merged, SPLIT - 1)
                with act.Fori(n * ITERS, (n + 1) * ITERS) as i:
                    for j in range(SP_IT):
                        stage_pair(i, n, j)

            def take_products(st, bias, dst, nf):
                for n in range(NT):
                    for f in range(nf):
                        src = wait_filled(act, st, n * nf + f)
                        nc.scalar.activation(dst[:, f, cols(n)], src[:, 0:width(n)], ACT.Identity, bias=v(bias, f),
                                             scale=1.0).then_inc(emptied[bank(st, n * nf + f)], 1)

            def bn_deviation(k, nf):
                act.wait_ge(bn_var, k)
                nc.scalar.activation(bA[:, 0:nf], bmv[:, 0:nf, 1], ACT.Sqrt, bias=epst[:, 0:1],
                                     scale=1.0).then_inc(bn_std, 1)
                act.wait_ge(bn_ready, k)

            def scale_tiles(dst, nf, func):
                for n in range(NT):
                    for f in range(nf):
                        nc.scalar.activation(dst[:, f, cols(n)], dst[:, f, cols(n)], func, bias=bC[:, f:f + 1],
                                             scale=bA[:, f:f + 1]).then_inc(act_ready, 1)

            for s in flip_copied:
                act.sem_inc(s, 1)
            act.wait_ge(order_ready, 1)
            stage_half(0, 0)
            stage_half(0, 1)
            stage_scatter(1, NORM_AT)
            deviations(1, 0, NB)
            act.wait_ge(order_ready, 2)
            act.wait_ge(zero_filled, 16 * SPLIT)
            norm_blocks(2, 0, NB)
            with act.Fori(NORM_AT, SIT) as i:
                for k in range(COLS):
                    if k in (0, COLS // 2):
                        stage_half(i, 1 if k else 0)
                    weigh((i - NORM_AT) * COLS + k, k // RING, k % RING)
            act.wait_ge(sc_staged[1], SIT)
            act.wait_ge(rec0_ready, 1)
            take_transposes(0)
            stage_pass(0)
            act.wait_ge(vec_loaded, 16 * NVEC)
            take_products("up0", "L0_gnn_b1", H, 4)
            bn_deviation(1, 4)
            scale_tiles(H, 4, ACT.Relu)
            bn_deviation(2, 2)
            scale_tiles(U, 2, ACT.Relu)
            norm_rows(1)
            take_transposes(1)
            bn_deviation(3, 2)
            scale_tiles(TT, 2, ACT.Identity)
            stage_pass(1)
            stage_pass(2)
            for q in range(2):
                for j in range(SP_IT):
                    act.wait_ge(added[j], (2 + q) * ITERS + 1)
                for k in range(2):
                    nc.scalar.activation(sums[q][:, k, 0:N], sums[q][:, k, 0:N], ACT.Copy,
                                         scale=bA[:, k:k + 1]).then_inc(scaled, 1)
            for n in range(NT):
                if n >= 2:
                    act.wait_ge(u_ready, n - 1)
                for f in range(4):
                    src = wait_filled(act, "gates1", n * 4 + f)
                    nc.scalar.activation(GT[n % 2][:, f, 0:width(n)], src[:, 0:width(n)],
                                         ACT.Sigmoid if f < 2 else ACT.Tanh, bias=v("L1_gnn_b_x2i", f),
                                         scale=1.0).then_inc(emptied[bank("gates1", n * 4 + f)], 1)
            norm_rows(2)
            take_transposes(2)
            stage_pass(3)
            take_products("up2", "L2_gnn_b1", H, 2)
            bn_deviation(4, 2)
            scale_tiles(H, 2, ACT.Relu)
            take_products("down2", "L2_gnn_b2", U, 2)
            bn_deviation(5, 2)
            scale_tiles(U, 2, ACT.Relu)
            norm_rows(3)
            take_transposes(3)
            for t in range(NB):
                src = wait_filled(act, "q3", t)
                if t >= QS:
                    act.wait_ge(q_stored[t % QS], 16 * (t // QS))
                nc.scalar.copy(qst[0:rows(t), t % QS, :], src[0:rows(t), :]).then_inc(
                    emptied[bank("q3", t)], 1)
            for t in range(NB):
                r = rows(t)
                wait_emptied(act, "p3", t)
                if t == NB - 1:
                    act.wait_ge(last_clear, 1)
                nc.scalar.copy(PT[0:r, t, 0, :], pf[t % 2][0:r, :]).then_inc(p_hi, 1)
                act.wait_ge(p_sum, t + 1)
                nc.scalar.copy(PT[0:r, t, 1, :], pf[t % 2][0:r, :]).then_inc(p_hi, 1)

            def flips(i, j):
                l = i - 4 * ITERS
                for c in (2 * j, 2 * j + 1):
                    act.wait_ge(flipped, l * CH_IT + c + 1 + OB)
                    act.wait_ge(spread[(c + OB) % CH_IT], l + 2 if c >= OB else l + 1)
                    nc.scalar.copy(ohT[:, c % OB, :], flip_bank(c)).then_inc(flip_copied[c], 1)

            def relus(i, j):
                for c in (2 * j, 2 * j + 1):
                    act.wait_ge(joined[c], i - 4 * ITERS + 2)
                    nc.scalar.activation(hbuf[:, c, :], hbuf[:, c, :], ACT.Relu).then_inc(relued, 1)

            for j in range(4):
                stage_pair(4 * ITERS, 4, j)
            flips(4 * ITERS, 0)
            flips(4 * ITERS, 1)
            relus(4 * ITERS, 0)

            def body4(i, last):
                for j in range(SP_IT):
                    for d, do in ((4, lambda i, j: stage_pair(i, 4, j)), (2, flips), (1, relus)):
                        if (nxt := ahead(i, j, d, last)) is not None:
                            do(*nxt)

            iterations(act, 4, body4)

        @block.vector
        def _(dve):
            nstep = [0]

            def link(ins):
                nstep[0] += 1
                ins.then_inc(vstep, 1)
                dve.wait_ge(vstep, nstep[0])

            V = nc.vector

            def sort(o):
                key, other = key_i[o], key_i[1 - o]
                link(V.tensor_scalar(ti, key, 7, None, ALU.arith_shift_right))
                link(V.tensor_copy(blkf, ti))
                link(V.tensor_scalar(ti2, key, 127, None, ALU.bitwise_and))
                if o == 1:
                    V.tensor_scalar(erec[:, :, 1], ti2, 1.0, None, ALU.add)
                    V.tensor_copy(erec[:, :, 0], other)
                    V.tensor_copy(erec[:, :, 2], wts[0])
                    V.tensor_copy(erec[:, :, 3], wts[1])
                else:
                    V.tensor_scalar(fields[:, :, 3], ti2, 1.0, None, ALU.add)
                    V.tensor_scalar(fields[:, :, 2], other, float(-MID), None, ALU.add)
                    link(V.tensor_copy(part16, wts[0]))
                    link(V.tensor_copy(fields[:, :, 4], part16))
                    link(V.tensor_tensor(wts[0], wts[0], fields[:, :, 4], ALU.subtract))
                    link(V.tensor_copy(part16, wts[0]))
                    link(V.tensor_copy(fields[:, :, 5], part16))
                    V.tensor_tensor(fields[:, :, 6], wts[0], fields[:, :, 5], ALU.subtract)
                link(V.tensor_tensor(mask, blkf[:, None, :].to_broadcast([EP, NB, EC]),
                                     iota_b[0:EP, :, None].to_broadcast([EP, NB, EC]), ALU.is_equal))
                flat = "p b c -> p (b c)"
                link(V.tensor_tensor_scan(run.rearrange(flat), ones[0:EP, 0:1].to_broadcast([EP, NB * EC]),
                                          mask.rearrange(flat), 0.0, ALU.mult, ALU.add))
                ends, tot, padded, bend, off = (srt[:, k, :] for k in range(5))
                link(V.tensor_copy(ends[0:EP, :], run[:, :, EC - 1]))
                V.tensor_copy(tot[0:EP, 0:1], ends[0:EP, 0:1])
                V.tensor_tensor(tot[0:EP, 1:NB], ends[0:EP, 1:NB], ends[0:EP, 0:NB - 1],
                                ALU.subtract).then_inc(totals_ready, 1)
                cnt = wait_filled(dve, f"count{o}", 0)
                link(V.tensor_scalar(srti[:, :], cnt[:, 32:32 + NB], float(PAIR - 1), None, ALU.add))
                link(V.tensor_scalar(srti[:, :], srti[:, :], 8, 8, ALU.arith_shift_right, ALU.logical_shift_left))
                link(V.tensor_copy(padded, srti[:, :]))
                link(V.tensor_tensor_scan(bend, ones[:, 0:NB], padded, 0.0, ALU.mult, ALU.add))
                e = slice(0, EP)
                link(V.tensor_tensor(off[e], bend[e], padded[e], ALU.subtract))
                V.tensor_tensor(off[e], off[e], cnt[e, 0:NB], ALU.add).then_inc(emptied[bank(f"count{o}", 0)], 1)
                wait_emptied(dve, f"count{o}", 0)
                link(V.tensor_tensor(off[e], off[e], ends[e], ALU.subtract))
                link(V.scalar_tensor_tensor(off[e], off[e], -1.0, tot[e], ALU.add, ALU.add))
                link(V.tensor_tensor(run, run, off[e][:, :, None].to_broadcast([EP, NB, EC]), ALU.add))
                link(V.tensor_tensor(run, run, mask, ALU.mult))
                link(V.tensor_reduce(pos, run.rearrange("p b c -> p c b"), AX.X, ALU.add))
                link(V.tensor_copy(ti, pos))
                V.tensor_scalar(ti2, ti, P - 1, None, ALU.bitwise_and)
                link(V.tensor_scalar(ti, ti, 7, None, ALU.arith_shift_right))
                if o == 1:
                    link(V.scalar_tensor_tensor(slot, ti2, float(CHUNKS), ti, ALU.mult, ALU.add))
                else:
                    V.tensor_copy(fields[:, :, 0], ti2)
                    link(V.tensor_copy(fields[:, :, 1], ti))
                q = slice(32 * o, 32 * o + 1)
                link(V.tensor_tensor(pairlt[q], pstart[q][:, :, None].to_broadcast([1, PAIRS, NB - 1]),
                                     bend[q][:, None, 0:NB - 1].to_broadcast([1, PAIRS, NB - 1]), ALU.is_ge))
                link(V.tensor_reduce(pairbf[q], pairlt[q], AX.X, ALU.add))
                V.tensor_scalar(blk_tab[o].rearrange("p (i j) -> p i j", j=TAB)[:, :, 0:SP_IT],
                                pairbf[q].rearrange("p (i j) -> p i j", j=SP_IT), float(P), None,
                                ALU.mult).then_inc(order_ready, 1)
                dve.wait_ge(order_ready, 2 - o)

            def ln_stats(g, back=None):
                stats = []
                for t in range(g * GROUP, (g + 1) * GROUP + 2):
                    if back is not None and t < (g + 1) * GROUP:
                        add_back(back, t)
                    if g * GROUP <= t - 1 < (g + 1) * GROUP:
                        r = rows(t - 1)
                        if back is not None:
                            wait_emptied(dve, back, t - 1)
                        V.bn_stats(lnst[0:r, (t - 1) % GROUP, :], xt[0:r, t - 1, :]).then_inc(vstep, 1)
                        nstep[0] += 1
                        stats.append(nstep[0])
                    if g * GROUP <= t - 2:
                        r = rows(t - 2)
                        dve.wait_ge(vstep, stats[t - 2 - g * GROUP])
                        last = V.bn_aggr(lnmv[0:r, t - 2, :], lnst[0:r, (t - 2) % GROUP, :])
                return last

            def ln_scale(n, sl):
                dve.wait_ge(std_ready, n)
                dve.wait_ge(ln_ready, 2 * n - 1)
                link(V.reciprocal(lnr[:, sl], lnr[:, sl]))
                V.scalar_tensor_tensor(lnb[:, sl], lnmv[:, sl, 0], -1.0, lnr[:, sl], ALU.mult,
                                       ALU.mult).then_inc(ln_ready, 1)

            def layer_norm(layer, back):
                for g in range(NB // GROUP):
                    ln_stats(g, back).then_inc(ln_ready, 1)
                    ln_scale((layer - 1) * (NB // GROUP) + g + 2, slice(g * GROUP, (g + 1) * GROUP))

            def add_back(st, t):
                r = rows(t)
                src = wait_filled(dve, st, t)
                V.tensor_tensor(xt[0:r, t, :], xt[0:r, t, :], src[0:r, 0:D], ALU.add).then_inc(
                    emptied[bank(st, t)], 1)

            def take_transposes(layer):
                st = f"T{layer}"
                for g in range(len(TG)):
                    src = wait_filled(dve, st, 2 * g + 1)
                    n = min(512, N - 512 * g)
                    V.tensor_copy(TT[:, 1, 512 * g:512 * g + n], src[:, 0:n]).then_inc(emptied[bank(st, 2 * g + 1)], 1)
                wait_emptied(dve, st, 2 * len(TG) - 2)
                wait_emptied(dve, st, 2 * len(TG) - 1)

            def make_hot(i, j, wcol):
                dve.wait_ge(staged[j], i + 1)
                for c in (2 * j, 2 * j + 1):
                    if wcol is None:
                        last = V.tensor_scalar(oh[:, c, :], iota1[:, :], stg_lw[:, c, 0:1], None, ALU.is_equal)
                    else:
                        last = V.tensor_scalar(oh[:, c, :], iota1[:, :], stg_lw[:, c, 0:1], stg_lw[:, c, wcol:wcol + 1],
                                               ALU.is_equal, ALU.mult)
                last.then_inc(hot[j], 1)

            def add_pair(i, j, dst, src, block0, slots):
                dve.wait_ge(summed[j], i + 2)
                dve.wait_ge(added[(j - 1) % SP_IT], i + 2 if j else i + 1)
                at = dst[:, 0:slots, ds(block0, P)]
                V.tensor_tensor(at, at, src.rearrange("p (k n) -> p k n", k=slots), ALU.add).then_inc(added[j], 1)

            def sum_pass(n):
                o, wcol, d = PASSES[n]

                def body(i, last):
                    first = block_starts(mybir.EngineType.DVE, o, i - n * ITERS, 0, SP_IT)
                    for j in range(SP_IT):
                        if (nxt := ahead(i, j, LEAD, last)) is not None:
                            make_hot(*nxt, wcol)
                        add_pair(i, j, sums[d], ps[j][:, 0:3 * P], first[j], 3)

                for j in range(LEAD):
                    make_hot(n * ITERS, j, wcol)
                iterations(dve, n, body)
                dve.wait_ge(added[SP_IT - 1], (n + 1) * ITERS + 1)

            def gin_input(col):
                for n in range(NT):
                    for k in range(2):
                        V.scalar_tensor_tensor(sums[0][:, k, cols(n)], TT[:, k, cols(n)], vec[:, col:col + 1],
                                               sums[0][:, k, cols(n)], ALU.mult, ALU.add).then_inc(z_ready, 1)

            def bn_scale(k, nf, gamma, beta):
                for f in range(nf):
                    last = V.bn_aggr(bmv[:, f, :], bst[:, f, :, :].rearrange("p n s -> p (n s)"))
                last.then_inc(bn_var, 1)
                dve.wait_ge(bn_std, k)
                dve.wait_ge(bn_var, k)
                link(V.reciprocal(bA[:, 0:nf], bA[:, 0:nf]))
                link(V.tensor_tensor(bA[:, 0:nf], bA[:, 0:nf], v(gamma), ALU.mult))
                link(V.tensor_tensor(bC[:, 0:nf], bmv[:, 0:nf, 0], bA[:, 0:nf], ALU.mult))
                V.tensor_tensor(bC[:, 0:nf], v(beta), bC[:, 0:nf], ALU.subtract).then_inc(bn_ready, 1)

            def stats_of(st, src, nf):
                last = None
                for n in range(NT):
                    for f in range(nf):
                        wait_emptied(dve, st, n * nf + f)
                        last = V.bn_stats(bst[:, f, n, :], src[:, f, cols(n)])
                link(last)

            def place_edges():
                with dve.Fori(0, PIT) as i:
                    for m in range(ROUNDS):
                        n = i * COLS + m * RING
                        dve.wait_ge(made, n + 1)
                        V.tensor_copy(held[:, m, :, :], fields[:, ds(n, RING), :]).then_inc(held_ready, 1)
                        dve.wait_ge(held_ready, i * ROUNDS + m + 1)
                        for c in range(RING):
                            dve.wait_ge(used, n + c + 1)
                            f = held[:, m, c, :]
                            V.tensor_scalar(lo_ring[:, c, :], iota_lo, f[:, 0:1], None,
                                            ALU.is_equal).then_inc(lo_made, 1)
                            V.tensor_scalar(hi_ring[:, c, :], iota_hi, f[:, 1:2], None, ALU.is_equal)
                            V.tensor_scalar(src_ring[:, c, :], iota_lo, f[:, 0:1], f[:, 2:3], ALU.is_equal, ALU.mult)
                            V.tensor_scalar(val_ring[:, c, 0, :], iota_lo, f[:, 0:1], f[:, 3:4], ALU.is_equal,
                                            ALU.mult).then_inc(made, 1)

            def take_order():
                dve.wait_ge(placed, 1)
                p = [ps[k][:, 0:CHUNKS] for k in range(PARTS)]
                V.tensor_scalar(recs[0][:, :, 0], p[0], float(MID), None, ALU.add)
                V.tensor_copy(recs[0][:, :, 1], p[1])
                link(V.tensor_copy(recs[0][:, :, 2], p[2]))
                link(V.tensor_tensor(recs[0][:, :, 2], recs[0][:, :, 2], p[3], ALU.add))
                V.tensor_tensor(recs[0][:, :, 2], recs[0][:, :, 2], p[4], ALU.add).then_inc(rec0_ready, 1)

            for s in added + joined:
                dve.sem_inc(s, 1)
            dve.sem_inc(made, 1)
            V.memset(epst[:, :], LN_EPS)
            link(V.memset(lnmv[:, :, :], 1.0))
            dve.wait_ge(edges_loaded, 64)
            dve.wait_ge(consts, CONSTS)
            sort(1)
            dve.wait_ge(x_loaded, 32)
            for g in range(NB // GROUP):
                last = ln_stats(g)
            last.then_inc(ln_ready, 1)
            sort(0)
            ln_scale(1, slice(0, NB))
            V.memset(recs[0][:, :, 3], 0.0)
            place_edges()
            take_order()
            dve.wait_ge(vec_loaded, 16 * NVEC)
            V.tensor_scalar(vec[:, eps_col[0]:eps_col[0] + 1], vec[:, eps_col[0]:eps_col[0] + 1], 1.0, None, ALU.add)
            link(V.tensor_scalar(vec[:, eps_col[2]:eps_col[2] + 1], vec[:, eps_col[2]:eps_col[2] + 1], 1.0, None,
                                 ALU.add))
            dve.wait_ge(sc_staged[1], SIT)
            take_transposes(0)
            dve.wait_ge(sums_clear, 1)
            for k in range(SPLIT):
                dve.wait_ge(sc_done[k], 16 * (EC // SPLIT))
            sum_pass(0)
            gin_input(eps_col[0])
            stats_of("up0", H, 4)
            bn_scale(1, 4, "L0_gnn_g1", "L0_gnn_bt1")
            for n in range(NT):
                for f in range(2):
                    k = n * 2 + f
                    src = wait_filled(dve, "down0", k)
                    V.scalar_tensor_tensor(U[:, f, cols(n)], src[:, 0:width(n)], v("L0_gnn_b2", f), TT[:, f, cols(n)],
                                           ALU.add, ALU.add).then_inc(emptied[bank("down0", k)], 1)
            stats_of("down0", U, 2)
            bn_scale(2, 2, "L0_gnn_g2", "L0_gnn_bt2")
            layer_norm(1, "back0")
            take_transposes(1)
            for n in range(NT):
                for f in range(2):
                    last = V.bn_stats(bst[:, f, n, :], TT[:, f, cols(n)])
            link(last)
            bn_scale(3, 2, "L1_gnn_gamma", "L1_gnn_beta")
            dve.wait_ge(sums_clear, 3)
            sum_pass(1)
            sum_pass(2)

            def finish(n):
                w, q = width(n), n % 2
                wait_emptied(dve, "gates1", 4 * n + 3)
                t = AB[q][:, 0:2, 0:w]
                link(V.tensor_tensor(t, TT[:, :, cols(n)], GT[q][:, 2:4, 0:w], ALU.subtract))
                link(V.tensor_tensor(t, t, GT[q][:, 0:2, 0:w], ALU.mult))
                V.tensor_tensor(U[:, 0:2, cols(n)], t, GT[q][:, 2:4, 0:w], ALU.add).then_inc(u_ready, 1)

            def linear_in(n):
                if n >= 2:
                    dve.wait_ge(u_ready, n - 1)
                for q in range(2):
                    for f in range(2):
                        src = wait_filled(dve, "ab1", 4 * n + 2 * q + f)
                        V.scalar_tensor_tensor(AB[n % 2][:, 2 * q + f, 0:width(n)], sums[q][:, 2, cols(n)],
                                               v("L1_gnn_b_out" if q else "L1_gnn_b_in", f), src[:, 0:width(n)],
                                               ALU.mult, ALU.add).then_inc(emptied[bank("ab1", 4 * n + 2 * q + f)], 1)

            def shift(n):
                for q in range(2):
                    for k in range(2):
                        if n == 0:
                            dve.wait_ge(scaled, 2 * q + k + 1)
                        V.scalar_tensor_tensor(sums[q][:, k, cols(n)], sums[q][:, 2, cols(n)], bC[:, k:k + 1],
                                               sums[q][:, k, cols(n)], ALU.mult, ALU.add).then_inc(z_ready, 1)

            shift(0)
            for n in range(NT):
                if n + 1 < NT:
                    shift(n + 1)
                linear_in(n)
                if n >= 1:
                    finish(n - 1)
            finish(NT - 1)
            layer_norm(2, "back1")
            take_transposes(2)
            dve.wait_ge(sums_clear, 4)
            sum_pass(3)
            gin_input(eps_col[2])
            stats_of("up2", H, 2)
            bn_scale(4, 2, "L2_gnn_g1", "L2_gnn_be1")
            stats_of("down2", U, 2)
            bn_scale(5, 2, "L2_gnn_g2", "L2_gnn_be2")
            layer_norm(3, "back2")
            take_transposes(3)
            dve.wait_ge(w_loaded[3], 32)
            V.tensor_tensor(W1e[:, 0:2, :], W1e[:, 0:2, :], W1e[:, 2:4, :], ALU.subtract).then_inc(wdiff, 1)
            V.memset(PT[:, NB - 1, :, :].rearrange("p r f -> p (r f)"), 0.0).then_inc(last_clear, 1)
            dve.wait_ge(parked, 32)
            dve.wait_ge(b1_loaded, 16)
            for t in range(NB):
                r = rows(t)
                p = pf[t % 2][0:r, :]
                src = wait_filled(dve, "p3", t)
                V.tensor_tensor(p, src[0:r, :], b1bc[0:r, :], ALU.add).then_inc(emptied[bank("p3", t)], 1)
                dve.wait_ge(p_hi, 2 * t + 1)
                V.tensor_tensor(p, p, PT[0:r, t, 0, :], ALU.subtract).then_inc(p_sum, 1)
                dve.wait_ge(p_hi, 2 * t + 2)
                V.tensor_tensor(PT[0:r, t, 2, :], p, PT[0:r, t, 1, :], ALU.subtract).then_inc(p_ready, 1)
            for q in range(QS):
                dve.wait_ge(q_stored[q], 16 * (NB // QS))
            V.memset(Hm[:, NB * D:4 * NP], 0.0).then_inc(last_clear, 1)
            dve.wait_ge(last_clear, 2)
            dve.wait_ge(sums_clear, 5)

            def hots(i, j):
                l = i - 4 * ITERS
                make_hot(i, j, None)
                for c in (2 * j, 2 * j + 1):
                    dve.wait_ge(flipped, l * CH_IT + c + 1)
                    V.tensor_scalar(ohb[:, c % OB, :], iota1[:, :], stg_lw[:, c, 0:1], None,
                                    ALU.is_equal).then_inc(hotb, 1)

            def join(i, j):
                dve.wait_ge(landed[j], 32 * i + 32)
                for c in (2 * j, 2 * j + 1):
                    dve.wait_ge(spread[c], i - 4 * ITERS + 2)
                    V.tensor_tensor(hbuf[:, c, :], hbuf[:, c, :], spread_bank(c), ALU.add).then_inc(joined[c], 1)

            def add_hidden(i, j, start):
                add_pair(i, j, H, ps[j % 3][:, :], start, 4)

            hots(4 * ITERS, 0)
            hots(4 * ITERS, 1)
            join(4 * ITERS, 0)

            def body4(i, last):
                first = block_starts(mybir.EngineType.DVE, 0, i - 4 * ITERS, 0, SP_IT)
                for j in range(SP_IT):
                    if (nxt := ahead(i, j, 2, last)) is not None:
                        hots(*nxt)
                    if j >= 1:
                        add_hidden(i, j - 1, first[j - 1])
                    if (nxt := ahead(i, j, 1, last)) is not None:
                        join(*nxt)
                add_hidden(i, SP_IT - 1, first[SP_IT - 1])

            iterations(dve, 4, body4)
            dve.wait_ge(added[SP_IT - 1], 5 * ITERS + 1)
            dve.wait_ge(deg_loaded, 16)
            link(V.tensor_scalar(rdeg, deg, 1e-8, None, ALU.add))
            link(V.reciprocal(rdeg, rdeg))
            for n in range(NT):
                for f in range(2):
                    k = n * 2 + f
                    src = wait_filled(dve, "down3", k)
                    b, c = jobs["down3"][k]
                    V.scalar_tensor_tensor(U[:, f, cols(n)], deg[:, cols(n)], v("L3_gnn_b2", f), src[:, 0:width(n)],
                                           ALU.mult, ALU.add).then_inc(emptied[b], 1)
                    dve.wait_ge(emptied[b], c)
                    V.tensor_tensor(U[:, f, cols(n)], U[:, f, cols(n)], rdeg[:, cols(n)], ALU.mult).then_inc(u_ready, 1)
            dve.wait_ge(unparked, 32)
            for t in range(NB):
                add_back("back3", t)

        @block.tensor
        def _(pe):
            mm = nc.tensor.matmul

            def take_bank(st, k):
                b, c = jobs[st][k]
                if c > 1:
                    pe.wait_ge(emptied[b], c - 1)
                return ps[b]

            def done(ins, st, k):
                ins.then_inc(filled[bank(st, k)], 1)

            def counts(o, turn):
                pe.wait_ge(totals_ready, turn)
                dst = take_bank(f"count{o}", 0)
                tot = srt[0:EP, 1, :]
                mm(dst[0:EP, 0:NB], tri, tot, start=True, stop=True)
                done(mm(dst[:, 32:32 + NB], ones[0:EP, :], tot, start=True, stop=True), f"count{o}", 0)

            def transposes(layer):
                st = f"T{layer}"
                for g, (g0_, m) in enumerate(TG):
                    pe.wait_ge(normed, layer * NB + 4 * g + m)
                    for k in range(2):
                        dst = take_bank(st, 2 * g + k)
                        for t in range(4 * g, 4 * g + m):
                            r = rows(t)
                            o = (t - 4 * g) * P
                            last = nc.tensor.transpose(dst[:, o:o + r], Tm[0:r, t, k * P:(k + 1) * P],
                                                       ident[0:r, 0:r])
                        done(last, st, 2 * g + k)

            def back(st, ready, count):
                for t in range(NB):
                    r = rows(t)
                    pe.wait_ge(ready, count(min(NT - 1, (t * P + r - 1) // W)))
                    dst = take_bank(st, t)
                    for k in range(2):
                        last = nc.tensor.transpose(dst[0:r, k * P:(k + 1) * P], U[:, k, t * P:t * P + r],
                                                   ident[:, :])
                    done(last, st, t)

            def drained():
                for b in range(8):
                    if fills_at[0][b]:
                        pe.wait_ge(emptied[b], fills_at[0][b])

            fills_at = [[0] * 8]

            def before(stage):
                b0 = [0] * 8
                for name in ORDER[:ORDER.index(stage)]:
                    for b, c in jobs[name]:
                        b0[b] = max(b0[b], c)
                fills_at[0] = b0
                drained()

            def sum_pass(n):
                with pe.Fori(n * ITERS, (n + 1) * ITERS) as i:
                    for j in range(SP_IT):
                        pe.wait_ge(hot[j], i + 1)
                        pe.wait_ge(landed[j], 32 * i + 32)
                        pe.wait_ge(added[j], i + 1)
                        for k in range(3):
                            for c in (2 * j, 2 * j + 1):
                                lhs = rowsbuf[:, c, k * P:(k + 1) * P] if k < 2 else ones[:, :]
                                last = mm(ps[j][:, k * P:(k + 1) * P], lhs, oh[:, c, :], start=(c == 2 * j),
                                          stop=(c == 2 * j + 1))
                        last.then_inc(summed[j], 1)
                for j in range(SP_IT):
                    pe.wait_ge(added[j], (n + 1) * ITERS + 1)

            def products(st, n, nf, terms, k0=0):
                for f in range(nf):
                    dst = take_bank(st, k0 + f)
                    for m, (w, src) in enumerate(terms):
                        last = mm(dst[:, 0:width(n)], w[:, f * P:(f + 1) * P], src, start=(m == 0),
                                  stop=(m == len(terms) - 1))
                    done(last, st, k0 + f)

            def up(st, w, nf, z0):
                for n in range(NT):
                    pe.wait_ge(z_ready, z0 + 2 * (n + 1))
                    products(st, n, nf, [(w[:, k, :], sums[0][:, k, cols(n)]) for k in range(2)], n * nf)

            def down(st, w, nk, a0):
                for n in range(NT):
                    if a0 is not None:
                        pe.wait_ge(act_ready, a0 + nk * (n + 1))
                    products(st, n, 2, [(w[:, k, :], H[:, k, cols(n)]) for k in range(nk)], n * 2)

            for s in summed + spread:
                pe.sem_inc(s, 1)
            pe.sem_inc(used, RING)
            pe.sem_inc(flipped, OB)
            pe.wait_ge(consts, CONSTS)
            counts(1, 1)
            counts(0, 2)
            pe.wait_ge(order_ready, 2)
            for k in range(PARTS):
                mm(ps[k][:, 0:CHUNKS], zero16[:, 0:P], zero16, start=True, stop=False)
            with pe.Fori(0, PIT) as i:
                for k0 in range(COLS):
                    c = k0 % RING
                    pe.wait_ge(made, i * COLS + k0 + 2)
                    pe.wait_ge(weighed, i * COLS + k0 + 1)
                    for k in range(PARTS):
                        lhs = src_ring[:, c, :] if k == 0 else val_ring[:, c, k - 1, :]
                        last = mm(ps[k][:, 0:CHUNKS], lhs, hi_ring[:, c, :], start=False, stop=False)
                    last.then_inc(used, 1)
            for k in range(PARTS):
                last = mm(ps[k][:, 0:CHUNKS], zero16[:, 0:P], zero16, start=False, stop=True)
            last.then_inc(placed, 1)
            transposes(0)
            before("up0")
            sum_pass(0)
            pe.wait_ge(w_loaded[0], 32)
            up("up0", W1a, 4, 0)
            down("down0", W2a, 4, 0)
            back("back0", act_ready, lambda n: 4 * NT + 2 * (n + 1))
            transposes(1)
            before("ab1")
            sum_pass(1)
            sum_pass(2)
            pe.wait_ge(w_loaded[1], 64)
            pe.wait_ge(act_ready, 8 * NT)

            def linear_in(n):
                pe.wait_ge(z_ready, 2 * NT + 4 * (n + 1))
                if n >= 2:
                    pass
                for q, w in ((0, Win), (1, Wout)):
                    products("ab1", n, 2, [(w[:, k, :], sums[q][:, k, cols(n)]) for k in range(2)], 4 * n + 2 * q)

            linear_in(0)
            for n in range(NT):
                if n + 1 < NT:
                    linear_in(n + 1)
                for f in range(4):
                    b, c = jobs["ab1"][4 * n + f]
                    pe.wait_ge(emptied[b], c)
                products("gates1", n, 4, [(Wx2i[:, k, :], AB[n % 2][:, k, 0:width(n)]) for k in range(4)]
                         + [(Wh2h[:, k, :], TT[:, k, cols(n)]) for k in range(2)], 4 * n)
            back("back1", u_ready, lambda n: n + 1)
            transposes(2)
            before("up2")
            sum_pass(3)
            pe.wait_ge(w_loaded[2], 32)
            up("up2", W1c, 2, 6 * NT)
            down("down2", W2c, 2, 8 * NT)
            back("back2", act_ready, lambda n: 10 * NT + 2 * (n + 1))
            transposes(3)
            for k in (-1, -2):
                wait_emptied(pe, "T3", k)
            pe.wait_ge(w_loaded[3], 32)
            for st, w in (("q3", 2), ("p3", 0)):
                if st == "p3":
                    pe.wait_ge(wdiff, 1)
                for t in range(NB):
                    r = rows(t)
                    dst = take_bank(st, t)
                    for k in range(2):
                        last = mm(dst[0:r, :], TT[:, k, t * P:t * P + r], W1e[:, w + k, :], start=(k == 0),
                                  stop=(k == 1))
                    done(last, st, t)
            before("down3")
            pe.wait_ge(p_ready, NB)

            def flip(i, j):
                l = i - 4 * ITERS
                for c in (2 * j, 2 * j + 1):
                    pe.wait_ge(hotb, l * CH_IT + c + 1)
                    pe.wait_ge(flip_copied[(c - 2) % CH_IT], l + 2 if c >= 2 else l + 1)
                    nc.tensor.transpose(flip_bank(c), ohb[:, c % OB, :], identb[:, :]).then_inc(flipped, 1)

            def spread_pair(i, j, start):
                l = i - 4 * ITERS
                for c in (2 * j, 2 * j + 1):
                    pe.wait_ge(flip_copied[c], l + 2)
                    pe.wait_ge(joined[(c - 2) % CH_IT], l + 2 if c >= 2 else l + 1)
                    for part3 in range(3):
                        last = mm(spread_bank(c), ohT[:, c % OB, :],
                                  PTf[:, ds(start * (3 * HID // P) + part3 * HID, HID)], start=(part3 == 0),
                                  stop=(part3 == 2))
                    last.then_inc(spread[c], 1)

            def sum_hidden(i, j):
                l = i - 4 * ITERS
                before_j = (j - 3) if j >= 3 else (j + 3 if j + 3 < SP_IT else j)
                pe.wait_ge(added[before_j], i + 2 if j >= 3 else i + 1)
                pe.wait_ge(relued, l * CH_IT + 2 * j + 2)
                pe.wait_ge(hot[j], i + 1)
                for k in range(4):
                    for c in (2 * j, 2 * j + 1):
                        last = mm(ps[j % 3][:, k * P:(k + 1) * P], hbuf[:, c, k * P:(k + 1) * P], oh[:, c, :],
                                  start=(c == 2 * j), stop=(c == 2 * j + 1))
                last.then_inc(summed[j], 1)

            PEE = mybir.EngineType.PE
            flip(4 * ITERS, 0)
            flip(4 * ITERS, 1)
            spread_pair(4 * ITERS, 0, block_starts(PEE, 0, 0, 0, 1)[0])

            def body4(i, last):
                l = i - 4 * ITERS
                first = block_starts(PEE, 0, l, 1, SP_IT - 1)
                if not last:
                    first = (*first, *block_starts(PEE, 0, l + 1, 0, 1))
                for j in range(SP_IT):
                    if (nxt := ahead(i, j, 1, last)) is not None:
                        spread_pair(*nxt, first[j])
                    if (nxt := ahead(i, j, 2, last)) is not None:
                        flip(*nxt)
                    sum_hidden(i, j)

            iterations(pe, 4, body4)
            for j in range(SP_IT):
                pe.wait_ge(added[j], 5 * ITERS + 1)
            down("down3", W2e, 4, None)
            back("back3", u_ready, lambda n: NT + 2 * (n + 1))


_IN2D = {"L0_gnn_eps_gin": (1, 1), "L2_gnn_eps": (1, 1)}
_NAMES = ["x", "src", "dst", "edge_weight", "edge_weight_n2", "L0_gnn_W1", "L0_gnn_b1", "L0_gnn_g1", "L0_gnn_bt1",
          "L0_gnn_W2", "L0_gnn_b2", "L0_gnn_g2", "L0_gnn_bt2", "L0_gnn_eps_gin", "L1_gnn_gamma", "L1_gnn_beta",
          "L1_gnn_W_in", "L1_gnn_b_in", "L1_gnn_W_out", "L1_gnn_b_out", "L1_gnn_W_x2i", "L1_gnn_b_x2i",
          "L1_gnn_W_h2h", "L2_gnn_eps", "L2_gnn_W1", "L2_gnn_b1", "L2_gnn_g1", "L2_gnn_be1", "L2_gnn_W2", "L2_gnn_b2",
          "L2_gnn_g2", "L2_gnn_be2", "L3_gnn_W1", "L3_gnn_b1", "L3_gnn_W2", "L3_gnn_b2"]


def kernel(**inputs):
    import numpy as np
    import concourse.bacc as bacc
    from concourse import mybir as mb
    from concourse.bass_utils import run_bass_kernel_spmd

    nc = bacc.Bacc("TRN2", target_bir_lowering=False, num_devices=1)
    arrays, aps = {}, {}
    for name in _NAMES:
        arr = np.ascontiguousarray(inputs[name])
        if name in _IN2D:
            arr = arr.reshape(_IN2D[name])
        arrays[f"in_{name}"] = arr
        aps[name] = nc.dram_tensor(f"in_{name}", arr.shape, mb.dt.from_np(arr.dtype), kind="ExternalInput").ap()
    out = nc.dram_tensor("out_x", (N, D), mb.dt.float32, kind="ExternalOutput").ap()
    gnn_kernel(nc, aps, out)
    r = run_bass_kernel_spmd(nc, [arrays], core_ids=[0])
    return r.results[0]["out_x"]
```

```python
import concourse.bass as bass
from concourse import mybir
from contextlib import ExitStack

P = 128
N = 3125
D = 256
E = 50000
EP = 125
EC = E // EP
NB = -(-N // P)
LAST = N - (NB - 1) * P
NP = NB * P
SP_IT = 5
CH_IT = 2 * SP_IT
ITERS = -(-(E + NB * (P - 1)) // (P * CH_IT))
CHUNKS = ITERS * CH_IT
SB = 5
assert CH_IT % SB == 0 and EP * EC == E
LEAD = 2
HID = 512
W = 448
NT = -(-N // W)
LN_EPS = 1e-5
SC = 10
SIT = EC // (2 * SC)
NORM_AT = 4
SPLIT = 5
RING = 5
PIT = SIT - NORM_AT
ROUNDS = EC // (PIT * RING)
COLS = ROUNDS * RING
FIELDS = 7
PARTS = FIELDS - 2
assert PIT * COLS == EC
MID = N // 2
Q_FIRST = 16
PFS = 3
GROUP = 5
UNIT = 80
UNITS = NP // UNIT
FOLD_AT = 8
TU = 6
GTILES = -(-UNITS // TU)
assert UNITS * UNIT == NP and UNITS < ITERS and 4 * UNIT <= 512 and TU * UNIT <= 512


def rows(t):
    return LAST if t == NB - 1 else P


def width(n):
    return min(W, N - n * W)


def cols(n):
    return slice(n * W, n * W + width(n))


def ended_by(n):
    return [t for t in range(NB) if (t * P + rows(t) - 1) // W == n]


def groups_by(n):
    return [g for g in range(NB // GROUP) if ((g + 1) * GROUP * P - 1) // (TU * UNIT) == n]


def units(n):
    return slice(n * TU, min((n + 1) * TU, UNITS))


def unit_cols(n):
    return slice(n * TU * UNIT, min((n + 1) * TU * UNIT, NP))


def gnn_kernel(nc, a, out):
    f32, bf16, f16, i32 = mybir.dt.float32, mybir.dt.bfloat16, mybir.dt.float16, mybir.dt.int32
    ALU, ACT, AX = mybir.AluOpType, mybir.ActivationFunctionType, mybir.AxisListType
    ds = bass.ds

    table = nc.dram_tensor("table", [N, D], f32).ap()
    qtable = nc.dram_tensor("qtable", [N, HID], f32).ap()
    xpark = nc.dram_tensor("xpark", [N, D], f32).ap()
    degrow = nc.dram_tensor("degrow", [1, N], f32).ap()
    rdegrow = nc.dram_tensor("rdegrow", [1, N], f32).ap()
    recs_dram = [nc.dram_tensor(f"recs_{k}", [P * CHUNKS, 4], f32).ap() for k in range(SPLIT)]

    ctx = ExitStack()
    with ctx:
        def sb(name, shape, dt):
            return ctx.enter_context(nc.sbuf_tensor(name, shape, dt))

        def sem(name):
            return ctx.enter_context(nc.semaphore(name))

        def sems(name, n):
            return [sem(f"{name}{k}") for k in range(n)]

        x = sb("x", [P, NB * D], f32)
        xt = x[:, :].rearrange("p (t f) -> p t f", t=NB)
        TTm = sb("TT", [P, N + NP], f32)
        TT = TTm[:, 0:2 * N].rearrange("p (k n) -> p k n", k=2)
        acc = sb("acc", [P, 2 * 3 * NP], f32)
        sums = [acc[:, o * 3 * NP:(o + 1) * 3 * NP].rearrange("p (k n) -> p k n", k=3) for o in range(2)]
        Hm = sb("H", [P, 4 * NP + 260], f32)
        H = Hm[:, 0:4 * NP].rearrange("p (k n) -> p k n", k=4)
        Tm = Hm[:, 0:NB * D].rearrange("p (t f) -> p t f", t=NB)
        g0 = NB * D
        rowsbuf = Hm[:, g0:g0 + CH_IT * D].rearrange("p (c f) -> p c f", c=CH_IT)
        w0 = g0 + CH_IT * D
        Win = Hm[:, w0:w0 + 512].rearrange("p (k n) -> p k n", k=2)
        Wout = Hm[:, w0 + 512:w0 + 1024].rearrange("p (k n) -> p k n", k=2)
        Wx2i = Hm[:, w0 + 1024:w0 + 3072].rearrange("p (k n) -> p k n", k=4)
        Wh2h = Hm[:, w0 + 3072:w0 + 4096].rearrange("p (k n) -> p k n", k=2)
        W1e = Hm[:, w0:w0 + 2048].rearrange("p (k n) -> p k n", k=4)
        recs = [sb(f"rec{o}", [P, CHUNKS, 4], f32) for o in range(2)]
        Wm = sb("Wm", [P, 2048], f32)
        W1a = Wm[:, 0:1024].rearrange("p (k n) -> p k n", k=2)
        W2a = Wm[:, 1024:2048].rearrange("p (k n) -> p k n", k=4)
        W1c = Wm[:, 0:512].rearrange("p (k n) -> p k n", k=2)
        W2c = Wm[:, 512:1024].rearrange("p (k n) -> p k n", k=2)
        W2e = Wm[:, 1024:2048].rearrange("p (k n) -> p k n", k=4)
        b1bc = Wm[:, 0:HID]
        oh = sb("oh", [P, CH_IT, P], f32)
        iota1 = sb("iota1", [P, P], f32)
        ident = sb("ident", [P, P], f32)
        identb = sb("identb", [P, P], bf16)
        ones = sb("ones", [P, P], f32)
        stg_idx = sb("stg_idx", [P, CH_IT], i32)
        stg_lw = sb("stg_lw", [P, CH_IT, 3], f32)
        blk_tabs = sb("blk_tabs", [64, CHUNKS], i32)
        blk_tab = [blk_tabs[32 * o:32 * o + 1, :] for o in range(2)]
        rdeg_sq = sb("rdeg_sq", [EP, N // EP], f32)
        vec = sb("vec", [P, 48], f32)
        lnst = sb("lnst", [P, 2 * GROUP, 6], f32)
        lnmv = sb("lnmv", [P, NB, 2], f32)
        lnr = sb("lnr", [P, NB], f32)
        lnb = sb("lnb", [P, NB], f32)
        bst = sb("bst", [P, 4, NT, 6], f32)
        bmv = sb("bmv", [P, 4, 2], f32)
        bA = sb("bA", [P, 4], f32)
        bC = sb("bC", [P, 4], f32)
        epst = sb("epst", [P, 1], f32)
        ccol = sb("ccol", [P, 4], f32)

        mask = acc[0:EP, 0:NB * EC // 2].bitcast(bf16).rearrange("p (b c) -> p b c", b=NB)
        run0 = NB * EC // 2
        run = acc[0:EP, run0:run0 + NB * EC].rearrange("p (b c) -> p b c", b=NB)
        key_i = [Hm[0:EP, 0:EC].bitcast(i32), Hm[0:EP, EC:2 * EC].bitcast(i32)]
        wts = [Hm[0:EP, 2 * EC:3 * EC], Hm[0:EP, 3 * EC:4 * EC]]
        ti = Hm[0:EP, 4 * EC:5 * EC].bitcast(i32)
        ti2 = Hm[0:EP, 5 * EC:6 * EC].bitcast(i32)
        blkf = Hm[0:EP, 6 * EC:6 * EC + EC // 2].bitcast(f16)
        pos = Hm[0:EP, 7 * EC:8 * EC]
        slot = TTm[0:EP, 0:EC]
        erec = TTm[0:EP, EC:5 * EC].rearrange("p (c r) -> p c r", r=4)
        fields = TTm[0:EP, 5 * EC:(5 + FIELDS) * EC].rearrange("p (c r) -> p c r", r=FIELDS)
        part16 = TTm[0:EP, (5 + FIELDS) * EC:(5 + FIELDS) * EC + EC // 2].bitcast(bf16)
        r0 = g0 + CH_IT * D
        hi_ring = Hm[0:EP, r0:r0 + RING * CHUNKS // 2].bitcast(bf16).rearrange("p (s c) -> p s c", s=RING)
        r1 = r0 + RING * CHUNKS // 2
        src_ring = Hm[0:EP, r1:r1 + RING * P // 2].bitcast(f16).rearrange("p (s n) -> p s n", s=RING)
        r2 = r1 + RING * P // 2
        val_ring = Hm[0:EP, r2:r2 + RING * 4 * P // 2].bitcast(bf16).rearrange("p (s v n) -> p s v n", s=RING, v=4)
        r3 = r2 + RING * 4 * P // 2
        zero16 = Hm[0:EP, r3:r3 + CHUNKS // 2].bitcast(bf16)
        r4 = r3 + CHUNKS // 2
        iota_hi = Hm[0:EP, r4:r4 + CHUNKS // 2].bitcast(f16)
        r5 = r4 + CHUNKS // 2
        iota_lo = Hm[0:EP, r5:r5 + P // 2].bitcast(f16)
        r6 = r5 + P // 2
        held = Hm[0:EP, r6:r6 + COLS * FIELDS].rearrange("p (h c r) -> p h c r", h=ROUNDS, r=FIELDS)
        r7 = r6 + COLS * FIELDS
        lo_ring = Hm[0:EP, r7:r7 + RING * P // 2].bitcast(bf16).rearrange("p (s n) -> p s n", s=RING)
        assert r7 + RING * P // 2 <= 4 * NP + 260
        zeros = Hm[:, 8 * EC:8 * EC + 4 * CHUNKS]
        tri = Hm[0:EP, 8 * EC + 4 * CHUNKS:8 * EC + 4 * CHUNKS + EP]
        ends0 = 8 * EC + 4 * CHUNKS + 2 * P
        cstart = Hm[:, ends0:ends0 + CHUNKS]
        lt0 = ends0 + CHUNKS
        ends_ge = Hm[0:NB - 1, lt0:lt0 + CHUNKS]
        srt0 = lt0 + CHUNKS
        srt = Hm[:, srt0:srt0 + 5 * NB].rearrange("p (k b) -> p k b", b=NB)
        srti = Hm[:, srt0 + 5 * NB:srt0 + 6 * NB].bitcast(i32)
        ends_col = Hm[0:NB - 1, srt0 + 6 * NB:srt0 + 6 * NB + 1]
        sst_idx = oh[0:EP, 0:1, 0:2 * SC].bitcast(i32).rearrange("p a c -> p (a c)")
        sst_rec = oh[0:EP, 1:3, :].rearrange("p a c -> p (a c)")[:, 0:2 * SC * 4].rearrange(
            "p (c r) -> p c r", r=4)

        part = [acc[:, 3 * NP + k * 4 * CHUNKS:3 * NP + (k + 1) * 4 * CHUNKS].rearrange("p (c r) -> p c r", r=4)
                for k in range(SPLIT - 1)]

        gate01 = Hm[:, 0:2 * NP].rearrange("p (u f n) -> p u f n", f=2, n=UNIT)
        gate23 = sums[0][:, 0:2, :].rearrange("p f (u n) -> p u f n", n=UNIT)
        TTu = [TTm[:, k * N:k * N + NP] for k in range(2)]
        WT = [Hm[:, q * 512:(q + 1) * 512].rearrange("p (m n) -> p m n", m=2) for q in range(2)]
        fold = [Wm[:, q * 1024:(q + 1) * 1024].rearrange("p (k n) -> p k n", k=2) for q in range(2)]
        fold_row = [w[0:1, :, :].rearrange("p k n -> p (k n)") for w in (Win, Wout)]
        U = sums[0]
        PT = acc[:, 0:NB * 3 * HID // 2].bitcast(bf16).rearrange("p (b r f) -> p b r f", b=NB, r=3)
        PTf = acc[:, 0:NB * 3 * HID // 2].bitcast(bf16)
        hbuf = x[:, 0:CH_IT * HID].rearrange("p (c f) -> p c f", c=CH_IT)
        pf = [recs[1][:, :, :].rearrange("p c r -> p (c r)")[:, q * HID:(q + 1) * HID] for q in range(PFS)]
        qst = rowsbuf.rearrange("p c f -> p (c f)").rearrange("p (q f) -> p q f", f=HID)
        QS = 5
        ohb = oh[:, :, :].rearrange("p c n -> p (c n)").bitcast(bf16).rearrange("p (c n h) -> p c n h", n=P, h=2)
        ohT = recs[1][:, :, :].rearrange("p c r -> p (c r)")[:, 0:CH_IT * P // 2].bitcast(bf16).rearrange(
            "p (c n) -> p c n", n=P)
        deg = TT[:, 0, :]
        rdeg = TT[:, 1, :]

        VCOL, at = {}, 0
        for name, n in (("L0_gnn_b1", 4), ("L0_gnn_g1", 4), ("L0_gnn_bt1", 4), ("L0_gnn_b2", 2),
                        ("L0_gnn_g2", 2), ("L0_gnn_bt2", 2), ("L1_gnn_gamma", 2), ("L1_gnn_beta", 2),
                        ("L1_gnn_b_in", 2), ("L1_gnn_b_out", 2), ("L1_gnn_b_x2i", 4),
                        ("L2_gnn_b1", 2), ("L2_gnn_g1", 2), ("L2_gnn_be1", 2), ("L2_gnn_b2", 2),
                        ("L2_gnn_g2", 2), ("L2_gnn_be2", 2), ("L3_gnn_b2", 2)):
            VCOL[name] = (at, n)
            at += n
        eps_col = {0: at, 2: at + 1}
        NVEC = len(VCOL) + 2

        def v(name, k=None):
            o, n = VCOL[name]
            return vec[:, o:o + n] if k is None else vec[:, o + k:o + k + 1]

        ps = [ctx.enter_context(nc.psum_tensor(f"ps{b}", [P, 512], f32)) for b in range(8)]

        flip_bank = ps[SB + 2][:, 0:P].bitcast(bf16).rearrange("p (c n) -> p c n", n=P)

        def spread_bank(c):
            return ps[SB + c % 2][:, :]

        def sum_bank(c):
            return ps[c % SB][:, :]

        CONSTS = 12

        edges_loaded = sem("edges_loaded")
        x_loaded = sem("x_loaded")
        vec_loaded = sem("vec_loaded")
        w_loaded = sems("w_loaded", 4)
        b1_loaded = sem("b1_loaded")
        consts = sem("consts")
        stages_begun = sem("stages_begun")
        zero_filled = sem("zero_filled")
        held_ready = sem("held_ready")
        lo_made = sem("lo_made")
        made = sem("made")
        weighed = sem("weighed")
        used = sem("used")
        placed = sem("placed")
        rec0_ready = sem("rec0_ready")
        vstep = sem("vstep")
        totals_ready = sem("totals_ready")
        ends_ready = sem("ends_ready")
        order_ready = sem("order_ready")
        sc_staged = sems("sc_staged", 2)
        sc_done = sems("sc_done", SPLIT)
        merged = sem("merged")
        rec_loaded = sem("rec_loaded")
        filled = sems("filled", 8)
        emptied = sems("emptied", 8)
        ln_var = sem("ln_var")
        ln_ready = sem("ln_ready")
        std_ready = sem("std_ready")
        normed = sem("normed")
        tab_written = sem("tab_written")
        bn_var = sem("bn_var")
        bn_std = sem("bn_std")
        bn_ready = sem("bn_ready")
        act_ready = sem("act_ready")
        staged = sem("staged")
        landed = sems("landed", SP_IT)
        hot = sem("hot")
        summed = sem("summed")
        added = sem("added")
        sums_clear = sem("sums_clear")
        last_clear = sem("last_clear")
        z_ready = sem("z_ready")
        gates_begun = sem("gates_begun")
        gates_kept = sem("gates_kept")
        gates_ready = sem("gates_ready")
        u_ready = sem("u_ready")
        deg_stored = sem("deg_stored")
        rdeg_ready = sem("rdeg_ready")
        deg_loaded = sem("deg_loaded")
        parked = sem("parked")
        unparked = sem("unparked")
        q_stored = sems("q_stored", QS)
        wdiff = sem("wdiff")
        p_sum = sem("p_sum")
        p_hi = sem("p_hi")
        p_ready = sem("p_ready")
        flipped = sem("flipped")
        flip_copied = sem("flip_copied")
        spread = sem("spread")
        joined = sem("joined")
        relued = sem("relued")
        out_stored = sem("out_stored")

        fills = [0] * 8
        jobs = {}

        def plan(stage, count, banks=range(8)):
            banks = list(banks)
            jobs[stage] = []
            for k in range(count):
                b = banks[k % len(banks)]
                fills[b] += 1
                jobs[stage].append((b, fills[b]))

        TG = [(g, min(4, NB - 4 * g)) for g in range(-(-NB // 4))]
        for o in range(2):
            plan(f"count{o}", 1, [6 + o])
        for o in (1, 0):
            plan(f"table{o}", 2, [PARTS])
        plan("T0", 2 * len(TG), range(PARTS, 8))
        plan("up0", 4 * NT)
        plan("down0", 2 * NT)
        plan("back0", NB)
        plan("T1", 2 * len(TG))
        plan("turn1", 3, (5, 6, 7))
        plan("fold1", 6, (5, 6, 7))
        plan("gates1", 4 * GTILES, range(4))
        plan("back1", NB, range(4, 8))
        plan("T2", 2 * len(TG))
        plan("up2", 2 * NT)
        plan("down2", 2 * NT)
        plan("back2", NB)
        plan("T3", 2 * len(TG), (6, 7))
        plan("q3", NB, (0, 1, 2))
        plan("p3", NB, (3, 4, 5))
        plan("down3", 2 * NT, range(4))
        plan("back3", NB, range(4, 8))

        def blocks_of(g):
            return range(4 * g, min(4 * g + 4, NB)) if g >= 0 else ()

        def wait_filled(eng, stage, k):
            b, c = jobs[stage][k]
            eng.wait_ge(filled[b], c)
            return ps[b]

        def wait_emptied(eng, stage, k):
            b, c = jobs[stage][k]
            eng.wait_ge(emptied[b], c)

        def bank(stage, k):
            return jobs[stage][k][0]

        def block_starts(eng, o, row, first, count):
            at = row * CH_IT + first
            return nc.values_load_multi_w_load_instructions(
                blk_tab[o][:, ds(at, count)], engines=[eng], min_val=0, max_val=(NB - 1) * P,
                skip_runtime_bounds_check_because="a count of blocks times their nodes")[1]

        def iterations(eng, n, body, first=0):
            with eng.Fori(n * ITERS + first, (n + 1) * ITERS - 1) as i:
                body(i, False)
            body((n + 1) * ITERS - 1, True)

        def ahead(i, j, d, last):
            if j + d < SP_IT:
                return i, j + d
            return None if last else (i + 1, j + d - SP_IT)

        PASSES = [(0, None, 0), (0, 1, 0), (1, 2, 1), (1, 1, 0), (0, None, 0)]
        ORDER = ["count1", "table1", "count0", "table0", "T0", "up0", "down0", "back0", "T1", "turn1", "fold1",
                 "gates1", "back1", "T2", "up2", "down2", "back2", "T3", "q3", "p3", "down3", "back3"]

        block = ctx.enter_context(nc.Block())

        @block.sync
        def _(sp):
            def edge_view(name):
                return a[name].rearrange("(p c) -> p c", p=EP)

            sp.dma_start(key_i[0], edge_view("dst")).then_inc(edges_loaded, 16)
            sp.dma_start(key_i[1], edge_view("src")).then_inc(edges_loaded, 16)
            sp.dma_start(wts[0], edge_view("edge_weight")).then_inc(edges_loaded, 16)
            sp.dma_start(wts[1], edge_view("edge_weight_n2")).then_inc(edges_loaded, 16)
            nfull = NB - 1

            def tiles(dram):
                return (dram[0:nfull * P, :].rearrange("(t p) f -> p t f", p=P), dram[nfull * P:N, :])

            main, tail = tiles(a["x"])
            sp.dma_start(xt[:, 0:nfull, :], main).then_inc(x_loaded, 16)
            sp.dma_start(xt[0:LAST, nfull, :], tail).then_inc(x_loaded, 16)
            with nc.allow_non_contiguous_dma(reason="per-feature vectors"):
                for name, (o, n) in VCOL.items():
                    sp.dma_start(vec[:, o:o + n], a[name].rearrange("(k p) -> p k", p=P)).then_inc(vec_loaded, 16)
            sp.dma_start(vec[:, eps_col[0]:eps_col[0] + 1],
                         a["L0_gnn_eps_gin"].to_broadcast([P, 1])).then_inc(vec_loaded, 16)
            sp.dma_start(vec[:, eps_col[2]:eps_col[2] + 1],
                         a["L2_gnn_eps"].to_broadcast([P, 1])).then_inc(vec_loaded, 16)

            def weight(dst, name, s):
                sp.dma_start(dst, a[name].rearrange("(k p) n -> p k n", p=P)).then_inc(s, 16)

            weight(W1a, "L0_gnn_W1", w_loaded[0])
            weight(W2a, "L0_gnn_W2", w_loaded[0])
            sp.wait_ge(consts, 1)
            for k in range(SPLIT):
                sp.dma_start(recs_dram[k].rearrange("(p c) r -> p (c r)", p=P), zeros).then_inc(zero_filled, 16)
            def store_table(layer):
                for gidx in range(NB // GROUP):
                    sp.wait_ge(normed, layer * NB + (gidx + 1) * GROUP)
                    t0, t1 = gidx * GROUP, (gidx + 1) * GROUP
                    full = min(t1, nfull)
                    sp.dma_start(table[t0 * P:full * P, :].rearrange("(t p) f -> p t f", p=P),
                                 Tm[:, t0:full, :]).then_inc(tab_written, 16)
                sp.dma_start(table[nfull * P:N, :], Tm[0:LAST, nfull, :]).then_inc(tab_written, 16)

            store_table(0)
            for k in range(SPLIT):
                sp.wait_ge(sc_done[k], 16 * (EC // SPLIT))
                sp.dma_start(recs[1][:, :, :] if k == 0 else part[k - 1],
                             recs_dram[k].rearrange("(p c) r -> p c r", p=P)).then_inc(rec_loaded, 16)
            sp.wait_ge(added, CHUNKS + SB)
            sp.dma_start(degrow, sums[0][0:1, 2, 0:N]).then_inc(deg_stored, 16)
            sp.wait_ge(deg_stored, 16)
            sp.dma_start(rdeg_sq[:, :], degrow.rearrange("o (p c) -> (o p) c", p=EP)).then_inc(deg_loaded, 16)
            b, c = jobs["down0"][-1]
            sp.wait_ge(filled[b], c)
            weight(Win, "L1_gnn_W_in", w_loaded[1])
            weight(Wout, "L1_gnn_W_out", w_loaded[1])
            weight(Wx2i, "L1_gnn_W_x2i", w_loaded[1])
            weight(Wh2h, "L1_gnn_W_h2h", w_loaded[1])
            sp.wait_ge(rdeg_ready, 2)
            sp.dma_start(rdegrow.rearrange("o (p c) -> (o p) c", p=EP), rdeg_sq[:, :]).then_inc(deg_stored, 16)
            store_table(1)
            for k in range(1, 5):
                b, c = jobs["gates1"][-k]
                sp.wait_ge(filled[b], c)
            weight(W1c, "L2_gnn_W1", w_loaded[2])
            weight(W2c, "L2_gnn_W2", w_loaded[2])
            weight(W2e, "L3_gnn_W2", w_loaded[3])
            store_table(2)
            weight(W1e, "L3_gnn_W1", w_loaded[3])
            b, c = jobs["down2"][-1]
            sp.wait_ge(filled[b], c)
            sp.dma_start(b1bc, a["L3_gnn_b1"].rearrange("(o n) -> o n", o=1).to_broadcast([P, HID])).then_inc(
                b1_loaded, 16)
            sp.wait_ge(normed, 4 * NB)
            main, tail = tiles(xpark)
            sp.dma_start(main, xt[:, 0:nfull, :]).then_inc(parked, 16)
            sp.dma_start(tail, xt[0:LAST, nfull, :]).then_inc(parked, 16)
            for t in range(NB):
                wait_emptied(sp, "q3", t)
                sp.dma_start(qtable[t * P:t * P + rows(t), :], qst[0:rows(t), t % QS, :]).then_inc(q_stored[t % QS], 16)
            b, c = jobs["p3"][-1]
            sp.wait_ge(filled[b], c)
            sp.wait_ge(deg_stored, 32)
            sp.dma_start(deg, degrow.to_broadcast([P, N])).then_inc(deg_loaded, 16)
            sp.dma_start(rdeg, rdegrow.to_broadcast([P, N])).then_inc(deg_loaded, 16)
            sp.wait_ge(parked, 32)
            sp.wait_ge(summed, 5 * CHUNKS + CH_IT)
            sp.dma_start(xt[:, 0:nfull, :], main).then_inc(unparked, 16)
            sp.dma_start(xt[0:LAST, nfull, :], tail).then_inc(unparked, 16)
            for gidx in range(NB // GROUP):
                for t in range(gidx * GROUP, (gidx + 1) * GROUP):
                    wait_emptied(sp, "back3", t)
                t0, t1 = gidx * GROUP, (gidx + 1) * GROUP
                full = min(t1, nfull)
                sp.dma_start(out[t0 * P:full * P, :].rearrange("(t p) f -> p t f", p=P),
                             xt[:, t0:full, :]).then_inc(out_stored, 16)
            sp.dma_start(out[nfull * P:N, :], xt[0:LAST, nfull, :]).then_inc(out_stored, 16)
            sp.wait_ge(out_stored, 16 * (NB // GROUP + 1))

        @block.gpsimd
        def _(pool):
            nc.gpsimd.memset(zeros, 0.0).then_inc(consts, 1)
            nc.gpsimd.iota(iota1[:, :], [[1, P]], base=1, channel_multiplier=0,
                           allow_small_or_imprecise_dtypes=True).then_inc(consts, 1)
            nc.gpsimd.iota(cstart, [[P, CHUNKS]], base=0, channel_multiplier=0,
                           allow_small_or_imprecise_dtypes=True).then_inc(consts, 1)
            nc.gpsimd.memset(ones[:, :], 1.0).then_inc(consts, 1)
            nc.gpsimd.memset(ident[:, :], 0.0).then_inc(consts, 1)
            nc.gpsimd.memset(tri, 1.0).then_inc(consts, 1)
            nc.gpsimd.memset(zero16, 0.0).then_inc(consts, 1)
            nc.gpsimd.iota(iota_hi, [[1, CHUNKS]], base=0, channel_multiplier=0,
                           allow_small_or_imprecise_dtypes=True).then_inc(consts, 1)
            nc.gpsimd.iota(iota_lo, [[1, P]], base=0, channel_multiplier=0,
                           allow_small_or_imprecise_dtypes=True).then_inc(consts, 1)
            pool.wait_ge(consts, 9)
            nc.gpsimd.affine_select(out=ident[:, :], in_=ident[:, :], compare_op=ALU.not_equal, fill=1.0, base=0,
                                    pattern=[[-1, P]], channel_multiplier=1).then_inc(consts, 1)
            nc.gpsimd.affine_select(out=tri, in_=tri, compare_op=ALU.is_gt, fill=0.0, base=0,
                                    pattern=[[1, EP]], channel_multiplier=-1).then_inc(consts, 1)
            pool.wait_ge(consts, CONSTS - 1)
            nc.gpsimd.tensor_copy(identb[:, :], ident[:, :]).then_inc(consts, 1)

            def scatter_stage(i):
                for q in range(2):
                    pool.wait_ge(sc_staged[q], i + 1)
                    pool.sem_inc(stages_begun, 1)
                    for k in range(SC):
                        s = q * SC + k
                        if not isinstance(i, int) or s >= SPLIT:
                            pool.wait_ge(sc_done[k % SPLIT], 16 * (2 * q + k // SPLIT) + i * (32 * SC // SPLIT))
                            pool.sem_inc(stages_begun, 1)
                        pool.indirect_dma_start(
                            out=recs_dram[k % SPLIT],
                            out_offset=bass.IndirectOffsetOnAxis(ap=sst_idx[:, s:s + 1], axis=0),
                            in_=sst_rec[:, s, :], in_offset=None).then_inc(sc_done[k % SPLIT], 16)

            def gather_pair(i, j, src, dst):
                pool.wait_ge(staged, i * SP_IT + j + 1)
                pool.sem_inc(stages_begun, 1)
                for c in (2 * j, 2 * j + 1):
                    pool.indirect_dma_start(
                        out=dst[:, c, :], out_offset=None, in_=src,
                        in_offset=bass.IndirectOffsetOnAxis(ap=stg_idx[:, c:c + 1], axis=0)
                    ).then_inc(landed[j], 16)

            def gathers(n, src, dst, first=0):
                with pool.Fori(n * ITERS + first, (n + 1) * ITERS) as i:
                    for j in range(SP_IT):
                        gather_pair(i, j, src, dst)

            def table_ready(layer):
                pool.wait_ge(tab_written, 16 * (NB // GROUP + 1) * (layer + 1))

            def clear(which):
                nc.gpsimd.memset(acc[:, which * 3 * NP:(which + 1) * 3 * NP], 0.0).then_inc(sums_clear, 1)

            def all_filled(st):
                b, c = jobs[st][-1]
                pool.wait_ge(filled[b], c)

            pool.wait_ge(zero_filled, 16 * SPLIT)
            scatter_stage(0)
            with pool.Fori(1, NORM_AT + 1) as i:
                scatter_stage(i)
            pool.wait_ge(order_ready, 2)
            clear(0)
            with pool.Fori(NORM_AT + 1, SIT) as i:
                scatter_stage(i)
            table_ready(0)
            gathers(0, table, rowsbuf)
            pool.wait_ge(rec_loaded, 16 * SPLIT)
            for k in range(SPLIT - 1):
                nc.gpsimd.tensor_tensor(recs[1][:, :, :], recs[1][:, :, :], part[k], ALU.add).then_inc(merged, 1)
                pool.wait_ge(merged, k + 1)
            clear(1)
            all_filled("back0")
            pool.wait_ge(deg_stored, 16)
            clear(0)
            table_ready(1)
            gathers(1, table, rowsbuf)
            gathers(2, table, rowsbuf)
            all_filled("back1")
            clear(0)
            table_ready(2)
            gathers(3, table, rowsbuf)
            all_filled("T3")
            nc.gpsimd.memset(Hm[:, 0:NB * D], 0.0).then_inc(sums_clear, 1)
            pool.wait_ge(parked, 32)
            for q in range(QS):
                pool.wait_ge(q_stored[q], 16 * (NB // QS))
            for j in range(4):
                gather_pair(4 * ITERS, j, qtable, hbuf)
            all_filled("p3")
            nc.gpsimd.memset(Hm[:, NB * D:4 * NP], 0.0).then_inc(sums_clear, 1)
            for j in range(4, SP_IT):
                gather_pair(4 * ITERS, j, qtable, hbuf)
            gathers(4, qtable, hbuf, 1)

        @block.scalar
        def _(act):
            def stage_half(i, q):
                uses = 2 * SC // SPLIT
                if not isinstance(i, int) or i > 0:
                    for k in range(SPLIT):
                        act.wait_ge(sc_done[k], i * (16 * uses) + (0 if q else -8 * uses))
                c0 = i * (2 * SC) + q * SC
                nc.scalar.copy(sst_idx[:, q * SC:(q + 1) * SC], slot[:, ds(c0, SC)])
                nc.scalar.copy(sst_rec[:, q * SC:(q + 1) * SC, :], erec[:, ds(c0, SC), :]).then_inc(sc_staged[q], 1)

            def stage_scatter(first, end):
                with act.Fori(first, end) as i:
                    for q in range(2):
                        stage_half(i, q)

            def weigh(n, m, c):
                act.wait_ge(lo_made, n + 1)
                for k in range(1, 4):
                    last = nc.scalar.activation(val_ring[:, c, k, :], lo_ring[:, c, :], ACT.Copy,
                                                scale=held[:, m, c, 3 + k:4 + k])
                last.then_inc(weighed, 1)

            def deviations(n, t0, m):
                act.wait_ge(ln_var, n)
                nc.scalar.activation(lnr[:, t0:t0 + m], lnmv[:, t0:t0 + m, 1], ACT.Sqrt,
                                     bias=epst[:, 0:1], scale=1.0).then_inc(std_ready, 1)

            def norm_blocks(n, t0, m):
                act.wait_ge(ln_ready, n)
                for t in range(t0, t0 + m):
                    r = rows(t)
                    nc.scalar.activation(Tm[0:r, t, :], xt[0:r, t, :], ACT.Relu, bias=lnb[0:r, t:t + 1],
                                         scale=lnr[0:r, t:t + 1]).then_inc(normed, 1)

            def norm_group(layer, g):
                n = (layer - 1) * (NB // GROUP) + g + 2
                deviations(n, g * GROUP, GROUP)
                if g >= 1:
                    norm_blocks(n - 1, (g - 1) * GROUP, GROUP)
                if g == NB // GROUP - 1:
                    norm_blocks(n, g * GROUP, GROUP)

            def norm_rows(layer):
                for g in range(NB // GROUP):
                    norm_group(layer, g)

            def take_transpose(layer, g):
                st = f"T{layer}"
                src = wait_filled(act, st, 2 * g)
                n = min(512, N - 512 * g)
                nc.scalar.copy(TT[:, 0, 512 * g:512 * g + n], src[:, 0:n]).then_inc(emptied[bank(st, 2 * g)], 1)

            def take_transposes(layer):
                for g in range(len(TG)):
                    take_transpose(layer, g)

            def stage_pair(i, n, j):
                act.wait_ge(summed, i * CH_IT + 2 * j + 2)
                c0 = (i - n * ITERS) * CH_IT + 2 * j
                o = PASSES[n][0]
                nc.scalar.copy(stg_lw[:, 2 * j:2 * j + 2, :], recs[o][:, ds(c0, 2), 1:4])
                nc.scalar.copy(stg_idx[:, 2 * j:2 * j + 2], recs[o][:, ds(c0, 2), 0]).then_inc(staged, 1)

            def stage_iteration(i, n):
                for j in range(SP_IT):
                    stage_pair(i, n, j)

            def stage_first(n):
                stage_iteration(n * ITERS, n)

            def stage_rest(n):
                with act.Fori(n * ITERS + 1, (n + 1) * ITERS) as i:
                    stage_iteration(i, n)

            def take_products(st, bias, dst, nf):
                for n in range(NT):
                    for f in range(nf):
                        src = wait_filled(act, st, n * nf + f)
                        nc.scalar.activation(dst[:, f, cols(n)], src[:, 0:width(n)], ACT.Identity, bias=v(bias, f),
                                             scale=1.0).then_inc(emptied[bank(st, n * nf + f)], 1)

            def bn_deviation(k, nf):
                act.wait_ge(bn_var, k)
                nc.scalar.activation(bA[:, 0:nf], bmv[:, 0:nf, 1], ACT.Sqrt, bias=epst[:, 0:1],
                                     scale=1.0).then_inc(bn_std, 1)
                act.wait_ge(bn_ready, k)

            def scale_tiles(dst, nf, func):
                for n in range(NT):
                    for f in range(nf):
                        nc.scalar.activation(dst[:, f, cols(n)], dst[:, f, cols(n)], func, bias=bC[:, f:f + 1],
                                             scale=bA[:, f:f + 1]).then_inc(act_ready, 1)

            act.sem_inc(flip_copied, 1)
            act.sem_inc(gates_kept, 1)
            act.wait_ge(order_ready, 1)
            stage_half(0, 0)
            stage_half(0, 1)
            stage_scatter(1, NORM_AT - 1)
            deviations(1, 0, NB)
            stage_half(NORM_AT - 1, 0)
            act.wait_ge(order_ready, 2)
            act.wait_ge(zero_filled, 16 * SPLIT)
            norm_blocks(1, 0, NB)
            stage_half(NORM_AT - 1, 1)
            with act.Fori(NORM_AT, SIT) as i:
                for k in range(COLS):
                    if k in (0, COLS // 2):
                        stage_half(i, 1 if k else 0)
                    weigh((i - NORM_AT) * COLS + k, k // RING, k % RING)
            act.wait_ge(sc_staged[1], SIT)
            act.wait_ge(rec0_ready, 1)
            stage_first(0)
            take_transposes(0)
            stage_rest(0)
            act.wait_ge(vec_loaded, 16 * NVEC)
            take_products("up0", "L0_gnn_b1", H, 4)
            bn_deviation(1, 4)
            scale_tiles(H, 4, ACT.Relu)
            bn_deviation(2, 2)
            scale_tiles(U, 2, ACT.Relu)
            norm_rows(1)
            stage_first(1)
            take_transposes(1)
            for k in range(1, 4):
                stage_iteration(ITERS + k, 1)
            bn_deviation(3, 2)
            for f in range(2):
                stage_iteration(ITERS + 4 + f, 1)
                for n in range(NT):
                    nc.scalar.activation(TT[:, f, cols(n)], TT[:, f, cols(n)], ACT.Identity, bias=bC[:, f:f + 1],
                                         scale=bA[:, f:f + 1]).then_inc(act_ready, 1)
            with act.Fori(ITERS + 6, ITERS + FOLD_AT + 1) as i:
                stage_iteration(i, 1)
            for q in range(2):
                src = wait_filled(act, "turn1", q)
                nc.scalar.copy(WT[q].rearrange("p m n -> p (m n)"), src[:, :]).then_inc(emptied[bank("turn1", q)], 1)
            src = wait_filled(act, "turn1", 2)
            for q, name in enumerate(("L1_gnn_b_in", "L1_gnn_b_out")):
                for m in range(2):
                    last = nc.scalar.activation(ccol[:, 2 * q + m:2 * q + m + 1], src[:, 2 * q + m:2 * q + m + 1],
                                                ACT.Identity, bias=v(name, m), scale=1.0)
            last.then_inc(emptied[bank("turn1", 2)], 1)
            for q in range(2):
                with act.Fori(ITERS + FOLD_AT + 1 + q, ITERS + FOLD_AT + 2 + q) as i:
                    stage_iteration(i, 1)
                for k in range(2):
                    src = wait_filled(act, "fold1", 3 * q + k)
                    nc.scalar.activation(fold[q][:, k, :], src[:, :], ACT.Copy,
                                         scale=bA[:, k:k + 1]).then_inc(emptied[bank("fold1", 3 * q + k)], 1)
                src = wait_filled(act, "fold1", 3 * q + 2)
                nc.scalar.copy(fold_row[q], src[0:1, :]).then_inc(emptied[bank("fold1", 3 * q + 2)], 1)
            with act.Fori(ITERS + FOLD_AT + 3, 2 * ITERS) as i:
                stage_iteration(i, 1)
            act.wait_ge(merged, SPLIT - 1)

            def keep_gates(u):
                act.wait_ge(gates_begun, u + 1)
                src = ps[5][:, 0:4 * UNIT].rearrange("p (f n) -> p f n", f=4)
                nc.scalar.copy(gate01[:, ds(u, 1), :, :].rearrange("p u f n -> p (u f) n"), src[:, 0:2, :])
                nc.scalar.copy(sums[0][:, 0:2, ds(u * UNIT, UNIT)], src[:, 2:4, :]).then_inc(gates_kept, 1)

            stage_iteration(2 * ITERS, 2)
            with act.Fori(1, UNITS + 1) as u:
                for j in range(SP_IT):
                    stage_pair(u + 2 * ITERS, 2, j)
                    if j == 0:
                        keep_gates(u - 1)
            with act.Fori(2 * ITERS + UNITS + 1, 3 * ITERS) as i:
                stage_iteration(i, 2)
            for n in range(GTILES):
                for f in range(4):
                    wait_emptied(act, "gates1", 4 * n + f)
                    at = (gate01 if f < 2 else gate23)[:, units(n), f % 2, :]
                    last = nc.scalar.activation(at, at, ACT.Sigmoid if f < 2 else ACT.Tanh,
                                                bias=v("L1_gnn_b_x2i", f), scale=1.0)
                last.then_inc(gates_ready, 1)
                for g in groups_by(n - 2):
                    norm_group(2, g)
            for g in groups_by(GTILES - 2) + groups_by(GTILES - 1):
                norm_group(2, g)
            stage_first(3)
            take_transposes(2)
            stage_rest(3)
            take_products("up2", "L2_gnn_b1", H, 2)
            bn_deviation(4, 2)
            scale_tiles(H, 2, ACT.Relu)
            take_products("down2", "L2_gnn_b2", U, 2)
            bn_deviation(5, 2)
            scale_tiles(U, 2, ACT.Relu)
            norm_rows(3)

            def take_q(t):
                src = wait_filled(act, "q3", t)
                if t >= QS:
                    act.wait_ge(q_stored[t % QS], 16 * (t // QS))
                nc.scalar.copy(qst[0:rows(t), t % QS, :], src[0:rows(t), :]).then_inc(emptied[bank("q3", t)], 1)

            for g in range(len(TG) + 1):
                if g < len(TG):
                    take_transpose(3, g)
                for t in blocks_of(g - 1):
                    if t < Q_FIRST:
                        take_q(t)
            for j in range(4):
                stage_pair(4 * ITERS, 4, j)

            def p_part(t, part3):
                nc.scalar.copy(PT[0:rows(t), t, part3, :], pf[t % PFS][0:rows(t), :]).then_inc(p_hi, 1)

            for t in range(NB + 1):
                if t < NB:
                    wait_emptied(act, "p3", t)
                    if t == NB - 1:
                        act.wait_ge(last_clear, 1)
                    p_part(t, 0)
                if t >= 1:
                    act.wait_ge(p_sum, t)
                    p_part(t - 1, 1)
                if Q_FIRST + t < NB:
                    take_q(Q_FIRST + t)

            def flips(i, j):
                l = i - 4 * ITERS
                act.wait_ge(flipped, l * SP_IT + j + 1)
                act.wait_ge(spread, l * CH_IT + 2 * j + 2)
                nc.scalar.copy(ohT[:, 2 * j:2 * j + 2, :], flip_bank).then_inc(flip_copied, 1)

            def relus(i, j):
                for c in (2 * j, 2 * j + 1):
                    act.wait_ge(joined, (i - 4 * ITERS) * CH_IT + c + 3)
                    nc.scalar.activation(hbuf[:, c, :], hbuf[:, c, :], ACT.Relu).then_inc(relued, 1)

            act.wait_ge(p_ready, NB)
            flips(4 * ITERS, 0)
            flips(4 * ITERS, 1)
            relus(4 * ITERS, 0)

            def body4(i, last):
                for j in range(SP_IT):
                    for d, do in ((4, lambda i, j: stage_pair(i, 4, j)), (2, flips), (1, relus)):
                        if (nxt := ahead(i, j, d, last)) is not None:
                            do(*nxt)

            iterations(act, 4, body4)

        @block.vector
        def _(dve):
            nstep = [0]

            def link(ins):
                nstep[0] += 1
                ins.then_inc(vstep, 1)
                dve.wait_ge(vstep, nstep[0])

            V = nc.vector

            def sort(o):
                key, other = key_i[o], key_i[1 - o]
                link(V.tensor_scalar(ti, key, 7, None, ALU.arith_shift_right))
                link(V.tensor_copy(blkf, ti))
                link(V.tensor_scalar(ti2, key, 127, None, ALU.bitwise_and))
                if o == 1:
                    V.tensor_scalar(erec[:, :, 1], ti2, 1.0, None, ALU.add)
                    V.tensor_copy(erec[:, :, 0], other)
                    V.tensor_copy(erec[:, :, 2], wts[0])
                    V.tensor_copy(erec[:, :, 3], wts[1])
                else:
                    V.tensor_scalar(fields[:, :, 3], ti2, 1.0, None, ALU.add)
                    V.tensor_scalar(fields[:, :, 2], other, float(-MID), None, ALU.add)
                    link(V.tensor_copy(part16, wts[0]))
                    link(V.tensor_copy(fields[:, :, 4], part16))
                    link(V.tensor_tensor(wts[0], wts[0], fields[:, :, 4], ALU.subtract))
                    link(V.tensor_copy(part16, wts[0]))
                    link(V.tensor_copy(fields[:, :, 5], part16))
                    V.tensor_tensor(fields[:, :, 6], wts[0], fields[:, :, 5], ALU.subtract)
                for b in range(NB):
                    last = V.tensor_scalar(mask[:, b, :], blkf, float(b), None, ALU.is_equal)
                link(last)
                flat = "p b c -> p (b c)"
                link(V.tensor_tensor_scan(run.rearrange(flat), ones[0:EP, 0:1].to_broadcast([EP, NB * EC]),
                                          mask.rearrange(flat), 0.0, ALU.mult, ALU.add))
                ends, tot, padded, bend, off = (srt[:, k, :] for k in range(5))
                link(V.tensor_copy(ends[0:EP, :], run[:, :, EC - 1]))
                V.tensor_copy(tot[0:EP, 0:1], ends[0:EP, 0:1])
                V.tensor_tensor(tot[0:EP, 1:NB], ends[0:EP, 1:NB], ends[0:EP, 0:NB - 1],
                                ALU.subtract).then_inc(totals_ready, 1)
                cnt = wait_filled(dve, f"count{o}", 0)
                link(V.tensor_scalar(srti[:, :], cnt[:, 32:32 + NB], float(P - 1), None, ALU.add))
                link(V.tensor_scalar(srti[:, :], srti[:, :], 7, 7, ALU.arith_shift_right, ALU.logical_shift_left))
                link(V.tensor_copy(padded, srti[:, :]))
                V.tensor_tensor_scan(bend, ones[:, 0:NB], padded, 0.0, ALU.mult, ALU.add).then_inc(ends_ready, 1)
                dve.wait_ge(ends_ready, 3 - 2 * o)
                e = slice(0, EP)
                link(V.tensor_tensor(off[e], bend[e], padded[e], ALU.subtract))
                V.tensor_tensor(off[e], off[e], cnt[e, 0:NB], ALU.add).then_inc(emptied[bank(f"count{o}", 0)], 1)
                wait_emptied(dve, f"count{o}", 0)
                link(V.tensor_tensor(off[e], off[e], ends[e], ALU.subtract))
                link(V.scalar_tensor_tensor(off[e], off[e], -1.0, tot[e], ALU.add, ALU.add))
                src = wait_filled(dve, f"table{o}", 0)
                V.tensor_copy(ends_col, src[0:NB - 1, 0:1]).then_inc(emptied[bank(f"table{o}", 0)], 1)
                wait_emptied(dve, f"table{o}", 0)
                V.tensor_scalar(ends_ge, cstart[0:NB - 1, :], ends_col, None, ALU.is_ge).then_inc(ends_ready, 1)
                for b in range(NB):
                    last = V.scalar_tensor_tensor(run[:, b, :], run[:, b, :], off[e][:, b:b + 1], mask[:, b, :],
                                                  ALU.add, ALU.mult)
                link(last)
                link(V.tensor_reduce(pos, run.rearrange("p b c -> p c b"), AX.X, ALU.add))
                link(V.tensor_copy(ti, pos))
                V.tensor_scalar(ti2, ti, P - 1, None, ALU.bitwise_and)
                link(V.tensor_scalar(ti, ti, 7, None, ALU.arith_shift_right))
                if o == 1:
                    V.scalar_tensor_tensor(slot, ti2, float(CHUNKS), ti, ALU.mult, ALU.add).then_inc(order_ready, 1)
                else:
                    V.tensor_copy(fields[:, :, 0], ti2)
                    V.tensor_copy(fields[:, :, 1], ti).then_inc(order_ready, 1)
                dve.wait_ge(order_ready, 2 - o)
                q = slice(32 * o, 32 * o + 1)
                src = wait_filled(dve, f"table{o}", 1)
                V.tensor_scalar(blk_tab[o], src[q, 0:CHUNKS], float(P), None,
                                ALU.mult).then_inc(emptied[bank(f"table{o}", 1)], 1)
                wait_emptied(dve, f"table{o}", 1)

            def ln_stats(g, back=None):
                stats = []
                for t in range(g * GROUP, (g + 1) * GROUP + 2):
                    if back is not None and t < (g + 1) * GROUP:
                        add_back(back, t)
                    if g * GROUP <= t - 1 < (g + 1) * GROUP:
                        r = rows(t - 1)
                        if back is not None:
                            wait_emptied(dve, back, t - 1)
                        V.bn_stats(lnst[0:r, (t - 1) % (2 * GROUP), :], xt[0:r, t - 1, :]).then_inc(vstep, 1)
                        nstep[0] += 1
                        stats.append(nstep[0])
                    if g * GROUP <= t - 2:
                        r = rows(t - 2)
                        dve.wait_ge(vstep, stats[t - 2 - g * GROUP])
                        last = V.bn_aggr(lnmv[0:r, t - 2, :], lnst[0:r, (t - 2) % (2 * GROUP), :])
                return last

            def ln_scale(n, sl):
                dve.wait_ge(std_ready, n)
                dve.wait_ge(ln_var, n)
                link(V.reciprocal(lnr[:, sl], lnr[:, sl]))
                V.scalar_tensor_tensor(lnb[:, sl], lnmv[:, sl, 0], -1.0, lnr[:, sl], ALU.mult,
                                       ALU.mult).then_inc(ln_ready, 1)

            def ln_group(layer, back, g):
                ln_stats(g, back).then_inc(ln_var, 1)
                n = (layer - 1) * (NB // GROUP) + g + 2
                if g >= 1:
                    ln_scale(n - 1, slice((g - 1) * GROUP, g * GROUP))
                if g == NB // GROUP - 1:
                    ln_scale(n, slice(g * GROUP, (g + 1) * GROUP))

            def layer_norm(layer, back):
                for g in range(NB // GROUP):
                    ln_group(layer, back, g)

            def add_back(st, t):
                r = rows(t)
                src = wait_filled(dve, st, t)
                V.tensor_tensor(xt[0:r, t, :], xt[0:r, t, :], src[0:r, 0:D], ALU.add).then_inc(
                    emptied[bank(st, t)], 1)

            def take_transposes(layer):
                st = f"T{layer}"
                for g in range(len(TG)):
                    src = wait_filled(dve, st, 2 * g + 1)
                    n = min(512, N - 512 * g)
                    V.tensor_copy(TT[:, 1, 512 * g:512 * g + n], src[:, 0:n]).then_inc(emptied[bank(st, 2 * g + 1)], 1)
                wait_emptied(dve, st, 2 * len(TG) - 2)
                wait_emptied(dve, st, 2 * len(TG) - 1)

            def make_hot(i, j, wcol):
                dve.wait_ge(staged, i * SP_IT + j + 1)
                for c in (2 * j, 2 * j + 1):
                    if wcol is None:
                        last = V.tensor_scalar(oh[:, c, :], iota1[:, :], stg_lw[:, c, 0:1], None, ALU.is_equal)
                    else:
                        last = V.tensor_scalar(oh[:, c, :], iota1[:, :], stg_lw[:, c, 0:1], stg_lw[:, c, wcol:wcol + 1],
                                               ALU.is_equal, ALU.mult)
                last.then_inc(hot, 1)

            def add_chunk(i, c, dst, block0, slots):
                dve.wait_ge(summed, i * CH_IT + c + 1 + CH_IT)
                dve.wait_ge(added, i * CH_IT + c + SB)
                at = dst[:, 0:slots, ds(block0, P)]
                src = sum_bank(c)[:, 0:slots * P].rearrange("p (k n) -> p k n", k=slots)
                V.tensor_tensor(at, at, src, ALU.add).then_inc(added, 1)

            def sum_pass(n, between=()):
                o, wcol, d = PASSES[n]

                def body(i, last):
                    first = block_starts(mybir.EngineType.DVE, o, i - n * ITERS, 0, CH_IT)
                    for j in range(SP_IT):
                        if (nxt := ahead(i, j, LEAD, last)) is not None:
                            make_hot(*nxt, wcol)
                        for c in (2 * j, 2 * j + 1):
                            add_chunk(i, c, sums[d], first[c], 3)

                for j in range(LEAD):
                    make_hot(n * ITERS, j, wcol)
                for k, step in enumerate(between):
                    body(n * ITERS + k, False)
                    step()
                iterations(dve, n, body, len(between))
                dve.wait_ge(added, (n + 1) * CHUNKS + SB)

            def gin_input(col):
                for n in range(NT):
                    for k in range(2):
                        V.scalar_tensor_tensor(sums[0][:, k, cols(n)], TT[:, k, cols(n)], vec[:, col:col + 1],
                                               sums[0][:, k, cols(n)], ALU.mult, ALU.add).then_inc(z_ready, 1)

            def bn_scale(k, nf, gamma, beta):
                for f in range(nf):
                    last = V.bn_aggr(bmv[:, f, :], bst[:, f, :, :].rearrange("p n s -> p (n s)"))
                last.then_inc(bn_var, 1)
                dve.wait_ge(bn_std, k)
                dve.wait_ge(bn_var, k)
                link(V.reciprocal(bA[:, 0:nf], bA[:, 0:nf]))
                link(V.tensor_tensor(bA[:, 0:nf], bA[:, 0:nf], v(gamma), ALU.mult))
                link(V.tensor_tensor(bC[:, 0:nf], bmv[:, 0:nf, 0], bA[:, 0:nf], ALU.mult))
                V.tensor_tensor(bC[:, 0:nf], v(beta), bC[:, 0:nf], ALU.subtract).then_inc(bn_ready, 1)

            def stats_of_tile(st, src, nf, n):
                for f in range(nf):
                    wait_emptied(dve, st, n * nf + f)
                    last = V.bn_stats(bst[:, f, n, :], src[:, f, cols(n)])
                return last

            def stats_of(st, src, nf):
                for n in range(NT):
                    last = stats_of_tile(st, src, nf, n)
                link(last)

            def place_edges():
                with dve.Fori(0, PIT) as i:
                    for m in range(ROUNDS):
                        n = i * COLS + m * RING
                        dve.wait_ge(made, n + 1)
                        V.tensor_copy(held[:, m, :, :], fields[:, ds(n, RING), :]).then_inc(held_ready, 1)
                        dve.wait_ge(held_ready, i * ROUNDS + m + 1)
                        for c in range(RING):
                            dve.wait_ge(used, n + c + 1)
                            f = held[:, m, c, :]
                            V.tensor_scalar(lo_ring[:, c, :], iota_lo, f[:, 0:1], None,
                                            ALU.is_equal).then_inc(lo_made, 1)
                            V.tensor_scalar(hi_ring[:, c, :], iota_hi, f[:, 1:2], None, ALU.is_equal)
                            V.tensor_scalar(src_ring[:, c, :], iota_lo, f[:, 0:1], f[:, 2:3], ALU.is_equal, ALU.mult)
                            V.tensor_scalar(val_ring[:, c, 0, :], iota_lo, f[:, 0:1], f[:, 3:4], ALU.is_equal,
                                            ALU.mult).then_inc(made, 1)

            def take_order():
                dve.wait_ge(placed, 1)
                p = [ps[k][:, 0:CHUNKS] for k in range(PARTS)]
                V.tensor_scalar(recs[0][:, :, 0], p[0], float(MID), None, ALU.add)
                V.tensor_copy(recs[0][:, :, 1], p[1])
                link(V.tensor_copy(recs[0][:, :, 2], p[2]))
                link(V.tensor_tensor(recs[0][:, :, 2], recs[0][:, :, 2], p[3], ALU.add))
                V.tensor_tensor(recs[0][:, :, 2], recs[0][:, :, 2], p[4], ALU.add).then_inc(rec0_ready, 1)

            dve.sem_inc(added, SB)
            dve.sem_inc(joined, 2)
            dve.sem_inc(made, 1)
            V.memset(epst[:, :], LN_EPS)
            V.memset(TTm[:, 2 * N:N + NP], 0.0)
            link(V.memset(lnmv[:, :, :], 1.0))
            dve.wait_ge(edges_loaded, 64)
            dve.wait_ge(consts, CONSTS)
            sort(1)
            dve.wait_ge(x_loaded, 32)
            for g in range(NB // GROUP):
                last = ln_stats(g)
            last.then_inc(ln_var, 1)
            sort(0)
            ln_scale(1, slice(0, NB))
            V.memset(recs[0][:, :, 3], 0.0)
            place_edges()
            take_order()
            dve.wait_ge(vec_loaded, 16 * NVEC)
            V.tensor_scalar(vec[:, eps_col[0]:eps_col[0] + 1], vec[:, eps_col[0]:eps_col[0] + 1], 1.0, None, ALU.add)
            link(V.tensor_scalar(vec[:, eps_col[2]:eps_col[2] + 1], vec[:, eps_col[2]:eps_col[2] + 1], 1.0, None,
                                 ALU.add))
            dve.wait_ge(sc_staged[1], SIT)
            take_transposes(0)
            dve.wait_ge(sums_clear, 1)
            for k in range(SPLIT):
                dve.wait_ge(sc_done[k], 16 * (EC // SPLIT))
            sum_pass(0)
            gin_input(eps_col[0])
            dve.wait_ge(deg_loaded, 16)
            V.tensor_scalar(rdeg_sq[:, :], rdeg_sq[:, :], 1e-8, None, ALU.add).then_inc(rdeg_ready, 1)
            dve.wait_ge(rdeg_ready, 1)
            V.reciprocal(rdeg_sq[:, :], rdeg_sq[:, :]).then_inc(rdeg_ready, 1)
            stats_of("up0", H, 4)
            bn_scale(1, 4, "L0_gnn_g1", "L0_gnn_bt1")
            for n in range(NT):
                for f in range(2):
                    k = n * 2 + f
                    src = wait_filled(dve, "down0", k)
                    V.scalar_tensor_tensor(U[:, f, cols(n)], src[:, 0:width(n)], v("L0_gnn_b2", f), TT[:, f, cols(n)],
                                           ALU.add, ALU.add).then_inc(emptied[bank("down0", k)], 1)
                if n >= 1:
                    stats_of_tile("down0", U, 2, n - 1)
            link(stats_of_tile("down0", U, 2, NT - 1))
            bn_scale(2, 2, "L0_gnn_g2", "L0_gnn_bt2")
            layer_norm(1, "back0")
            take_transposes(1)
            dve.wait_ge(sums_clear, 3)

            def node_stats(f):
                for n in range(NT):
                    last = V.bn_stats(bst[:, f, n, :], TT[:, f, cols(n)])
                link(last)

            sum_pass(1, [lambda: node_stats(0), lambda: node_stats(1),
                         lambda: bn_scale(3, 2, "L1_gnn_gamma", "L1_gnn_beta")])
            sum_pass(2)

            def sum_gates(n):
                for f in range(4):
                    src = wait_filled(dve, "gates1", 4 * n + f)
                    at = (gate01 if f < 2 else gate23)[:, units(n), f % 2, :]
                    V.tensor_tensor(at, at, src[:, 0:unit_cols(n).stop - unit_cols(n).start].rearrange(
                        "p (u n) -> p u n", n=UNIT), ALU.add).then_inc(emptied[bank("gates1", 4 * n + f)], 1)

            def finish(n):
                dve.wait_ge(gates_ready, n + 1)
                c = unit_cols(n)
                for k in range(2):
                    V.tensor_tensor(sums[1][:, k, c], TTu[k][:, c], sums[0][:, k, c], ALU.subtract).then_inc(vstep, 1)
                    nstep[0] += 1
                dve.wait_ge(vstep, nstep[0])
                t = sums[1][:, 0:2, c].rearrange("p f (u n) -> p u f n", n=UNIT)
                link(V.tensor_tensor(t, t, gate01[:, units(n), :, :], ALU.mult))
                V.tensor_tensor(sums[0][:, 0:2, c], sums[0][:, 0:2, c], sums[1][:, 0:2, c],
                                ALU.add).then_inc(u_ready, 1)

            for n in range(GTILES):
                sum_gates(n)
                for g in groups_by(n - 2):
                    ln_group(2, "back1", g)
                if n >= 1:
                    finish(n - 1)
            finish(GTILES - 1)
            for g in groups_by(GTILES - 2) + groups_by(GTILES - 1):
                ln_group(2, "back1", g)
            take_transposes(2)
            dve.wait_ge(sums_clear, 4)
            sum_pass(3)
            gin_input(eps_col[2])
            dve.wait_ge(w_loaded[3], 32)
            V.tensor_tensor(W1e[:, 0:2, :], W1e[:, 0:2, :], W1e[:, 2:4, :], ALU.subtract).then_inc(wdiff, 1)
            stats_of("up2", H, 2)
            bn_scale(4, 2, "L2_gnn_g1", "L2_gnn_be1")
            stats_of("down2", U, 2)
            bn_scale(5, 2, "L2_gnn_g2", "L2_gnn_be2")
            layer_norm(3, "back2")
            take_transposes(3)
            V.memset(PT[:, NB - 1, :, :].rearrange("p r f -> p (r f)"), 0.0).then_inc(last_clear, 1)
            dve.wait_ge(b1_loaded, 16)

            def hots(i, j):
                make_hot(i, j, None)

            hots(4 * ITERS, 0)
            hots(4 * ITERS, 1)

            def p_written(t, part3):
                return max(1, 2 * t) if part3 == 0 else min(2 * t + 3, 2 * NB)

            for t in range(NB + 2):
                if t < NB:
                    r = rows(t)
                    src = wait_filled(dve, "p3", t)
                    if t >= PFS:
                        dve.wait_ge(p_ready, t - PFS + 1)
                    V.tensor_tensor(pf[t % PFS][0:r, :], src[0:r, :], b1bc[0:r, :],
                                    ALU.add).then_inc(emptied[bank("p3", t)], 1)
                if 1 <= t <= NB:
                    r, p = rows(t - 1), pf[(t - 1) % PFS]
                    dve.wait_ge(p_hi, p_written(t - 1, 0))
                    V.tensor_tensor(p[0:r, :], p[0:r, :], PT[0:r, t - 1, 0, :], ALU.subtract).then_inc(p_sum, 1)
                if t >= 2:
                    r, p = rows(t - 2), pf[(t - 2) % PFS]
                    dve.wait_ge(p_hi, p_written(t - 2, 1))
                    V.tensor_tensor(PT[0:r, t - 2, 2, :], p[0:r, :], PT[0:r, t - 2, 1, :],
                                    ALU.subtract).then_inc(p_ready, 1)
            dve.wait_ge(last_clear, 1)
            dve.wait_ge(sums_clear, 6)

            def join(i, j):
                dve.wait_ge(landed[j], 32 * i + 32)
                for c in (2 * j, 2 * j + 1):
                    dve.wait_ge(spread, (i - 4 * ITERS) * CH_IT + c + 1 + CH_IT)
                    V.tensor_tensor(hbuf[:, c, :], hbuf[:, c, :], spread_bank(c), ALU.add).then_inc(joined, 1)

            def add_hidden(i, j, start):
                for c in (2 * j, 2 * j + 1):
                    add_chunk(i, c, H, start[c], 4)

            join(4 * ITERS, 0)

            def body4(i, last):
                first = block_starts(mybir.EngineType.DVE, 0, i - 4 * ITERS, 0, CH_IT)
                for j in range(SP_IT):
                    if (nxt := ahead(i, j, 2, last)) is not None:
                        hots(*nxt)
                    if j >= 1:
                        add_hidden(i, j - 1, first)
                    if (nxt := ahead(i, j, 1, last)) is not None:
                        join(*nxt)
                add_hidden(i, SP_IT - 1, first)

            iterations(dve, 4, body4)
            dve.wait_ge(added, 5 * CHUNKS + SB)
            dve.wait_ge(deg_loaded, 48)
            for n in range(NT):
                for f in range(2):
                    k = n * 2 + f
                    src = wait_filled(dve, "down3", k)
                    b, c = jobs["down3"][k]
                    V.scalar_tensor_tensor(U[:, f, cols(n)], deg[:, cols(n)], v("L3_gnn_b2", f), src[:, 0:width(n)],
                                           ALU.mult, ALU.add).then_inc(emptied[b], 1)
                    dve.wait_ge(emptied[b], c)
                    V.tensor_tensor(U[:, f, cols(n)], U[:, f, cols(n)], rdeg[:, cols(n)], ALU.mult).then_inc(u_ready, 1)
                if n == 1:
                    dve.wait_ge(unparked, 32)
                for t in ended_by(n - 1):
                    add_back("back3", t)
            for t in ended_by(NT - 1):
                add_back("back3", t)

        @block.tensor
        def _(pe):
            mm = nc.tensor.matmul

            def take_bank(st, k):
                b, c = jobs[st][k]
                if c > 1:
                    pe.wait_ge(emptied[b], c - 1)
                return ps[b]

            def done(ins, st, k):
                ins.then_inc(filled[bank(st, k)], 1)

            def counts(o, turn):
                pe.wait_ge(totals_ready, turn)
                dst = take_bank(f"count{o}", 0)
                tot = srt[0:EP, 1, :]
                mm(dst[0:EP, 0:NB], tri, tot, start=True, stop=True)
                done(mm(dst[:, 32:32 + NB], ones[0:EP, :], tot, start=True, stop=True), f"count{o}", 0)

            def chunk_table(o, turn):
                pe.wait_ge(ends_ready, turn + 1)
                dst = take_bank(f"table{o}", 0)
                done(nc.tensor.transpose(dst[0:NB, 0:P], srt[:, 3, :], ident[:, :]), f"table{o}", 0)
                pe.wait_ge(ends_ready, turn + 2)
                dst = take_bank(f"table{o}", 1)
                done(mm(dst[0:64, 0:CHUNKS], ones[0:NB - 1, 0:64], ends_ge, start=True, stop=True), f"table{o}", 1)

            def transpose_group(layer, g):
                st, blocks = f"T{layer}", blocks_of(g)
                pe.wait_ge(normed, layer * NB + blocks[-1] + 1)
                for k in range(2):
                    dst = take_bank(st, 2 * g + k)
                    for t in blocks:
                        r = rows(t)
                        o = (t - 4 * g) * P
                        last = nc.tensor.transpose(dst[:, o:o + r], Tm[0:r, t, k * P:(k + 1) * P],
                                                   ident[0:r, 0:r])
                    done(last, st, 2 * g + k)

            def transposes(layer):
                for g in range(len(TG)):
                    transpose_group(layer, g)

            def back(st, ready, count, blocks=range(NB), tile=W):
                for t in blocks:
                    r = rows(t)
                    pe.wait_ge(ready, count((t * P + r - 1) // tile))
                    dst = take_bank(st, t)
                    for k in range(2):
                        last = nc.tensor.transpose(dst[0:r, k * P:(k + 1) * P], U[:, k, t * P:t * P + r],
                                                   ident[:, :])
                    done(last, st, t)

            def drained(stage):
                last = [0] * 8
                for name in ORDER[:ORDER.index(stage)]:
                    for b, c in jobs[name]:
                        last[b] = max(last[b], c)
                for b in range(8):
                    if last[b]:
                        pe.wait_ge(emptied[b], last[b])

            def sum_pair(i, j):
                pe.wait_ge(hot, i * SP_IT + j + 1)
                pe.wait_ge(landed[j], 32 * i + 32)
                for c in (2 * j, 2 * j + 1):
                    pe.wait_ge(added, i * CH_IT + c + 1)
                    for k in range(3):
                        lhs = rowsbuf[:, c, k * P:(k + 1) * P] if k < 2 else ones[:, :]
                        last = mm(sum_bank(c)[:, k * P:(k + 1) * P], lhs, oh[:, c, :], start=True, stop=True)
                    last.then_inc(summed, 1)

            def sum_pass(n, first=0, end=ITERS):
                with pe.Fori(n * ITERS + first, n * ITERS + end) as i:
                    for j in range(SP_IT):
                        sum_pair(i, j)

            def pass_end(n):
                pe.wait_ge(added, (n + 1) * CHUNKS + SB)

            def products(st, n, nf, terms, k0=0):
                for f in range(nf):
                    dst = take_bank(st, k0 + f)
                    for m, (w, src) in enumerate(terms):
                        last = mm(dst[:, 0:width(n)], w[:, f * P:(f + 1) * P], src, start=(m == 0),
                                  stop=(m == len(terms) - 1))
                    done(last, st, k0 + f)

            def up(st, w, nf, z0):
                for n in range(NT):
                    pe.wait_ge(z_ready, z0 + 2 * (n + 1))
                    products(st, n, nf, [(w[:, k, :], sums[0][:, k, cols(n)]) for k in range(2)], n * nf)

            def down(st, w, nk, a0):
                for n in range(NT):
                    pe.wait_ge(act_ready, a0 + nk * (n + 1))
                    products(st, n, 2, [(w[:, k, :], H[:, k, cols(n)]) for k in range(nk)], n * 2)

            pe.sem_inc(summed, CH_IT)
            pe.sem_inc(spread, CH_IT)
            pe.sem_inc(used, RING)
            pe.wait_ge(consts, CONSTS)
            counts(1, 1)
            chunk_table(1, 0)
            counts(0, 2)
            chunk_table(0, 2)
            pe.wait_ge(order_ready, 2)
            for k in range(PARTS):
                mm(ps[k][:, 0:CHUNKS], zero16[:, 0:P], zero16, start=True, stop=False)
            with pe.Fori(0, PIT) as i:
                for k0 in range(COLS):
                    c = k0 % RING
                    pe.wait_ge(made, i * COLS + k0 + 2)
                    pe.wait_ge(weighed, i * COLS + k0 + 1)
                    for k in range(PARTS):
                        lhs = src_ring[:, c, :] if k == 0 else val_ring[:, c, k - 1, :]
                        last = mm(ps[k][:, 0:CHUNKS], lhs, hi_ring[:, c, :], start=False, stop=False)
                    last.then_inc(used, 1)
            for k in range(PARTS):
                last = mm(ps[k][:, 0:CHUNKS], zero16[:, 0:P], zero16, start=False, stop=True)
            last.then_inc(placed, 1)
            transposes(0)
            drained("up0")
            sum_pass(0)
            pass_end(0)
            pe.wait_ge(w_loaded[0], 32)
            up("up0", W1a, 4, 0)
            down("down0", W2a, 4, 0)
            back("back0", act_ready, lambda n: 4 * NT + 2 * (n + 1))
            transposes(1)
            drained("turn1")
            sum_pass(1, 0, FOLD_AT)
            pe.wait_ge(w_loaded[1], 64)
            for q, w in enumerate((Win, Wout)):
                dst = take_bank("turn1", q)
                for m in range(2):
                    for k in range(2):
                        last = nc.tensor.transpose(dst[:, m * D + k * P:m * D + (k + 1) * P],
                                                   w[:, k, m * P:(m + 1) * P], ident[:, :])
                done(last, "turn1", q)
            dst = take_bank("turn1", 2)
            pe.wait_ge(bn_ready, 3)
            for q, w in enumerate((Win, Wout)):
                for m in range(2):
                    for k in range(2):
                        last = mm(dst[:, 2 * q + m:2 * q + m + 1], w[:, k, m * P:(m + 1) * P], bC[:, k:k + 1],
                                  start=(k == 0), stop=(k == 1))
            done(last, "turn1", 2)
            for q in range(2):
                sum_pass(1, FOLD_AT + q, FOLD_AT + 1 + q)
                for k in range(3):
                    wait_emptied(pe, "turn1", k)
                for k in range(3):
                    dst = take_bank("fold1", 3 * q + k)
                    for m in range(2):
                        if k < 2:
                            last = mm(dst[:, :], WT[q][:, m, k * P:(k + 1) * P], Wx2i[:, 2 * q + m, :],
                                      start=(m == 0), stop=(m == 1))
                        else:
                            last = mm(dst[0:1, :], ccol[:, 2 * q + m:2 * q + m + 1], Wx2i[:, 2 * q + m, :],
                                      start=(m == 0), stop=(m == 1))
                    done(last, "fold1", 3 * q + k)
            sum_pass(1, FOLD_AT + 2, ITERS)
            pass_end(1)
            pe.wait_ge(act_ready, 8 * NT)
            for k in range(6):
                wait_emptied(pe, "fold1", k)
            with pe.Fori(0, UNITS) as u:
                for j in range(SP_IT):
                    sum_pair(u + 2 * ITERS, j)
                    if j == 0:
                        pe.wait_ge(gates_kept, u + 1)
                        for f in range(4):
                            fs = slice(f * P, (f + 1) * P)
                            terms = ([(fold[0][:, k, fs], sums[0][:, k, ds(u * UNIT, UNIT)]) for k in range(2)]
                                     + [(fold_row[0][:, fs], sums[0][0:1, 2, ds(u * UNIT, UNIT)])]
                                     + [(Wh2h[:, k, fs], TTu[k][:, ds(u * UNIT, UNIT)]) for k in range(2)])
                            for m, (w, src) in enumerate(terms):
                                last = mm(ps[5][:, f * UNIT:(f + 1) * UNIT], w, src, start=(m == 0),
                                          stop=(m == len(terms) - 1))
                        last.then_inc(gates_begun, 1)
            sum_pass(2, UNITS, ITERS)
            pass_end(2)
            pe.wait_ge(gates_kept, UNITS + 1)

            def back_groups(groups):
                for g in groups:
                    back("back1", u_ready, lambda n: n + 1, range(g * GROUP, (g + 1) * GROUP), TU * UNIT)

            for n in range(GTILES):
                c = unit_cols(n)
                for f in range(4):
                    fs = slice(f * P, (f + 1) * P)
                    dst = take_bank("gates1", 4 * n + f)
                    mm(dst[:, 0:c.stop - c.start], fold[1][:, 0, fs], sums[1][:, 0, c], start=True, stop=False)
                    mm(dst[:, 0:c.stop - c.start], fold[1][:, 1, fs], sums[1][:, 1, c], start=False, stop=False)
                    done(mm(dst[:, 0:c.stop - c.start], fold_row[1][:, fs], sums[1][0:1, 2, c], start=False,
                            stop=True), "gates1", 4 * n + f)
                back_groups(groups_by(n - 2))
            back_groups(groups_by(GTILES - 2) + groups_by(GTILES - 1))
            transposes(2)
            drained("up2")
            sum_pass(3)
            pass_end(3)
            pe.wait_ge(w_loaded[2], 32)
            up("up2", W1c, 2, 2 * NT)
            down("down2", W2c, 2, 8 * NT)
            back("back2", act_ready, lambda n: 10 * NT + 2 * (n + 1))

            def rows_product(st, t, w):
                r = rows(t)
                dst = take_bank(st, t)
                for k in range(2):
                    last = mm(dst[0:r, :], TT[:, k, t * P:t * P + r], W1e[:, w + k, :], start=(k == 0),
                              stop=(k == 1))
                done(last, st, t)

            pe.wait_ge(w_loaded[3], 32)
            for g in range(len(TG) + 1):
                if g < len(TG):
                    transpose_group(3, g)
                if g >= 1:
                    for k in (0, 1):
                        wait_emptied(pe, "T3", 2 * (g - 1) + k)
                for t in blocks_of(g - 1):
                    if t < Q_FIRST:
                        rows_product("q3", t, 2)
            pe.wait_ge(wdiff, 1)
            for t in range(NB):
                rows_product("p3", t, 0)
                if Q_FIRST + t < NB:
                    rows_product("q3", Q_FIRST + t, 2)
            drained("down3")

            def flip(i, j):
                l = i - 4 * ITERS
                pe.wait_ge(hot, i * SP_IT + j + 1)
                pe.wait_ge(flip_copied, l * SP_IT + j + 1)
                for c in range(2):
                    last = nc.tensor.transpose(flip_bank[:, c, :], ohb[:, 2 * j + c, :, 1], identb[:, :])
                last.then_inc(flipped, 1)

            def spread_pair(i, j, starts):
                l = i - 4 * ITERS
                pe.wait_ge(flip_copied, l * SP_IT + j + 2)
                for c in (2 * j, 2 * j + 1):
                    pe.wait_ge(joined, l * CH_IT + c + 1)
                    for part3 in range(3):
                        last = mm(spread_bank(c), ohT[:, c, :],
                                  PTf[:, ds(starts[c % 2] * (3 * HID // P) + part3 * HID, HID)], start=(part3 == 0),
                                  stop=(part3 == 2))
                    last.then_inc(spread, 1)

            def sum_hidden(i, j):
                l = i - 4 * ITERS
                pe.wait_ge(relued, l * CH_IT + 2 * j + 2)
                for c in (2 * j, 2 * j + 1):
                    pe.wait_ge(added, i * CH_IT + c + 1)
                    for k in range(4):
                        last = mm(sum_bank(c)[:, k * P:(k + 1) * P], hbuf[:, c, k * P:(k + 1) * P], oh[:, c, :],
                                  start=True, stop=True)
                    last.then_inc(summed, 1)

            PEE = mybir.EngineType.PE
            flip(4 * ITERS, 0)
            pe.wait_ge(p_ready, NB)
            flip(4 * ITERS, 1)
            spread_pair(4 * ITERS, 0, block_starts(PEE, 0, 0, 0, 2))

            def body4(i, last):
                l = i - 4 * ITERS
                first = block_starts(PEE, 0, l, 2, CH_IT - 2)
                if not last:
                    first = (*first, *block_starts(PEE, 0, l + 1, 0, 2))
                for j in range(SP_IT):
                    if (nxt := ahead(i, j, 1, last)) is not None:
                        spread_pair(*nxt, first[2 * j:2 * j + 2])
                    if (nxt := ahead(i, j, 2, last)) is not None:
                        flip(*nxt)
                    sum_hidden(i, j)

            iterations(pe, 4, body4)
            pe.wait_ge(added, 5 * CHUNKS + SB)
            for n in range(NT):
                products("down3", n, 2, [(W2e[:, k, :], H[:, k, cols(n)]) for k in range(4)], n * 2)
                back("back3", u_ready, lambda n: GTILES + 2 * (n + 1), ended_by(n - 1))
            back("back3", u_ready, lambda n: GTILES + 2 * (n + 1), ended_by(NT - 1))


_IN2D = {"L0_gnn_eps_gin": (1, 1), "L2_gnn_eps": (1, 1)}
_NAMES = ["x", "src", "dst", "edge_weight", "edge_weight_n2", "L0_gnn_W1", "L0_gnn_b1", "L0_gnn_g1", "L0_gnn_bt1",
          "L0_gnn_W2", "L0_gnn_b2", "L0_gnn_g2", "L0_gnn_bt2", "L0_gnn_eps_gin", "L1_gnn_gamma", "L1_gnn_beta",
          "L1_gnn_W_in", "L1_gnn_b_in", "L1_gnn_W_out", "L1_gnn_b_out", "L1_gnn_W_x2i", "L1_gnn_b_x2i",
          "L1_gnn_W_h2h", "L2_gnn_eps", "L2_gnn_W1", "L2_gnn_b1", "L2_gnn_g1", "L2_gnn_be1", "L2_gnn_W2", "L2_gnn_b2",
          "L2_gnn_g2", "L2_gnn_be2", "L3_gnn_W1", "L3_gnn_b1", "L3_gnn_W2", "L3_gnn_b2"]


def kernel(**inputs):
    import numpy as np
    import concourse.bacc as bacc
    from concourse import mybir as mb
    from concourse.bass_utils import run_bass_kernel_spmd

    nc = bacc.Bacc("TRN2", target_bir_lowering=False, num_devices=1)
    arrays, aps = {}, {}
    for name in _NAMES:
        arr = np.ascontiguousarray(inputs[name])
        if name in _IN2D:
            arr = arr.reshape(_IN2D[name])
        arrays[f"in_{name}"] = arr
        aps[name] = nc.dram_tensor(f"in_{name}", arr.shape, mb.dt.from_np(arr.dtype), kind="ExternalInput").ap()
    out = nc.dram_tensor("out_x", (N, D), mb.dt.float32, kind="ExternalOutput").ap()
    gnn_kernel(nc, aps, out)
    r = run_bass_kernel_spmd(nc, [arrays], core_ids=[0])
    return r.results[0]["out_x"]
```
